# Optimizing a Trainium2 kernel written in Bass

```python
import numpy as np
import jax
import jax.numpy as jnp

def _softmax(x, axis=-1):
    return jax.nn.softmax(x, axis=axis)

def _gelu(x):
    return jax.nn.gelu(x, approximate=True)

def _silu(x):
    return jax.nn.silu(x)

def _sigmoid(x):
    return jax.nn.sigmoid(x)

def _layernorm(x, axis=-1, eps=1e-05):
    m = jnp.mean(x, axis=axis, keepdims=True)
    v = jnp.var(x, axis=axis, keepdims=True)
    return (x - m) / jnp.sqrt(v + eps)

def _scatter_add(tgt, idx, src, axis=0):
    return tgt.at[idx].add(src)

def _segment_sum(src, seg, n):
    return jax.ops.segment_sum(src, seg, n)
kernel_name = 'mk_xattn_ffn_d2_seqx_r8_f5d6c7'

def setup_inputs(seed: int=0):
    np.random.seed(seed)
    _w = jnp.asarray

    def _rec_inputs():
        import jax
        import jax.numpy as jnp
        _rk = jax.random.key(seed)
        x = -0.0002928 + 1 * jax.random.normal(jax.random.fold_in(_rk, 1), (16, 100, 256), jnp.float32)
        _lenS = 100 - jax.random.randint(jax.random.fold_in(_rk, 7), (16,), 0, max(1, 100 // 4) + 1, jnp.int32)
        _lenS2 = 1444 - jax.random.randint(jax.random.fold_in(_rk, 8), (16,), 0, max(1, 1444 // 4) + 1, jnp.int32)
        _ctx_512P = jax.random.normal(jax.random.fold_in(_rk, 11), (16, 16, 64), jnp.float32)
        _ctx_512c = jax.random.dirichlet(jax.random.fold_in(_rk, 511), 0.3 * jnp.ones((16,), jnp.float32), (16, 1444))
        _ctx_512t = jnp.einsum('bsk,bkd->bsd', _ctx_512c, _ctx_512P)
        _ctx_512t = _ctx_512t * jax.lax.rsqrt(jnp.mean(jnp.square(_ctx_512t)) + 1e-12) * 0.953939
        ctx_512 = 0.000227908 + 0.99994 * (_ctx_512t + 0.3 * jax.random.normal(jax.random.fold_in(_rk, 611), (16, 1444, 64), jnp.float32))
        return (x, ctx_512)
    x, ctx_512 = _rec_inputs()

    def _L0_xattn_setup():
        import jax, jax.numpy as jnp
        import numpy as np
        B, S, L = (2, 128, 128)
        DIM_Q, H, K, D_C, D_CQ, R = (256, 16, 128, 64, 192, 64)

        def _rope_tables(length, dim):
            inv = 1.0 / 10000.0 ** (jnp.arange(0, dim, 2, dtype=jnp.float32) / dim)
            f = jnp.arange(length, dtype=jnp.float32)[:, None] * inv[None, :]
            sin = jnp.repeat(jnp.sin(f), 2, axis=-1)
            cos = jnp.repeat(jnp.cos(f), 2, axis=-1)
            return (sin, cos)

        def _rotate_half(x):
            half = x.shape[-1] // 2
            return jnp.concatenate([-x[..., half:], x[..., :half]], axis=-1)

        def _apply_rope(x, sin, cos):
            return x * cos + _rotate_half(x) * sin
        key = jax.random.key(seed)
        ks = jax.random.split(key, 8)
        return {'hidden_q': jax.random.normal(ks[0], (B, S, DIM_Q), jnp.float32), 'kv_c': jax.random.normal(ks[1], (B, L, D_C), jnp.float32), 'Wq': jax.random.normal(ks[2], (H * K, DIM_Q), jnp.float32) / np.sqrt(DIM_Q).astype(np.float32), 'w_kc_q': jax.random.normal(ks[3], (H, K, D_CQ), jnp.float32) / np.sqrt(K).astype(np.float32), 'w_kc_kv': jax.random.normal(ks[4], (H, K, D_C), jnp.float32) / np.sqrt(K).astype(np.float32), 'W_qr': jax.random.normal(ks[5], (H, D_CQ, R), jnp.float32) / np.float32(np.sqrt(D_CQ) * np.sqrt(R)), 'W_kr': jax.random.normal(ks[6], (H, D_C, R), jnp.float32) / np.sqrt(D_C).astype(np.float32), 'Wo': jax.random.normal(ks[7], (DIM_Q, H * K), jnp.float32) / np.sqrt(H * K).astype(np.float32)}
    _L0_xattn_all = _L0_xattn_setup()
    _L0_xattn_in = {k: v for k, v in _L0_xattn_all.items() if k in ('Wq', 'w_kc_q', 'w_kc_kv', 'W_qr', 'W_kr', 'Wo')}
    del _L0_xattn_all

    def _L0_ffn_setup():
        import jax, jax.numpy as jnp
        import numpy as np
        H = 256
        I = 688
        E = 8
        TOPK = 2
        key = jax.random.key(seed)
        ks = jax.random.split(key, 5)
        s = 0.02
        x = jax.random.normal(ks[0], (2, 256, H), dtype=jnp.float32)
        router_w = jax.random.normal(ks[1], (E, H), dtype=jnp.float32) * s
        Wg = jax.random.normal(ks[2], (E, I, H), dtype=jnp.float32) * s
        Wu = jax.random.normal(ks[3], (E, I, H), dtype=jnp.float32) * s
        Wd = jax.random.normal(ks[4], (E, H, I), dtype=jnp.float32) * s
        return {'x': x, 'router_w': router_w, 'Wg': Wg, 'Wu': Wu, 'Wd': Wd}
    _L0_ffn_all = _L0_ffn_setup()
    _L0_ffn_in = {k: v for k, v in _L0_ffn_all.items() if k in ('router_w', 'Wg', 'Wu', 'Wd')}
    del _L0_ffn_all

    def _L1_xattn_setup():
        import jax, jax.numpy as jnp
        import numpy as np
        B, S, H, NH, L = (2, 256, 256, 16, 64)
        HD = H // NH
        key = jax.random.key(seed)
        k1, k2, k3, k4, k5 = jax.random.split(key, 5)
        scale = 0.02
        return {'q': jax.random.normal(k1, (B, S, H), dtype=jnp.float32), 'latent_kv': jax.random.normal(k2, (B, S, L), dtype=jnp.float32), 'Wq': jax.random.normal(k3, (H, H), dtype=jnp.float32) * scale, 'Wkv_expand': jax.random.normal(k4, (2 * H, L), dtype=jnp.float32) * scale, 'Wout': jax.random.normal(k5, (H, H), dtype=jnp.float32) * scale}
    _L1_xattn_all = _L1_xattn_setup()
    _L1_xattn_in = {k: v for k, v in _L1_xattn_all.items() if k in ('Wq', 'Wkv_expand', 'Wout')}
    del _L1_xattn_all

    def _L1_ffn_setup():
        import jax, jax.numpy as jnp
        import numpy as np
        B, T, D, H = (4, 256, 256, 176)
        E, K = (16, 2)
        G, TKG, S = (4, 2, 1)
        SCALE = 1.0

        def _moe(x, gate_w, w1, w2, sw1, sw2):
            Bx, Tx, Dx = x.shape
            xf = x.reshape(-1, Dx)
            N = xf.shape[0]
            shared = jnp.zeros_like(xf)
            for s in range(S):
                shared = shared + jax.nn.silu(xf @ sw1[s]) @ sw2[s]
            scores = jax.nn.sigmoid(xf @ gate_w.T)
            gs = E // G
            sg = scores.reshape(N, G, gs)
            group_scores = jax.lax.top_k(sg, min(2, gs))[0].sum(axis=-1)
            _, gidx = jax.lax.top_k(group_scores, TKG)
            gmask = jax.nn.one_hot(gidx, G, dtype=scores.dtype).max(axis=1)
            masked = (sg * gmask[:, :, None]).reshape(N, E)
            tw, ti = jax.lax.top_k(masked, K)
            tw = tw / (tw.sum(axis=-1, keepdims=True) + 1e-20) * SCALE
            combine = jnp.zeros((N, E), scores.dtype).at[jnp.arange(N)[:, None], ti].add(tw)
            out = shared
            for e in range(E):
                out = out + combine[:, e:e + 1] * (jax.nn.silu(xf @ w1[e]) @ w2[e])
            return out.reshape(Bx, Tx, Dx)
        key = jax.random.key(seed)
        ks = jax.random.split(key, 6)
        x = jax.random.normal(ks[0], (B, T, D), jnp.float32)
        gate_w = jax.random.normal(ks[1], (E, D), jnp.float32) * 0.02
        w1 = jax.random.normal(ks[2], (E, D, H), jnp.float32) * 0.02
        w2 = jax.random.normal(ks[3], (E, H, D), jnp.float32) * 0.02
        sw1 = jax.random.normal(ks[4], (S, D, H), jnp.float32) * 0.02
        sw2 = jax.random.normal(ks[5], (S, H, D), jnp.float32) * 0.02
        return {'x': x, 'gate_w': gate_w, 'w1': w1, 'w2': w2, 'sw1': sw1, 'sw2': sw2}
    _L1_ffn_all = _L1_ffn_setup()
    _L1_ffn_in = {k: v for k, v in _L1_ffn_all.items() if k in ('gate_w', 'w1', 'w2', 'sw1', 'sw2')}
    del _L1_ffn_all
    return {'x': x, 'ctx_512': ctx_512, 'L0_xattn_Wq': _L0_xattn_in['Wq'], 'L0_xattn_w_kc_q': _L0_xattn_in['w_kc_q'], 'L0_xattn_w_kc_kv': _L0_xattn_in['w_kc_kv'], 'L0_xattn_W_qr': _L0_xattn_in['W_qr'], 'L0_xattn_W_kr': _L0_xattn_in['W_kr'], 'L0_xattn_Wo': _L0_xattn_in['Wo'], 'L0_ffn_router_w': _L0_ffn_in['router_w'], 'L0_ffn_Wg': _L0_ffn_in['Wg'], 'L0_ffn_Wu': _L0_ffn_in['Wu'], 'L0_ffn_Wd': _L0_ffn_in['Wd'], 'L1_xattn_Wq': _L1_xattn_in['Wq'], 'L1_xattn_Wkv_expand': _L1_xattn_in['Wkv_expand'], 'L1_xattn_Wout': _L1_xattn_in['Wout'], 'L1_ffn_gate_w': _L1_ffn_in['gate_w'], 'L1_ffn_w1': _L1_ffn_in['w1'], 'L1_ffn_w2': _L1_ffn_in['w2'], 'L1_ffn_sw1': _L1_ffn_in['sw1'], 'L1_ffn_sw2': _L1_ffn_in['sw2']}

def reference(x, ctx_512, L0_xattn_Wq, L0_xattn_w_kc_q, L0_xattn_w_kc_kv, L0_xattn_W_qr, L0_xattn_W_kr, L0_xattn_Wo, L0_ffn_router_w, L0_ffn_Wg, L0_ffn_Wu, L0_ffn_Wd, L1_xattn_Wq, L1_xattn_Wkv_expand, L1_xattn_Wout, L1_ffn_gate_w, L1_ffn_w1, L1_ffn_w2, L1_ffn_sw1, L1_ffn_sw2):
    import jax
    import jax.numpy as jnp

    def _L0_xattn_ref(hidden_q, kv_c, Wq, w_kc_q, w_kc_kv, W_qr, W_kr, Wo):
        import jax, jax.numpy as jnp
        import numpy as np
        B, S, L = (2, 128, 128)
        DIM_Q, H, K, D_C, D_CQ, R = (256, 16, 128, 64, 192, 64)

        def _rope_tables(length, dim):
            inv = 1.0 / 10000.0 ** (jnp.arange(0, dim, 2, dtype=jnp.float32) / dim)
            f = jnp.arange(length, dtype=jnp.float32)[:, None] * inv[None, :]
            sin = jnp.repeat(jnp.sin(f), 2, axis=-1)
            cos = jnp.repeat(jnp.cos(f), 2, axis=-1)
            return (sin, cos)

        def _rotate_half(x):
            half = x.shape[-1] // 2
            return jnp.concatenate([-x[..., half:], x[..., :half]], axis=-1)

        def _apply_rope(x, sin, cos):
            return x * cos + _rotate_half(x) * sin
        Bv, Sv, _ = hidden_q.shape
        _, Lv, _ = kv_c.shape
        q_hk = (hidden_q @ Wq.T).reshape(Bv, Sv, H, K)
        q_big = jnp.einsum('bshk,hkq->bshq', q_hk, w_kc_q)
        sin_q, cos_q = _rope_tables(Sv, D_CQ)
        q_big = _apply_rope(q_big, sin_q[None, :, None, :], cos_q[None, :, None, :])
        sin_k, cos_k = _rope_tables(Lv, D_C)
        kv_r = _apply_rope(kv_c, sin_k[None], cos_k[None])
        q_r = jnp.einsum('bshq,hqr->bhsr', q_big, W_qr)
        k_r = jnp.einsum('bld,hdr->bhlr', kv_r, W_kr)
        scores = jnp.einsum('bhsr,bhlr->bhsl', q_r, k_r)
        attn = jax.nn.softmax(scores, axis=-1)
        ctx_c = jnp.einsum('bhsl,bld->bhsd', attn, kv_r)
        ctx_lat = jnp.einsum('bhsd,hkd->bhsk', ctx_c, w_kc_kv)
        ctx = ctx_lat.transpose(0, 2, 1, 3).reshape(Bv, Sv, H * K)
        return ctx @ Wo.T

    def _L0_ffn_ref(x, router_w, Wg, Wu, Wd):
        import jax, jax.numpy as jnp
        import numpy as np
        H = 256
        I = 688
        E = 8
        TOPK = 2
        B, S, Hh = x.shape
        xf = x.reshape(-1, Hh)
        logits = xf @ router_w.T
        top_vals, top_idx = jax.lax.top_k(logits, TOPK)
        top_w = jax.nn.softmax(top_vals, axis=-1)
        combine = jnp.sum(jax.nn.one_hot(top_idx, E, dtype=xf.dtype) * top_w[..., None], axis=1)
        out = jnp.zeros_like(xf)
        for e in range(E):
            h = jax.nn.silu(xf @ Wg[e].T) * (xf @ Wu[e].T)
            y = h @ Wd[e].T
            out = out + combine[:, e:e + 1] * y
        return out.reshape(B, S, Hh)

    def _L1_xattn_ref(q, latent_kv, Wq, Wkv_expand, Wout):
        import jax, jax.numpy as jnp
        import numpy as np
        B, S, H, NH, L = (2, 256, 256, 16, 64)
        HD = H // NH
        b, sq, _ = q.shape
        sk = latent_kv.shape[1]
        qp = q @ Wq.T
        kv = latent_kv @ Wkv_expand.T
        k, v = jnp.split(kv, 2, axis=-1)
        qh = qp.reshape(b, sq, NH, HD).transpose(0, 2, 1, 3)
        kh = k.reshape(b, sk, NH, HD).transpose(0, 2, 1, 3)
        vh = v.reshape(b, sk, NH, HD).transpose(0, 2, 1, 3)
        inv_sqrt_d = 1.0 / jnp.sqrt(jnp.float32(HD))
        scores = jnp.einsum('bhqd,bhkd->bhqk', qh, kh) * inv_sqrt_d
        causal = jnp.tril(jnp.ones((sq, sk), dtype=bool))
        scores = jnp.where(causal, scores, jnp.finfo(scores.dtype).min)
        attn = jax.nn.softmax(scores, axis=-1)
        out = jnp.einsum('bhqk,bhkd->bhqd', attn, vh)
        out = out.transpose(0, 2, 1, 3).reshape(b, sq, H)
        return out @ Wout.T

    def _L1_ffn_ref(x, gate_w, w1, w2, sw1, sw2):
        import jax, jax.numpy as jnp
        import numpy as np
        B, T, D, H = (4, 256, 256, 176)
        E, K = (16, 2)
        G, TKG, S = (4, 2, 1)
        SCALE = 1.0

        def _moe(x, gate_w, w1, w2, sw1, sw2):
            Bx, Tx, Dx = x.shape
            xf = x.reshape(-1, Dx)
            N = xf.shape[0]
            shared = jnp.zeros_like(xf)
            for s in range(S):
                shared = shared + jax.nn.silu(xf @ sw1[s]) @ sw2[s]
            scores = jax.nn.sigmoid(xf @ gate_w.T)
            gs = E // G
            sg = scores.reshape(N, G, gs)
            group_scores = jax.lax.top_k(sg, min(2, gs))[0].sum(axis=-1)
            _, gidx = jax.lax.top_k(group_scores, TKG)
            gmask = jax.nn.one_hot(gidx, G, dtype=scores.dtype).max(axis=1)
            masked = (sg * gmask[:, :, None]).reshape(N, E)
            tw, ti = jax.lax.top_k(masked, K)
            tw = tw / (tw.sum(axis=-1, keepdims=True) + 1e-20) * SCALE
            combine = jnp.zeros((N, E), scores.dtype).at[jnp.arange(N)[:, None], ti].add(tw)
            out = shared
            for e in range(E):
                out = out + combine[:, e:e + 1] * (jax.nn.silu(xf @ w1[e]) @ w2[e])
            return out.reshape(Bx, Tx, Dx)
        return _moe(x, gate_w, w1, w2, sw1, sw2)
    x = x + _L0_xattn_ref(_layernorm(x, axis=-1), ctx_512, L0_xattn_Wq, L0_xattn_w_kc_q, L0_xattn_w_kc_kv, L0_xattn_W_qr, L0_xattn_W_kr, L0_xattn_Wo)
    x = x + _L0_ffn_ref(_layernorm(x, axis=-1), L0_ffn_router_w, L0_ffn_Wg, L0_ffn_Wu, L0_ffn_Wd)
    x = x + _L1_xattn_ref(_layernorm(x, axis=-1), ctx_512, L1_xattn_Wq, L1_xattn_Wkv_expand, L1_xattn_Wout)
    x = x + _L1_ffn_ref(_layernorm(x, axis=-1), L1_ffn_gate_w, L1_ffn_w1, L1_ffn_w2, L1_ffn_sw1, L1_ffn_sw2)
    return x

_drawn_inputs = setup_inputs


def setup_inputs(seed=0):
    import zlib

    import numpy as np

    out = dict(_drawn_inputs(seed))
    spreads = {}
    factors = {'L0_ffn_router_w': 3.252,
     'L0_ffn_Wg': 2.878,
     'L0_ffn_Wu': 2.827,
     'L0_ffn_Wd': 2.844,
     'L1_xattn_Wq': 64.0}
    for name, (base, spread) in spreads.items():
        noise = np.random.default_rng([zlib.crc32(name.encode()), seed]).standard_normal(out[name].shape)
        drawn = base * np.exp(spread * noise) if base else spread * noise
        out[name] = jnp.asarray(drawn.astype(out[name].dtype))
    for name, factor in factors.items():
        out[name] = (out[name] * factor).astype(out[name].dtype)
    return out
```

```python
from contextlib import ExitStack

import concourse.bass as bass
from concourse import mybir

ALU = mybir.AluOpType
ACT = mybir.ActivationFunctionType
F32 = mybir.dt.float32
F32R = mybir.dt.float32r
BF16 = mybir.dt.bfloat16
U32 = mybir.dt.uint32
AX = mybir.AxisListType

P = 128
B, S, D = 16, 100, 256
SK, DC = 1444, 64
H = 16
K0, DQ, R0 = 128, 192, 64
KD = D // P
CB = 4
CH = CB * S
NC = B // CB
HALF = DQ // 2
KT = -(-SK // P)
SKP = KT * P
HD = D // H
EPS = 1e-5
PSUM_COLS = 512


class Core:

    def __init__(self, nc, ctx):
        self.nc, self.ctx = nc, ctx
        self.psum = [ctx.enter_context(nc.psum_tensor(f"bank{i}", [P, PSUM_COLS], F32)) for i in range(8)]

    def sem(self, name):
        return self.ctx.enter_context(self.nc.semaphore(name))


def fixed(ctx, nc, name, shape, dtype=F32):
    return ctx.enter_context(nc.sbuf_tensor(name, shape, dtype))


def as_f32(ap):
    return ap.bitcast(F32)


def layernorm(core, tag, X, ident, XH, XL):
    nc, psum = core.nc, core.psum
    with ExitStack() as ctx:
        stats = fixed(ctx, nc, tag + "stats", [S, B, 6])
        small = fixed(ctx, nc, tag + "small", [S, 8, B])
        XN = fixed(ctx, nc, tag + "XN", [S, B, D])
        dve = core.sem(tag + "dve")
        var_ready = core.sem(tag + "var")
        std_ready = core.sem(tag + "std")
        xn_ready = core.sem(tag + "xn")
        turned = core.sem(tag + "turned")
        hi_ready = core.sem(tag + "hi")
        with nc.Block() as block:

            @block.vector
            def _(v):
                with v.Fori(0, B) as b:
                    nc.vector.bn_stats(stats[:, b, :], X[:, b, :]).then_inc(dve, 1)
                mean, var, std, rstd, diff, sq, y2 = (small[:, i, :] for i in range(7))
                me, qe, mo, qo = (stats[:, :, i] for i in (1, 2, 4, 5))
                step = B

                def chained(ins):
                    nonlocal step
                    step += 1
                    ins.then_inc(dve, 1)
                    v.wait_ge(dve, step)

                v.wait_ge(dve, step)
                chained(nc.vector.tensor_tensor(mean, me, mo, ALU.add))
                chained(nc.vector.tensor_scalar(mean, mean, 0.5, None, ALU.mult))
                chained(nc.vector.tensor_tensor(diff, me, mo, ALU.subtract))
                chained(nc.vector.tensor_tensor(diff, diff, diff, ALU.mult))
                chained(nc.vector.tensor_tensor(sq, qe, qo, ALU.add))
                chained(nc.vector.tensor_scalar(sq, sq, 1.0 / D, EPS, ALU.mult, ALU.add))
                nc.vector.scalar_tensor_tensor(var, diff, 0.25, sq, ALU.mult, ALU.add).then_inc(var_ready, 1)
                v.wait_ge(std_ready, 1)
                v.wait_ge(var_ready, 1)
                chained(nc.vector.reciprocal(rstd, std))
                chained(nc.vector.tensor_tensor(y2, rstd, rstd, ALU.mult))
                chained(nc.vector.tensor_tensor(y2, y2, var, ALU.mult))
                chained(nc.vector.tensor_scalar(y2, y2, -0.5, 1.5, ALU.mult, ALU.add))
                chained(nc.vector.tensor_tensor(rstd, rstd, y2, ALU.mult))
                for b in range(B):
                    nc.vector.tensor_scalar(XN[:, b, :], X[:, b, :], small[:, 0, b:b + 1], small[:, 3, b:b + 1],
                                            ALU.subtract, ALU.mult).then_inc(xn_ready, 1)
                for n in range(NC * KD):
                    c, k = divmod(n, KD)
                    v.wait_ge(hi_ready, n + 1)
                    hi = XH[:, k, c * CH:(c + 1) * CH]
                    nc.vector.tensor_tensor(XL[:, k, c * CH:(c + 1) * CH], psum[n][:, 0:CH], as_f32(hi), ALU.subtract)

            @block.scalar
            def _(act):
                act.wait_ge(var_ready, 1)
                nc.scalar.activation(small[:, 2, :], small[:, 1, :], ACT.Sqrt).then_inc(std_ready, 1)
                for n in range(NC * KD):
                    c, k = divmod(n, KD)
                    act.wait_ge(turned, n + 1)
                    nc.scalar.activation(XH[:, k, c * CH:(c + 1) * CH], psum[n][:, 0:CH], ACT.Copy).then_inc(hi_ready, 1)

            @block.tensor
            def _(pe):
                for n in range(NC * KD):
                    c, k = divmod(n, KD)
                    pe.wait_ge(xn_ready, (c + 1) * CB)
                    for t in range(CB):
                        last = nc.tensor.transpose(psum[n][:, t * S:(t + 1) * S],
                                                   XN[:, c * CB + t, k * P:(k + 1) * P], ident[0:S, 0:S])
                    last.then_inc(turned, 1)


def split_products(nc, out, parts, first=True, last=True):
    todo = []
    for lh, ll, rh, rl in parts:
        todo += [(lh, rh), (lh, rl), (ll, rh)]
    for n, (lhs, rhs) in enumerate(todo):
        ins = nc.tensor.matmul(out, lhs, rhs, start=first and n == 0, stop=last and n == len(todo) - 1)
    return ins


def fold_weights(core, dram, AH, AL, M2, BB):
    nc, psum = core.nc, core.psum
    with ExitStack() as ctx:
        wq = fixed(ctx, nc, "wq", [K0, H, D])
        wkq = fixed(ctx, nc, "wkq", [K0, H, DQ])
        wqr = fixed(ctx, nc, "wqr", [R0, H, DQ])
        wkr = fixed(ctx, nc, "wkr", [R0, H, DC])
        wo = fixed(ctx, nc, "wo", [K0, H, D])
        wkv = fixed(ctx, nc, "wkv", [K0, H, DC])
        in_q = core.sem("fw_in_q")
        in_r = core.sem("fw_in_r")
        in_o = core.sem("fw_in_o")
        a_ready = core.sem("fw_a")
        a_hi = core.sem("fw_ahi")
        a_lo = core.sem("fw_alo")
        mb_ready = core.sem("fw_mb")
        mb_out = core.sem("fw_mbout")
        with nc.Block() as block:

            @block.sync
            def _(sp):
                sp.dma_start(wq[:], dram["Wq"].rearrange("(h k) d -> k h d", k=K0)).then_inc(in_q, 16)
                sp.dma_start(wkq[:], dram["w_kc_q"].rearrange("h k q -> k h q")).then_inc(in_q, 16)
                sp.dma_start(wqr[:], dram["W_qrT"]).then_inc(in_r, 16)
                sp.dma_start(wkr[:], dram["W_krT"]).then_inc(in_r, 16)
                sp.dma_start(wo[:], dram["WoT"].rearrange("(h k) d -> k h d", k=K0)).then_inc(in_o, 16)
                sp.dma_start(wkv[:], dram["w_kc_kv"].rearrange("h k q -> k h q")).then_inc(in_o, 16)

            @block.tensor
            def _(pe):
                pe.wait_ge(in_q, 32)
                pe.wait_ge(in_r, 32)
                pe.wait_ge(in_o, 32)
                for h in range(H):
                    if h >= 2:
                        pe.wait_ge(a_lo, h - 1)
                        pe.wait_ge(mb_out, h - 1)
                    for k in range(KD):
                        last = nc.tensor.matmul(psum[h % 2][:, k * DQ:(k + 1) * DQ], wq[:, h, k * P:(k + 1) * P],
                                                wkq[:, h, :], start=True, stop=True)
                    last.then_inc(a_ready, 1)
                    for half in range(2):
                        nc.tensor.matmul(psum[2 + h % 2][0:HALF, half * P:(half + 1) * P],
                                         wqr[:, h, half * HALF:(half + 1) * HALF],
                                         wkr[:, h, :].rearrange("p (o d) -> p o d", o=1).to_broadcast([R0, 2, DC]),
                                         start=True, stop=True)
                    nc.tensor.matmul(psum[4 + h % 2][0:DC, 0:D], wkv[:, h, :], wo[:, h, :],
                                     start=True, stop=True).then_inc(mb_ready, 1)

            @block.scalar
            def _(act):
                for h in range(H):
                    act.wait_ge(a_ready, h + 1)
                    nc.scalar.activation(AH[:, :, h, :], psum[h % 2][:, 0:KD * DQ].rearrange("p (k q) -> p k q", k=KD),
                                         ACT.Copy).then_inc(a_hi, 1)

            @block.vector
            def _(v):
                for h in range(H):
                    v.wait_ge(a_hi, h + 1)
                    nc.vector.tensor_tensor(AL[:, :, h, :], psum[h % 2][:, 0:KD * DQ].rearrange("p (k q) -> p k q", k=KD),
                                            as_f32(AH[:, :, h, :]), ALU.subtract).then_inc(a_lo, 1)
                    v.wait_ge(mb_ready, h + 1)
                    nc.vector.tensor_copy(M2[:, :, h, :],
                                          psum[2 + h % 2][0:HALF, 0:2 * P].rearrange("p (a c) -> p a c", a=2))
                    nc.vector.tensor_copy(BB[(h % 2) * DC:(h % 2 + 1) * DC, h // 2, :],
                                          psum[4 + h % 2][0:DC, 0:D]).then_inc(mb_out, 1)


def latent_queries(core, dram, XH, XL, AH, AL, M2, queries):
    nc, psum = core.nc, core.psum
    SLOTS, BUFS = 4, 2
    with ExitStack() as ctx:
        rope = fixed(ctx, nc, "rope_q", [HALF, 4, S])
        prod = fixed(ctx, nc, "rope_prod", [HALF, 2, 4, CH])
        rot = fixed(ctx, nc, "rotated", [HALF, 2, 2, CH])
        out = fixed(ctx, nc, "q_out", [P, SLOTS, CH], F32R)
        rope_in = core.sem("lq_rope")
        q_ready = core.sem("lq_q")
        mul_done = core.sem("lq_mul")
        rot_done = core.sem("lq_rot")
        qq_ready = core.sem("lq_qq")
        lo_done = core.sem("lq_lo")
        hi_done = core.sem("lq_hi")
        sent = [core.sem(f"lq_sent{i}") for i in range(SLOTS)]
        with nc.Block() as block:

            @block.sync
            def _(sp):
                sp.dma_start(rope[:], dram["rope_q"]).then_inc(rope_in, 16)
                for s in sent:
                    sp.sem_inc(s, 16)
                with sp.Fori(0, NC) as c:
                    for h in range(H):
                        sp.wait_ge(lo_done, c * H + (BUFS + h + 1))
                        sp.dma_start(queries[bass.ts(c, CB)].rearrange("b p h s -> p h b s")[:, h],
                                     as_f32(out[:, h % SLOTS, :]).rearrange("p (b s) -> p b s", b=CB)).then_inc(sent[h % SLOTS], 16)
                for s in sent:
                    sp.wait_ge(s, 16 * (1 + NC * H // SLOTS))

            @block.tensor
            def _(pe):
                def narrow(c, h):
                    pe.wait_ge(rot_done, c * H + (BUFS + h + 1))
                    pe.wait_ge(lo_done, c * H + (h + 1))
                    for half in range(2):
                        last = nc.tensor.matmul(psum[4 + h % 2][:, 0:CH], M2[:, half, h, :], rot[:, h % 2, half, :],
                                                start=half == 0, stop=half == 1)
                    last.then_inc(qq_ready, 1)

                pe.sem_inc(qq_ready, BUFS)
                with pe.Fori(0, NC) as c:
                    for h in range(H):
                        pe.wait_ge(mul_done, c * H + (h + 1))
                        for half in range(2):
                            last = split_products(nc, psum[2 * (h % 2) + half][0:HALF, 0:CH],
                                                  [(AH[:, k, h, half * HALF:(half + 1) * HALF],
                                                    AL[:, k, h, half * HALF:(half + 1) * HALF],
                                                    XH[:, k, bass.ts(c, CH)], XL[:, k, bass.ts(c, CH)]) for k in range(KD)])
                        last.then_inc(q_ready, 1)
                        if h >= 1:
                            narrow(c, h - 1)
                    narrow(c, H - 1)

            @block.vector
            def _(v):
                v.wait_ge(rope_in, 16)
                v.sem_inc(mul_done, BUFS)
                v.sem_inc(lo_done, BUFS)

                def low(c, h):
                    v.wait_ge(hi_done, c * H + (h + 1))
                    nc.vector.tensor_tensor(out[DC:P, h % SLOTS, :], psum[4 + h % 2][DC:P, 0:CH],
                                            as_f32(out[DC:P, h % SLOTS, :]), ALU.subtract).then_inc(lo_done, 1)

                with v.Fori(0, NC) as c:
                    for h in range(H):
                        v.wait_ge(q_ready, c * H + (h + 1))
                        v.wait_ge(rot_done, c * H + (h + 1))
                        for n, half in enumerate((0, 1, 1, 0)):
                            last = nc.vector.tensor_tensor(
                                prod[:, h % 2, n, :].rearrange("p (b s) -> p b s", b=CB),
                                psum[2 * (h % 2) + half][0:HALF, 0:CH].rearrange("p (b s) -> p b s", b=CB),
                                rope[:, n:n + 1, :].to_broadcast([HALF, CB, S]), ALU.mult)
                        last.then_inc(mul_done, 1)
                        if h >= 2:
                            low(c, h - 2)
                    low(c, H - 2)
                    low(c, H - 1)

            @block.gpsimd
            def _(pool):
                pool.sem_inc(rot_done, BUFS)
                with pool.Fori(0, NC) as c:
                    for h in range(H):
                        pool.wait_ge(mul_done, c * H + (BUFS + h + 1))
                        pool.wait_ge(qq_ready, c * H + (h + 1))
                        for half in range(2):
                            last = nc.gpsimd.tensor_tensor(rot[:, h % 2, half, :], prod[:, h % 2, 2 * half, :],
                                                           prod[:, h % 2, 2 * half + 1, :], ALU.add)
                        last.then_inc(rot_done, 1)

            @block.scalar
            def _(act):
                with act.Fori(0, NC) as c:
                    for h in range(H):
                        act.wait_ge(qq_ready, c * H + (BUFS + h + 1))
                        act.wait_ge(sent[h % SLOTS], c * (16 * H // SLOTS) + 16 * (h // SLOTS + 1))
                        nc.scalar.activation(out[:, h % SLOTS, :], psum[4 + h % 2][:, 0:CH], ACT.Copy).then_inc(hi_done, 1)


def latent_attention(core, dram, X, ident, queries, BB):
    nc, psum = core.nc, core.psum
    BUFS = 3
    QG = H * S // CH
    HG = CH // S
    QT = -(-H * S // P)
    QW = QT * P
    NS = QG * KT
    KC = 3
    KW = [482, 482, 480]
    NF = QT * KC
    SB, FB, PB = 3, 2, 4
    S0, F0, A0, MISC = 0, 3, 5, 7
    F_AT = 1
    TURN_AT, OUT_AT, HI_AT = 43, 6, 20
    with ExitStack() as ctx:
        QS = [fixed(ctx, nc, f"QS{r}", [P, QW], F32R) for r in range(BUFS)]
        QB = [fixed(ctx, nc, f"QB{r}", [DC + 2, QW], F32R) for r in range(BUFS)]
        KH = [fixed(ctx, nc, f"KH{r}", [P, SKP], F32R) for r in range(BUFS)]
        KB = [fixed(ctx, nc, f"KB{r}", [DC + 2, SKP], F32R) for r in range(BUFS)]
        KV = [fixed(ctx, nc, f"KV{r}", [P, KT, 2 * DC]) for r in range(BUFS)]
        raw = fixed(ctx, nc, "raw", [P, 2, SK])
        rawk = fixed(ctx, nc, "rawk", [P, KT, DC])
        prodk = fixed(ctx, nc, "prodk", [P, 2, KT, DC])
        ropeT = fixed(ctx, nc, "ropeT", [P, 2, SK])
        ropek = fixed(ctx, nc, "ropek", [P, 2, KT, DC])
        E = fixed(ctx, nc, "E", [P, PB, CH])
        PM = fixed(ctx, nc, "PM", [P, NF])
        NM = fixed(ctx, nc, "NM", [P, QT])
        MH = fixed(ctx, nc, "MH", [QT, P], F32R)
        ML = fixed(ctx, nc, "ML", [QT, P], F32R)
        RS = fixed(ctx, nc, "RS", [P, 2, S])
        CT = fixed(ctx, nc, "CT", [P, H // 2, S])

        consts = core.sem("at_consts")
        pads = core.sem("at_pads")
        q_in = [core.sem(f"at_q{r}") for r in range(BUFS)]
        kv_in = core.sem("at_kvin")
        mulT = core.sem("at_mulT")
        rot_ready = core.sem("at_rot")
        kh_ready = core.sem("at_kh")
        k_ready = core.sem("at_k")
        s_ready = core.sem("at_s")
        exp_done = core.sem("at_exp")
        av_done = core.sem("at_av")
        f_ready = core.sem("at_f")
        red_done = core.sem("at_red")
        nm_ready = core.sem("at_nm")
        turned = core.sem("at_turned")
        mh_ready = core.sem("at_mh")
        ml_ready = core.sem("at_ml")
        m_in = core.sem("at_min")
        recip = core.sem("at_recip")
        norm_done = core.sem("at_norm")
        out_ready = core.sem("at_out")
        res_done = core.sem("at_res")

        def key_loads(sp, b):
            sp.dma_start(raw[:], dram["ctx_T"][b]).then_inc(kv_in, 16)
            sp.dma_start(rawk[:], dram["ctx_k"][b]).then_inc(kv_in, 16)

        def query_loads(sp, b, r):
            sp.dma_start(as_f32(QS[r][:, 0:H * S]), queries[b].rearrange("p h s -> p (h s)")).then_inc(q_in[r], 16)
            sp.dma_start(as_f32(QB[r][0:DC, 0:H * S]),
                         queries[b].rearrange("p h s -> p (h s)")[0:DC]).then_inc(q_in[r], 16)

        def max_rows(sp, b, r):
            sp.wait_ge(ml_ready, b + 1)
            for row, part in enumerate((MH, ML)):
                sp.dma_start(as_f32(QB[r][DC + row:DC + row + 1, :]).rearrange("o (t p) -> o t p", p=P),
                             as_f32(part[:, :])).then_inc(m_in, 16)

        def rotate_keys(pool, b, step):
            r = b_mod(b)
            pool.wait_ge(kv_in, b_val(b) * 32 + 32)
            nc.gpsimd.tensor_tensor(raw[:, 0, :], raw[:, 0, :], ropeT[:, 0, :], ALU.mult).then_inc(mulT, 1)
            nc.gpsimd.tensor_tensor(raw[:, 1, :], raw[:, 1, :], ropeT[:, 1, :], ALU.mult).then_inc(mulT, 1)
            nc.gpsimd.tensor_tensor(prodk[:, 0], rawk[:], ropek[:, 0], ALU.mult).then_inc(mulT, 1)
            for half in range(2):
                a, z = half * DC // 2, (1 - half) * DC // 2
                nc.gpsimd.tensor_tensor(prodk[:, 1, :, a:a + DC // 2], rawk[:, :, z:z + DC // 2],
                                        ropek[:, 1, :, a:a + DC // 2], ALU.mult).then_inc(mulT, 1)
            pool.wait_ge(mulT, b_val(b) * 5 + 2)
            nc.gpsimd.tensor_tensor(raw[:, 0, :], raw[:, 0, :], raw[:, 1, :], ALU.add).then_inc(rot_ready, 1)
            if step is not None:
                pool.wait_ge(av_done, b_val(step) * NS + PB)
            pool.wait_ge(mulT, b_val(b) * 5 + 5)
            nc.gpsimd.tensor_tensor(KV[r][:, :, 0:DC], prodk[:, 0], prodk[:, 1], ALU.add)
            pool.wait_ge(kh_ready, b_val(b) + 1)
            nc.gpsimd.tensor_tensor(KB[r][0:DC, 0:SK], raw[0:DC, 0, :], as_f32(KH[r][0:DC, 0:SK]),
                                    ALU.subtract).then_inc(k_ready, 1)

        def keys_high(act, b, step):
            act.wait_ge(rot_ready, b_val(b) + 1)
            if step is not None:
                act.wait_ge(av_done, b_val(step) * NS + PB)
            nc.scalar.activation(KH[b_mod(b)][:, 0:SK], raw[:, 0, :], ACT.Copy).then_inc(kh_ready, 1)

        def max_piece(pe, b, f):
            r = b_mod(b)
            t, j = divmod(f, KC)
            if f >= FB:
                pe.wait_ge(red_done, b_val(b) * NF + (f - FB + 1))
            elif b is not FIRST:
                pe.wait_ge(red_done, b_val(b) * NF)
            nc.tensor.matmul(psum[F0 + f % FB][:, 0:KW[j]], QS[r][:, t * P:(t + 1) * P],
                             KH[r][:, sum(KW[:j]):sum(KW[:j + 1])], start=True, stop=True).then_inc(f_ready, 1)

        def turn_max(pe, b):
            pe.wait_ge(nm_ready, b_val(b) + 1)
            nc.tensor.transpose(psum[MISC][0:QT, 0:P], NM[:, :], ident[:, :]).then_inc(turned, 1)

        def max_high(act, b):
            act.wait_ge(turned, b_val(b) + 1)
            if b is not FIRST:
                act.wait_ge(m_in, b_val(b) * 32)
            nc.scalar.activation(MH[:, :], psum[MISC][0:QT, 0:P], ACT.Copy).then_inc(mh_ready, 1)

        def max_low(v, b):
            v.wait_ge(mh_ready, b_val(b) + 1)
            nc.vector.tensor_tensor(ML[:, :], psum[MISC][0:QT, 0:P], as_f32(MH[:, :]), ALU.subtract).then_inc(ml_ready, 1)

        def reduce_piece(v, b, f):
            v.wait_ge(f_ready, b_val(b) * NF + (f + 1))
            if f == 0 and b is not FIRST:
                v.wait_ge(nm_ready, b_val(b))
            nc.vector.tensor_reduce(PM[:, f:f + 1], psum[F0 + f % FB][:, 0:KW[f % KC]], AX.X, ALU.max).then_inc(red_done, 1)

        def batch_max(v, b):
            v.wait_ge(red_done, b_val(b) * NF + NF)
            if b is not FIRST:
                v.wait_ge(turned, b_val(b))
            nc.vector.tensor_reduce(NM[:, :], PM[:, :].rearrange("p (t k) -> p t k", k=KC), AX.X, ALU.max,
                                    negate=True).then_inc(nm_ready, 1)

        def project(pe, b):
            pe.wait_ge(norm_done, b_val(b) * H + (H + 2 * HG))
            for j in range(H // 2):
                last = nc.tensor.matmul(psum[MISC][0:S, 0:D], CT[:, j, :], BB[:, j, :], start=j == 0, stop=j == H // 2 - 1)
            last.then_inc(out_ready, 1)

        def add_output(v, b):
            v.wait_ge(out_ready, b_val(b) + 1)
            x = X[:, b_val(b), :]
            nc.vector.tensor_tensor(x, psum[MISC][0:S, 0:D], x, ALU.add).then_inc(res_done, 1)

        def normalise(v, b, h):
            g, j = divmod(h, HG)
            acc = psum[A0 + g % 2]
            v.wait_ge(av_done, b_val(b) * NS + (PB + KT * (g + 1)))
            if h == 0 and b is not FIRST:
                v.wait_ge(out_ready, b_val(b))
            if b is not FIRST or h >= 2:
                v.wait_ge(norm_done, b_val(b) * H + (2 * HG + h - 1))
            nc.vector.reciprocal(RS[DC:P, h % 2, :], acc[DC:P, j * S:(j + 1) * S]).then_inc(recip, 1)
            v.wait_ge(recip, b_val(b) * H + (h + 1))
            rows = slice((h % 2) * DC, (h % 2 + 1) * DC)
            nc.vector.tensor_tensor(CT[rows, h // 2, :], acc[0:DC, j * S:(j + 1) * S], RS[DC:P, h % 2, :],
                                    ALU.mult).then_inc(norm_done, 1)

        class Batch:
            def __init__(self, turn, r):
                self.turn, self.r = turn + r // BUFS, r % BUFS

            def __add__(self, n):
                return Batch(self.turn, self.r + n)

        def b_val(b):
            return b.turn * BUFS + b.r

        def b_mod(b):
            return b.r

        FIRST = Batch(0, 0)

        def steps(eng, body):
            body(FIRST, True, True)
            with eng.Fori(0, (B - 1 - BUFS) // BUFS) as i:
                for u in range(BUFS):
                    body(Batch(i, 1 + u), True, True)
            body(Batch(0, B - 3), True, True)
            body(Batch(0, B - 2), True, False)
            body(Batch(0, B - 1), False, False)

        with nc.Block() as block:

            @block.sync
            def _(sp):
                sp.dma_start(ropeT[:], dram["rope_T"]).then_inc(consts, 16)
                sp.dma_start(ropek[:], dram["rope_k"]).then_inc(consts, 16)
                for r in range(BUFS):
                    sp.dma_start(KV[r][:, :, DC:], dram["key_ones"]).then_inc(consts, 16)
                key_loads(sp, 0)
                query_loads(sp, 0, 0)
                query_loads(sp, 1, 1)
                sp.wait_ge(k_ready, 1)
                key_loads(sp, 1)
                max_rows(sp, 0, 0)
                sp.wait_ge(k_ready, 2)
                key_loads(sp, 2)

                def step(b, has_next, has_keys):
                    if has_keys:
                        sp.wait_ge(av_done, b_val(b) * NS + PB)
                        query_loads(sp, b_val(b + 2), b_mod(b + 2))
                        sp.wait_ge(k_ready, b_val(b) + 3)
                        if not (isinstance(b.turn, int) and b_val(b) == B - BUFS):
                            key_loads(sp, b_val(b + 3))
                    if has_next:
                        max_rows(sp, b_val(b + 1), b_mod(b + 1))

                steps(sp, step)

            @block.gpsimd
            def _(pool):
                pool.wait_ge(consts, 16 * (2 + BUFS))
                rotate_keys(pool, FIRST, None)
                rotate_keys(pool, FIRST + 1, None)

                def step(b, has_next, has_keys):
                    if has_keys:
                        rotate_keys(pool, b + 2, b)

                steps(pool, step)

            @block.scalar
            def _(act):
                act.sem_inc(exp_done, SB)
                keys_high(act, FIRST, None)
                max_high(act, FIRST)
                keys_high(act, FIRST + 1, None)

                def step(b, has_next, has_keys):
                    for n in range(NS):
                        act.wait_ge(s_ready, b_val(b) * NS + (n + 1))
                        act.wait_ge(av_done, b_val(b) * NS + (n + 1))
                        nc.scalar.activation(E[:, n % PB, :], psum[S0 + n % SB][:, 0:CH], ACT.Exp).then_inc(exp_done, 1)
                        if n == HI_AT and has_keys:
                            keys_high(act, b + 2, b)
                        if n == TURN_AT and has_next:
                            max_high(act, b + 1)

                steps(act, step)

            @block.tensor
            def _(pe):
                pe.sem_inc(av_done, PB)
                pe.wait_ge(pads, BUFS)
                pe.wait_ge(consts, 16 * (2 + BUFS))
                pe.wait_ge(q_in[0], 32)
                pe.wait_ge(k_ready, 1)
                for f in range(NF):
                    max_piece(pe, FIRST, f)
                turn_max(pe, FIRST)

                def values(b, n):
                    g, t = divmod(n, KT)
                    pe.wait_ge(exp_done, b_val(b) * NS + (SB + n + 1))
                    if t == 0:
                        pe.wait_ge(norm_done, b_val(b) * H + HG * (g + 1))
                    nc.tensor.matmul(psum[A0 + g % 2][:, 0:CH], KV[b_mod(b)][:, t, :], E[:, n % PB, :],
                                     start=t == 0, stop=t == KT - 1).then_inc(av_done, 1)

                def step(b, has_next, has_keys):
                    r = b_mod(b)
                    pe.wait_ge(m_in, b_val(b) * 32 + 32)
                    for n in range(NS):
                        g, t = divmod(n, KT)
                        pe.wait_ge(exp_done, b_val(b) * NS + (n + 1))
                        out = psum[S0 + n % SB][:, 0:CH]
                        keys, cols = slice(t * P, (t + 1) * P), slice(g * CH, (g + 1) * CH)
                        nc.tensor.matmul(out, KH[r][:, keys], QS[r][:, cols], start=True, stop=False)
                        nc.tensor.matmul(out, KB[r][:, keys], QB[r][:, cols], start=False, stop=True).then_inc(s_ready, 1)
                        if has_next and n == F_AT:
                            pe.wait_ge(k_ready, b_val(b) + 2)
                            pe.wait_ge(q_in[b_mod(b + 1)], (b + 1).turn * 32 + 32)
                        if has_next and 0 <= n - F_AT < NF:
                            max_piece(pe, b + 1, n - F_AT)
                        if n >= 2:
                            values(b, n - 2)
                        if n == OUT_AT and b is not FIRST:
                            project(pe, Batch(b.turn, b.r - 1) if b.r else Batch(b.turn - 1, BUFS - 1))
                        if n == TURN_AT and has_next:
                            if b is not FIRST:
                                pe.wait_ge(res_done, b_val(b))
                            turn_max(pe, b + 1)
                    values(b, NS - 2)
                    values(b, NS - 1)

                steps(pe, step)
                project(pe, Batch(0, B - 1))

            @block.vector
            def _(v):
                v.sem_inc(norm_done, 2 * HG)
                for r in range(BUFS):
                    v.memset(as_f32(QS[r][:, H * S:]), 0.0)
                    v.memset(as_f32(KH[r][:, SK:]), 0.0)
                    v.memset(as_f32(KB[r][:, SK:]), 0.0)
                    v.memset(as_f32(KB[r][DC:DC + 2, 0:SK]), 1.0).then_inc(pads, 1)
                for f in range(NF):
                    reduce_piece(v, FIRST, f)
                batch_max(v, FIRST)
                max_low(v, FIRST)

                def step(b, has_next, has_keys):
                    todo = {}
                    for h in range(H - HG):
                        todo[KT * (h // HG + 1) + 3 + 2 * (h % HG)] = h
                    for n in range(NS):
                        if has_next and 0 <= n - F_AT < NF:
                            reduce_piece(v, b + 1, n - F_AT)
                        if n - F_AT == NF and has_next:
                            batch_max(v, b + 1)
                        if n == OUT_AT + 2 and b is not FIRST:
                            add_output(v, Batch(b.turn, b.r - 1) if b.r else Batch(b.turn - 1, BUFS - 1))
                        if n in todo:
                            normalise(v, b, todo[n])
                        if n == TURN_AT + 1 and has_next:
                            max_low(v, b + 1)
                    for h in range(H - HG, H):
                        normalise(v, b, h)

                steps(v, step)
                add_output(v, Batch(0, B - 1))


def router_scores(core, tag, XH, XL, weights, E):
    nc, psum = core.nc, core.psum
    WH, WL = weights
    for b in range(B):
        cols = slice(b * S, (b + 1) * S)
        todo = [(x[:, k, cols], w[:, k, :]) for k in range(KD) for x in (XH, XL) for w in (WH, WL)]
        for n, (x, w) in enumerate(todo):
            last = nc.tensor.matmul(psum[0][0:S, b * E:(b + 1) * E], x, w, start=n == 0, stop=n == len(todo) - 1)
    return last


class Chain:

    def __init__(self, eng, sem):
        self.eng, self.sem, self.done = eng, sem, 0

    def __call__(self, ins):
        self.done += 1
        ins.then_inc(self.sem, 1)
        self.eng.wait_ge(self.sem, self.done)


def route(core, dram, tag, XH, XL, E, C, grouped):
    nc, psum = core.nc, core.psum
    G = 4
    with ExitStack() as ctx:
        wr = fixed(ctx, nc, tag + "wr", [P, KD, E])
        WH = fixed(ctx, nc, tag + "wrh", [P, KD, E], F32R)
        WL = fixed(ctx, nc, tag + "wrl", [P, KD, E], F32R)
        iota = fixed(ctx, nc, tag + "iota", [S, E])
        sc = fixed(ctx, nc, tag + "sc", [S, B, E])
        top = fixed(ctx, nc, tag + "top", [S, B, 8])
        idx = fixed(ctx, nc, tag + "idx", [S, B, 8], U32)
        idf = fixed(ctx, nc, tag + "idf", [S, B, 8])
        one = fixed(ctx, nc, tag + "one", [S, B, E])
        two = fixed(ctx, nc, tag + "two", [S, B, E])
        w = fixed(ctx, nc, tag + "w", [S, 4, B])
        gs = fixed(ctx, nc, tag + "gs", [S, B, G])
        gt = fixed(ctx, nc, tag + "gt", [S, B, G])
        rank = fixed(ctx, nc, tag + "rank", [S, B, G])
        loaded = core.sem(tag + "loaded")
        parts = core.sem(tag + "parts")
        scores = core.sem(tag + "scores")
        chain = core.sem(tag + "chain")
        asked = core.sem(tag + "asked")
        given = core.sem(tag + "given")
        with nc.Block() as block:

            @block.sync
            def _(sp):
                sp.dma_start(wr[:], dram[tag + "router"]).then_inc(loaded, 16)
                sp.dma_start(iota[:], dram[tag + "iota"]).then_inc(loaded, 16)

            @block.tensor
            def _(pe):
                pe.wait_ge(parts, 1)
                router_scores(core, tag, XH, XL, (WH, WL), E).then_inc(scores, 1)

            @block.scalar
            def _(act):
                if grouped:
                    act.wait_ge(scores, 1)
                    nc.scalar.activation(sc[:].rearrange("p b e -> p (b e)"), psum[0][0:S, 0:B * E],
                                         ACT.Sigmoid).then_inc(given, 1)
                else:
                    act.wait_ge(asked, 1)
                    nc.scalar.activation(w[:, 1, :], w[:, 0, :], ACT.Exp).then_inc(given, 1)

            @block.vector
            def _(v):
                vec = nc.vector
                do = Chain(v, chain)
                v.wait_ge(loaded, 32)
                do(vec.tensor_copy(WH[:], wr[:]))
                vec.tensor_tensor(WL[:], wr[:], as_f32(WH[:]), ALU.subtract).then_inc(parts, 1)
                if grouped:
                    v.wait_ge(given, 1)
                    g = sc[:].rearrange("p b (g i) -> p b g i", g=G)
                    pairs = [(i, j) for i in range(G) for j in range(i + 1, G)]
                    for n, (i, j) in enumerate(pairs):
                        do(vec.tensor_tensor((gt if n else gs)[:], g[:, :, :, i], g[:, :, :, j], ALU.add))
                        if n:
                            do(vec.tensor_tensor(gs[:], gs[:], gt[:], ALU.max))
                    do(vec.memset(rank[:], 0.0))
                    for i in range(G):
                        for j in range(G):
                            if i != j:
                                do(vec.tensor_tensor(gt[:, :, i], gs[:, :, j], gs[:, :, i], ALU.is_ge if j < i else ALU.is_gt))
                                do(vec.tensor_tensor(rank[:, :, i], rank[:, :, i], gt[:, :, i], ALU.add))
                    do(vec.tensor_scalar(rank[:], rank[:], 2.0, None, ALU.is_lt))
                    for i in range(G):
                        do(vec.tensor_tensor(g[:, :, :, i], g[:, :, :, i], rank[:], ALU.mult))
                else:
                    v.wait_ge(scores, 1)
                    do(vec.tensor_copy(sc[:].rearrange("p b e -> p (b e)"), psum[0][0:S, 0:B * E]))
                for b in range(B):
                    vec.max(top[:, b, :], sc[:, b, :]).then_inc(chain, 1)
                do.done += B
                v.wait_ge(chain, do.done)
                for b in range(B):
                    vec.max_index(idx[:, b, :], top[:, b, :], sc[:, b, :]).then_inc(chain, 1)
                do.done += B
                v.wait_ge(chain, do.done)
                do(vec.tensor_copy(idf[:], idx[:]))
                if grouped:
                    do(vec.tensor_tensor(w[:, 0, :], top[:, :, 0], top[:, :, 1], ALU.add))
                    do(vec.tensor_scalar(w[:, 0, :], w[:, 0, :], 1e-20, None, ALU.add))
                    do(vec.reciprocal(w[:, 1, :], w[:, 0, :]))
                    do(vec.tensor_tensor(w[:, 2, :], top[:, :, 0], w[:, 1, :], ALU.mult))
                    do(vec.tensor_tensor(w[:, 3, :], top[:, :, 1], w[:, 1, :], ALU.mult))
                else:
                    vec.tensor_tensor(w[:, 0, :], top[:, :, 1], top[:, :, 0], ALU.subtract).then_inc(asked, 1)
                    v.wait_ge(given, 1)
                    do(vec.tensor_scalar(w[:, 0, :], w[:, 1, :], 1.0, None, ALU.add))
                    do(vec.reciprocal(w[:, 2, :], w[:, 0, :]))
                    do(vec.tensor_tensor(w[:, 3, :], w[:, 1, :], w[:, 2, :], ALU.mult))
                for n, hot in enumerate((one, two)):
                    do(vec.tensor_tensor(hot[:], iota[:].rearrange("p (o e) -> p o e", o=1).to_broadcast([S, B, E]),
                                         idf[:, :, n:n + 1].to_broadcast([S, B, E]), ALU.is_equal))
                    do(vec.tensor_tensor(hot[:], hot[:], w[:, 2 + n, :].rearrange("p (b o) -> p b o", o=1).to_broadcast([S, B, E]),
                                         ALU.mult))
                do(vec.tensor_tensor(C[:, 0:E * B].rearrange("p (e b) -> p b e", b=B), one[:], two[:], ALU.add))
                if grouped:
                    do(vec.memset(C[:, E * B:], 1.0))


def experts(core, dram, tag, X, XH, XL, C, E, NU, TR, NT, UPS):
    nc, psum = core.nc, core.psum
    I = TR * NT
    LAG = min(2, NT - 1)
    GB, AB = 2, 4
    with ExitStack() as ctx:
        stage_u = fixed(ctx, nc, tag + "stage_u", [P, KD, NU, I])
        stage_d = fixed(ctx, nc, tag + "stage_d", [TR, NT, D])
        UH = [fixed(ctx, nc, f"{tag}UH{u}", [P, KD, NU, I], F32R) for u in range(2)]
        UL = [fixed(ctx, nc, f"{tag}UL{u}", [P, KD, NU, I], F32R) for u in range(2)]
        DH = [fixed(ctx, nc, f"{tag}DH{u}", [TR, NT, D], F32R) for u in range(2)]
        DL = [fixed(ctx, nc, f"{tag}DL{u}", [TR, NT, D], F32R) for u in range(2)]
        G = fixed(ctx, nc, tag + "G", [TR, GB, CH])
        HF = fixed(ctx, nc, tag + "HF", [TR, GB, CH])
        HH = fixed(ctx, nc, tag + "HH", [TR, NT, CH], F32R)
        HL = fixed(ctx, nc, tag + "HL", [TR, NT, CH], F32R)
        unit = fixed(ctx, nc, tag + "unit", [P, NU, 1])
        unit_ready = core.sem(tag + "unit_ready")
        w_in = core.sem(tag + "w_in")
        w_hi = core.sem(tag + "w_hi")
        w_ready = core.sem(tag + "w_ready")
        up_ready = core.sem(tag + "up")
        g_ready = core.sem(tag + "g")
        h_ready = core.sem(tag + "h")
        hh_ready = core.sem(tag + "hh")
        hl_ready = core.sem(tag + "hl")
        down_done = core.sem(tag + "down")
        acc_done = core.sem(tag + "acc")
        FREE = (NC + 1) * NT

        def every_expert(eng, body):
            with eng.Fori(0, E // 2) as pair:
                for u in range(2):
                    body(pair * 2 + u, u)
            if E % 2:
                body(E - 1, 0)

        def every_step(eng, body):
            def chunks(e, u):
                with eng.Fori(0, NC) as c:
                    body(e * NC + c, e, u, c)
            every_expert(eng, chunks)

        with nc.Block() as block:

            @block.sync
            def _(sp):
                def load(e, u):
                    sp.wait_ge(w_ready, e + 1)
                    sp.dma_start(stage_u[:], dram[tag + "up"][e]).then_inc(w_in, 16)
                    sp.dma_start(stage_d[:], dram[tag + "down"][e]).then_inc(w_in, 16)
                every_expert(sp, load)

            @block.gpsimd
            def _(pool):
                pool.sem_inc(w_ready, 1)
                pool.memset(unit[:], 1.0).then_inc(unit_ready, 1)
                pool.wait_ge(unit_ready, 1)

                def split(e, u):
                    pool.wait_ge(w_in, e * 32 + 32)
                    pool.wait_ge(down_done, e * (NC * NT) + NT)
                    for k in range(KD):
                        nc.gpsimd.tensor_tensor(UH[u][:, k], stage_u[:, k], unit[:, :, 0:1].to_broadcast([P, NU, I]),
                                                ALU.mult).then_inc(w_hi, 1)
                    nc.gpsimd.tensor_tensor(DH[u][:], stage_d[:], unit[0:TR, 0:1, 0:1].to_broadcast([TR, NT, D]),
                                            ALU.mult).then_inc(w_hi, 1)
                    pool.wait_ge(w_hi, e * (KD + 1) + KD + 1)
                    for k in range(KD):
                        nc.gpsimd.tensor_tensor(UL[u][:, k], stage_u[:, k], as_f32(UH[u][:, k]), ALU.subtract)
                    nc.gpsimd.tensor_tensor(DL[u][:], stage_d[:], as_f32(DH[u][:]), ALU.subtract).then_inc(w_ready, 1)
                every_expert(pool, split)

            @block.tensor
            def _(pe):
                pe.sem_inc(down_done, FREE)

                def step(k, e, u, c):
                    def up(t):
                        if t == 0:
                            pe.wait_ge(w_ready, e + 2)
                        pe.wait_ge(h_ready, k * NT + (t + 1))
                        for n in range(NU):
                            cols = slice(t * TR, (t + 1) * TR)
                            last = split_products(nc, psum[GB * n + t % GB][0:TR, 0:CH],
                                                  [(UH[u][:, q, n, cols], UL[u][:, q, n, cols],
                                                    XH[:, q, bass.ts(c, CH)], XL[:, q, bass.ts(c, CH)]) for q in range(KD)])
                        last.then_inc(up_ready, 1)

                    def down(t):
                        pe.wait_ge(hl_ready, k * NT + (GB + t + 1))
                        if t == 0:
                            pe.wait_ge(acc_done, k * CB + CB)
                        for j in range(CB):
                            rows = slice(j * S, (j + 1) * S)
                            last = split_products(nc, psum[AB + j][0:S, 0:D],
                                                  [(HH[:, t, rows], HL[:, t, rows], DH[u][:, t, :], DL[u][:, t, :])],
                                                  first=t == 0, last=t == NT - 1)
                        last.then_inc(down_done, 1)

                    for t in range(NT + LAG):
                        if t < NT:
                            up(t)
                        if t >= LAG:
                            down(t - LAG)

                every_step(pe, step)

            @block.scalar
            def _(act):
                if NU == 1:
                    act.sem_inc(h_ready, GB)

                def step(k, e, u, c):
                    def gate(t):
                        act.wait_ge(up_ready, k * NT + (t + 1))
                        if NU == 2:
                            act.wait_ge(h_ready, k * NT + (t + 1))
                            nc.scalar.activation(G[:, t % GB, :], psum[t % GB][0:TR, 0:CH], ACT.Silu).then_inc(g_ready, 1)
                        else:
                            act.wait_ge(hl_ready, k * NT + (t + 1))
                            nc.scalar.activation(HF[:, t % GB, :], psum[t % GB][0:TR, 0:CH], ACT.Silu).then_inc(h_ready, 1)

                    def high(t):
                        act.wait_ge(h_ready, k * NT + (GB + t + 1))
                        act.wait_ge(down_done, k * NT + (NC * NT + t + 1))
                        nc.scalar.activation(HH[:, t, :], HF[:, t % GB, :], ACT.Copy).then_inc(hh_ready, 1)

                    for t in range(NT + 1):
                        if t < NT:
                            gate(t)
                        if t >= 1:
                            high(t - 1)
                every_step(act, step)

            @block.vector
            def _(v):
                if NU == 2:
                    v.sem_inc(h_ready, GB)
                v.sem_inc(hl_ready, GB)
                v.sem_inc(acc_done, CB)

                def step(k, e, u, c):
                    def hidden(t):
                        v.wait_ge(g_ready, k * NT + (t + 1))
                        v.wait_ge(hl_ready, k * NT + (t + 1))
                        nc.vector.tensor_tensor(HF[:, t % GB, :], psum[GB + t % GB][0:TR, 0:CH], G[:, t % GB, :],
                                                ALU.mult).then_inc(h_ready, 1)

                    def low(t):
                        v.wait_ge(hh_ready, k * NT + (t + 1))
                        nc.vector.tensor_tensor(HL[:, t, :], HF[:, t % GB, :], as_f32(HH[:, t, :]),
                                                ALU.subtract).then_inc(hl_ready, 1)

                    for t in range(NT + 1):
                        if t < NT and NU == 2:
                            hidden(t)
                        if t >= 1:
                            low(t - 1)
                    v.wait_ge(down_done, k * NT + (FREE + NT))
                    for j in range(CB):
                        x = X[:, bass.ds(c * CB + j, 1), :].rearrange("p o d -> p (o d)")
                        nc.vector.scalar_tensor_tensor(x, psum[AB + j][0:S, 0:D], C[:, bass.ds(e * B + c * CB + j, 1)], x,
                                                       ALU.mult, ALU.add).then_inc(acc_done, 1)
                every_step(v, step)


def gated_moe(core, dram, X, ident):
    nc, E, TR, NT = core.nc, 8, 116, 6
    with ExitStack() as ctx:
        XH = fixed(ctx, nc, "XH_b", [P, KD, B * S], F32R)
        XL = fixed(ctx, nc, "XL_b", [P, KD, B * S], F32R)
        C = fixed(ctx, nc, "C_b", [S, E * B])
        layernorm(core, "ln1_", X, ident, XH, XL)
        route(core, dram, "m0_", XH, XL, E, C, grouped=False)
        experts(core, dram, "m0_", X, XH, XL, C, E, 2, TR, NT, None)


def grouped_moe(core, dram, X, ident):
    nc, E, TR, NT = core.nc, 16, 88, 2
    with ExitStack() as ctx:
        XH = fixed(ctx, nc, "XH_d", [P, KD, B * S], F32R)
        XL = fixed(ctx, nc, "XL_d", [P, KD, B * S], F32R)
        C = fixed(ctx, nc, "C_d", [S, (E + 1) * B])
        layernorm(core, "ln3_", X, ident, XH, XL)
        route(core, dram, "m1_", XH, XL, E, C, grouped=True)
        experts(core, dram, "m1_", X, XH, XL, C, E + 1, 1, TR, NT, None)


def causal_attention(core, dram, X, ident):
    nc, psum = core.nc, core.psum
    HT = H // KD
    SCALE = HD ** -0.5
    with ExitStack() as ctx:
        XH = fixed(ctx, nc, "XH_c", [P, KD, B * S], F32R)
        XL = fixed(ctx, nc, "XL_c", [P, KD, B * S], F32R)
        layernorm(core, "ln2_", X, ident, XH, XL)
        wq = fixed(ctx, nc, "c_wq", [P, KD, D])
        wqh = fixed(ctx, nc, "c_wqh", [P, KD, D], F32R)
        wql = fixed(ctx, nc, "c_wql", [P, KD, D], F32R)
        wk = fixed(ctx, nc, "c_wk", [DC, D])
        wv = fixed(ctx, nc, "c_wv", [DC, D])
        wo = fixed(ctx, nc, "c_wo", [P, KD, D])
        lat = fixed(ctx, nc, "c_lat", [DC, B * S])
        mask = fixed(ctx, nc, "c_mask", [S, S])
        maskb = fixed(ctx, nc, "c_maskb", [S, S], BF16)
        identb = fixed(ctx, nc, "c_identb", [S, S], BF16)
        blocks = fixed(ctx, nc, "c_blocks", [P, HT])
        QT = fixed(ctx, nc, "c_QT", [P, KD, B * S])
        KTT = fixed(ctx, nc, "c_KT", [P, KD, B * S])
        V = fixed(ctx, nc, "c_V", [S, B, D])

        loaded = core.sem("ca_loaded")
        parts = core.sem("ca_parts")
        chain = core.sem("ca_chain")
        proj = core.sem("ca_proj")
        moved_a = core.sem("ca_moveda")
        moved_v = core.sem("ca_movedv")
        tiles = [("q", k, c) for c in range(NC) for k in range(KD)] + [("k", k, c) for c in range(NC) for k in range(KD)]
        tiles += [("v", b, 0) for b in range(B)]

        with nc.Block() as block:

            @block.sync
            def _(sp):
                for t, name in ((wq, "c_wq"), (wk, "c_wk"), (wv, "c_wv"), (wo, "c_wo"), (lat, "c_lat"),
                                (mask, "c_mask"), (blocks, "c_blocks")):
                    sp.dma_start(t[:], dram[name]).then_inc(loaded, 16)

            @block.tensor
            def _(pe):
                pe.wait_ge(loaded, 16 * 7)
                pe.wait_ge(parts, 1)
                for n, (kind, k, c) in enumerate(tiles):
                    if n >= 8:
                        pe.wait_ge(moved_v if n % 2 else moved_a, (n - 8) // 2 + 1)
                    out = psum[n % 8]
                    cols = slice(c * CH, (c + 1) * CH)
                    if kind == "q":
                        last = split_products(nc, out[:, 0:CH], [(wqh[:, j, k * P:(k + 1) * P], wql[:, j, k * P:(k + 1) * P],
                                                                  XH[:, j, cols], XL[:, j, cols]) for j in range(KD)])
                    elif kind == "k":
                        last = nc.tensor.matmul(out[:, 0:CH], wk[:, k * P:(k + 1) * P], lat[:, cols], start=True, stop=True)
                    else:
                        last = nc.tensor.matmul(out[0:S, 0:D], lat[:, k * S:(k + 1) * S], wv[:], start=True, stop=True)
                    last.then_inc(proj, 1)

            def place(n):
                kind, k, c = tiles[n]
                if kind == "v":
                    return V[:, k, :], psum[n % 8][0:S, 0:D]
                return (QT if kind == "q" else KTT)[:, k, c * CH:(c + 1) * CH], psum[n % 8][:, 0:CH]

            @block.scalar
            def _(act):
                for n in range(0, len(tiles), 2):
                    act.wait_ge(proj, n + 1)
                    nc.scalar.activation(*place(n), ACT.Copy).then_inc(moved_a, 1)

            @block.vector
            def _(v):
                do = Chain(v, chain)
                v.wait_ge(loaded, 16 * 7)
                do(nc.vector.tensor_copy(wqh[:], wq[:]))
                do(nc.vector.tensor_tensor(wql[:], wq[:], as_f32(wqh[:]), ALU.subtract))
                do(nc.vector.tensor_copy(maskb[:], mask[:]))
                nc.vector.tensor_copy(identb[:], ident[0:S, 0:S]).then_inc(parts, 1)
                for n in range(1, len(tiles), 2):
                    v.wait_ge(proj, n + 1)
                    nc.vector.tensor_copy(*place(n)).then_inc(moved_v, 1)

        qb = [fixed(ctx, nc, f"c_qb{u}", [P, S]) for u in range(2)]
        kb = [fixed(ctx, nc, f"c_kb{u}", [P, HT, S]) for u in range(2)]
        nmax = [fixed(ctx, nc, f"c_nmax{u}", [S, 2, HT]) for u in range(2)]
        sums = fixed(ctx, nc, "c_sums", [S, 2, H])
        rsum = fixed(ctx, nc, "c_rsum", [S, H])
        PR = [fixed(ctx, nc, f"c_PR{u}", [S, HT, S]) for u in range(2)]
        PT = [fixed(ctx, nc, f"c_PT{u}", [S, HT, S]) for u in range(2)]
        O = fixed(ctx, nc, "c_O", [S, D])
        OT = fixed(ctx, nc, "c_OT", [P, KD, S])
        HB = HT // 2
        SC, TB, OB, LB = 0, 4, 6, 7

        ops_ready = core.sem("cb_ops")
        s_ready = core.sem("cb_s")
        max_ready = core.sem("cb_max")
        neg_ready = core.sem("cb_neg")
        e_ready = core.sem("cb_e")
        t_ready = core.sem("cb_t")
        tc_act = core.sem("cb_tca")
        tc_dve = core.sem("cb_tcv")
        o_ready = core.sem("cb_o")
        r_ready = core.sem("cb_r")
        on_ready = core.sem("cb_on")
        ot_ready = core.sem("cb_ot")
        otc_ready = core.sem("cb_otc")
        y_ready = core.sem("cb_y")
        x_done = core.sem("cb_x")

        def steps(eng, body):
            for i in (0, 1):
                body(i, i % 2)
            with eng.Fori(0, (B - 4) // 2) as j:
                for w in range(2):
                    body(j * 2 + (2 + w), w)
            for i in range(B - 2, B + 2):
                body(i, i % 2)

        def has(i, first, last):
            return not isinstance(i, int) or first <= i <= last

        def bank_heads(ap):
            return ap.rearrange("p (h s) -> p h s", s=S)

        with nc.Block() as block:

            @block.tensor
            def _(pe):
                def scores(i, u):
                    n = i * 2 + u
                    pe.wait_ge(ops_ready, n + 1)
                    if has(i, 1, B):
                        pe.wait_ge(e_ready, n * HT - HT)
                    for g in range(2):
                        out = psum[SC + 2 * u + g][0:S, 0:HB * S]
                        nc.tensor.matmul(out, qb[u][:], kb[u][:, g * HB:(g + 1) * HB, :].rearrange("p h s -> p (h s)"),
                                         start=True, stop=False)
                        last = nc.tensor.matmul(out, identb[:],
                                                maskb[:].rearrange("p (o s) -> p o s", o=1).to_broadcast([S, HB, S]),
                                                start=False, stop=True)
                    last.then_inc(s_ready, 1)

                def turn(n, u, first):
                    pe.wait_ge(e_ready, n * HT + HT)
                    if not first:
                        pe.wait_ge(tc_act, n)
                        pe.wait_ge(tc_dve, n)
                    for h in range(HT):
                        ins = nc.tensor.transpose(psum[TB + h // HB][0:S, (h % HB) * S:(h % HB + 1) * S], PR[u][:, h, :],
                                                  ident[0:S, 0:S])
                        if h % HB == HB - 1:
                            ins.then_inc(t_ready, 1)

                def values(i, n, u):
                    pe.wait_ge(tc_act, n + 1)
                    pe.wait_ge(tc_dve, n + 1)
                    if u == 0 and has(i, 2, B):
                        pe.wait_ge(on_ready, i - 1)
                    for h in range(HT):
                        d = (u * HT + h) * HD
                        last = nc.tensor.matmul(psum[OB][0:S, d:d + HD], PT[u][:, h, :], V[:, i - 1, d:d + HD],
                                                start=True, stop=True)
                    last.then_inc(o_ready, 1)

                def step(i, w):
                    n = i * 2
                    if has(i, 0, B - 1):
                        scores(i, 0)
                    if has(i, 2, B + 1):
                        pe.wait_ge(on_ready, i - 1)
                        if has(i, 3, B + 1):
                            pe.wait_ge(x_done, i - 2)
                        for k in range(KD):
                            last = nc.tensor.transpose(psum[LB][:, k * S:(k + 1) * S], O[:, k * P:(k + 1) * P], ident[0:S, 0:S])
                        last.then_inc(ot_ready, 1)
                    if has(i, 1, B):
                        turn(n - 1, 1, False)
                        values(i, n - 2, 0)
                    if has(i, 0, B - 1):
                        scores(i, 1)
                        turn(n, 0, isinstance(i, int) and i == 0)
                    if has(i, 2, B + 1):
                        pe.wait_ge(otc_ready, i - 1)
                        for k in range(KD):
                            last = nc.tensor.matmul(psum[LB][0:S, 0:D], OT[:, k, :], wo[:, k, :], start=k == 0, stop=k == KD - 1)
                        last.then_inc(y_ready, 1)
                    if has(i, 1, B):
                        values(i, n - 1, 1)
                steps(pe, step)

            @block.scalar
            def _(act):
                def exps(i, u, w):
                    n = i * 2 + u
                    act.wait_ge(neg_ready, n + 1)
                    if has(i, 1, B):
                        act.wait_ge(t_ready, n * 2 - 2)
                    if has(i, 2, B):
                        act.wait_ge(r_ready, i - 1)
                    for h in range(HT):
                        nc.scalar.activation(PR[u][:, h, :], psum[SC + 2 * u + h // HB][0:S, (h % HB) * S:(h % HB + 1) * S],
                                             ACT.Exp, bias=nmax[u][:, 1, h:h + 1], scale=SCALE,
                                             accum_out=sums[:, w, u * HT + h:u * HT + h + 1]).then_inc(e_ready, 1)

                def move(n, u):
                    act.wait_ge(t_ready, n * 2 + 2)
                    nc.scalar.activation(PT[u][:, 0:HB, :], bank_heads(psum[TB][0:S, 0:HB * S]), ACT.Copy).then_inc(tc_act, 1)

                def step(i, w):
                    n = i * 2
                    if has(i, 0, B - 1):
                        exps(i, 0, w)
                    if has(i, 1, B):
                        move(n - 1, 1)
                    if has(i, 2, B + 1):
                        act.wait_ge(ot_ready, i - 1)
                        if has(i, 3, B + 1):
                            act.wait_ge(y_ready, i - 2)
                        nc.scalar.activation(OT[:], bank_heads(psum[LB][:, 0:KD * S]), ACT.Copy).then_inc(otc_ready, 1)
                    if has(i, 0, B - 1):
                        exps(i, 1, w)
                        move(n, 0)
                steps(act, step)

            @block.vector
            def _(v):
                def operands(i, u):
                    n = i * 2 + u
                    if has(i, 1, B):
                        v.wait_ge(s_ready, n - 1)
                    nc.vector.tensor_tensor(kb[u][:], KTT[:, u:u + 1, bass.ts(i, S)].to_broadcast([P, HT, S]),
                                            blocks[:].rearrange("p (h o) -> p h o", o=1).to_broadcast([P, HT, S]), ALU.mult)
                    nc.vector.tensor_copy(qb[u][:], QT[:, u, bass.ts(i, S)]).then_inc(ops_ready, 1)

                def maxima(i, u):
                    n = i * 2 + u
                    v.wait_ge(s_ready, n + 1)
                    if has(i, 1, B):
                        v.wait_ge(e_ready, n * HT - HT)
                    for g in range(2):
                        nc.vector.tensor_reduce(nmax[u][:, 0, g * HB:(g + 1) * HB],
                                                bank_heads(psum[SC + 2 * u + g][0:S, 0:HB * S]), AX.X,
                                                ALU.max).then_inc(max_ready, 1)
                    v.wait_ge(max_ready, n * 2 + 2)
                    nc.vector.tensor_scalar(nmax[u][:, 1, :], nmax[u][:, 0, :], -SCALE, None, ALU.mult).then_inc(neg_ready, 1)

                def move(n, u):
                    v.wait_ge(t_ready, n * 2 + 2)
                    nc.vector.tensor_copy(PT[u][:, HB:, :], bank_heads(psum[TB + 1][0:S, 0:HB * S])).then_inc(tc_dve, 1)

                operands(0, 0)
                operands(0, 1)

                def step(i, w):
                    n = i * 2
                    if has(i, 0, B - 1):
                        maxima(i, 0)
                    if has(i, 0, B - 2):
                        operands(i + 1, 0)
                    if has(i, 1, B):
                        move(n - 1, 1)
                    if has(i, 0, B - 1):
                        maxima(i, 1)
                    if has(i, 0, B - 2):
                        operands(i + 1, 1)
                    if has(i, 0, B - 1):
                        move(n, 0)
                    if has(i, 2, B + 1):
                        v.wait_ge(y_ready, i - 1)
                        nc.vector.tensor_tensor(X[:, i - 2, :], psum[LB][0:S, 0:D], X[:, i - 2, :], ALU.add).then_inc(x_done, 1)
                    if has(i, 1, B):
                        if has(i, 2, B):
                            v.wait_ge(on_ready, i - 1)
                        v.wait_ge(e_ready, n * HT)
                        nc.vector.reciprocal(rsum[:], sums[:, 1 - w, :]).then_inc(r_ready, 1)
                        v.wait_ge(r_ready, i)
                        v.wait_ge(o_ready, n)
                        if has(i, 2, B):
                            v.wait_ge(ot_ready, i - 1)
                        nc.vector.tensor_tensor(O[:].rearrange("p (h d) -> p h d", h=H),
                                                psum[OB][0:S, 0:D].rearrange("p (h d) -> p h d", h=H),
                                                rsum[:].rearrange("p (h o) -> p h o", o=1).to_broadcast([S, H, HD]),
                                                ALU.mult).then_inc(on_ready, 1)
                steps(v, step)


def model(nc, dram, out):
    with ExitStack() as ctx:
        core = Core(nc, ctx)
        X = fixed(ctx, nc, "X", [S, B, D])
        ident = fixed(ctx, nc, "ident", [P, P])
        loaded = core.sem("loaded")
        stored = core.sem("stored")
        queries = nc.dram_tensor("queries", (B, P, H, S), F32).ap()
        with nc.Block() as block:

            @block.sync
            def _(sp):
                sp.dma_start(X[:], dram["x"].rearrange("b s d -> s b d")).then_inc(loaded, 16)
                sp.dma_start(ident[:], dram["ident"]).then_inc(loaded, 16)
                sp.wait_ge(loaded, 32)

        with ExitStack() as layer:
            BB = fixed(layer, nc, "BB", [P, H // 2, D])
            with ExitStack() as stage:
                XH = fixed(stage, nc, "XH_a", [P, KD, B * S], F32R)
                XL = fixed(stage, nc, "XL_a", [P, KD, B * S], F32R)
                AH = fixed(stage, nc, "AH", [P, KD, H, DQ], F32R)
                AL = fixed(stage, nc, "AL", [P, KD, H, DQ], F32R)
                M2 = fixed(stage, nc, "M2", [HALF, 2, H, P])
                layernorm(core, "ln0_", X, ident, XH, XL)
                fold_weights(core, dram, AH, AL, M2, BB)
                latent_queries(core, dram, XH, XL, AH, AL, M2, queries)
            latent_attention(core, dram, X, ident, queries, BB)
        gated_moe(core, dram, X, ident)
        causal_attention(core, dram, X, ident)
        grouped_moe(core, dram, X, ident)
        with nc.Block() as block:

            @block.sync
            def _(sp):
                sp.dma_start(out.rearrange("b s d -> s b d"), X[:]).then_inc(stored, 16)
                sp.wait_ge(stored, 16)


def rope_tables(length, dim):
    import numpy as np
    inv = (np.float32(1.0) / np.power(np.float32(10000.0), np.arange(0, dim, 2, dtype=np.float32) / np.float32(dim)))
    f = np.arange(length, dtype=np.float32)[:, None] * inv.astype(np.float32)[None, :]
    return np.repeat(np.sin(f), 2, axis=-1), np.repeat(np.cos(f), 2, axis=-1)


def layouts(inputs):
    import numpy as np
    a = {k: np.asarray(v) for k, v in inputs.items()}
    T = np.ascontiguousarray
    out = {
        "x": a["x"],
        "Wq": a["L0_xattn_Wq"],
        "w_kc_q": a["L0_xattn_w_kc_q"],
        "w_kc_kv": a["L0_xattn_w_kc_kv"],
        "W_qrT": T(a["L0_xattn_W_qr"].transpose(2, 0, 1)),
        "W_krT": T(a["L0_xattn_W_kr"].transpose(2, 0, 1)),
        "WoT": T(a["L0_xattn_Wo"].T),
        "ident": np.eye(P, dtype=np.float32),
    }
    sin, cos = rope_tables(S, DQ)
    sin, cos = sin.T, cos.T
    out["rope_q"] = T(np.stack([cos[:HALF], -sin[:HALF], cos[HALF:], sin[HALF:]], axis=1))
    ctxT = a["ctx_512"].transpose(0, 2, 1)
    swapped = np.concatenate([ctxT[:, DC // 2:], ctxT[:, :DC // 2]], axis=1)
    out["ctx_T"] = T(np.stack([np.concatenate([ctxT, ctxT], axis=1), np.concatenate([swapped, swapped], axis=1)], axis=2))
    padded = np.zeros((B, SKP, DC), np.float32)
    padded[:, :SK] = a["ctx_512"]
    out["ctx_k"] = T(padded.reshape(B, KT, P, DC).transpose(0, 2, 1, 3))
    sin, cos = rope_tables(SK, DC)
    sign = np.where(np.arange(DC) < DC // 2, -1.0, 1.0).astype(np.float32)
    sin = sin * sign
    out["rope_T"] = T(np.stack([np.concatenate([cos.T, cos.T]), np.concatenate([sin.T, sin.T])], axis=1))
    table = np.zeros((2, SKP, DC), np.float32)
    table[0, :SK], table[1, :SK] = cos, sin
    out["rope_k"] = T(table.reshape(2, KT, P, DC).transpose(2, 0, 1, 3))
    ones = np.zeros((SKP, DC), np.float32)
    ones[:SK] = 1.0
    out["key_ones"] = T(ones.reshape(KT, P, DC).transpose(1, 0, 2))
    more_layouts(a, out)
    return out


def more_layouts(a, out):
    import numpy as np
    T = np.ascontiguousarray

    def by_part(w, ni):
        return w.reshape(w.shape[0], KD, P, ni).transpose(0, 2, 1, 3)

    E, I, NI, TR = 8, 688, 696, 116
    gu = np.zeros((E, P, KD, 2, NI), np.float32)
    gu[:, :, :, 0, :I] = by_part(a["L0_ffn_Wg"].transpose(0, 2, 1), I)
    gu[:, :, :, 1, :I] = by_part(a["L0_ffn_Wu"].transpose(0, 2, 1), I)
    out["m0_up"] = gu
    wd = np.zeros((E, NI, D), np.float32)
    wd[:, :I] = a["L0_ffn_Wd"].transpose(0, 2, 1)
    out["m0_down"] = T(wd.reshape(E, NI // TR, TR, D).transpose(0, 2, 1, 3))
    out["m0_router"] = T(a["L0_ffn_router_w"].T.reshape(KD, P, E).transpose(1, 0, 2))
    out["m0_iota"] = np.tile(np.arange(E, dtype=np.float32), (S, 1))

    wkv = a["L1_xattn_Wkv_expand"]
    out["c_wq"] = T(a["L1_xattn_Wq"].T.reshape(KD, P, D).transpose(1, 0, 2))
    out["c_wk"], out["c_wv"] = T(wkv[:D].T), T(wkv[D:].T)
    out["c_wo"] = T(a["L1_xattn_Wout"].T.reshape(KD, P, D).transpose(1, 0, 2))
    out["c_lat"] = T(a["ctx_512"][:, :S].transpose(2, 0, 1).reshape(DC, B * S))
    out["c_mask"] = np.triu(np.full((S, S), -3.0e38, np.float32), 1)
    out["c_blocks"] = np.repeat(np.eye(H // KD, dtype=np.float32), HD, axis=0)

    E, I, TR = 16, 176, 88
    w1 = np.concatenate([a["L1_ffn_w1"], a["L1_ffn_sw1"]])
    w2 = np.concatenate([a["L1_ffn_w2"], a["L1_ffn_sw2"]])
    out["m1_up"] = T(by_part(w1, I).reshape(E + 1, P, KD, 1, I))
    out["m1_down"] = T(w2.reshape(E + 1, I // TR, TR, D).transpose(0, 2, 1, 3))
    out["m1_router"] = T(a["L1_ffn_gate_w"].T.reshape(KD, P, E).transpose(1, 0, 2))
    out["m1_iota"] = np.tile(np.arange(E, dtype=np.float32), (S, 1))


def kernel(**inputs):
    import numpy as _np
    import concourse.bacc as _bacc
    from concourse import mybir as _mybir
    from concourse.bass_utils import run_bass_kernel_spmd as _run

    nc = _bacc.Bacc("TRN2", target_bir_lowering=False, num_devices=1)
    arrays, dram = {}, {}
    for name, a in layouts(inputs).items():
        a = _np.ascontiguousarray(a)
        arrays[f"in_{name}"] = a
        dram[name] = nc.dram_tensor(f"in_{name}", a.shape, _mybir.dt.from_np(a.dtype), kind="ExternalInput").ap()
    out = nc.dram_tensor("out", (B, S, D), F32, kind="ExternalOutput").ap()
    model(nc, dram, out)
    r = _run(nc, [arrays], core_ids=[0])
    return r.results[0]["out"]
```

```python
from contextlib import ExitStack

import concourse.bass as bass
from concourse import mybir

ALU = mybir.AluOpType
ACT = mybir.ActivationFunctionType
F32 = mybir.dt.float32
F32R = mybir.dt.float32r
BF16 = mybir.dt.bfloat16
U32 = mybir.dt.uint32
AX = mybir.AxisListType

P = 128
B, S, D = 16, 100, 256
SK, DC = 1444, 64
H = 16
K0, DQ, R0 = 128, 192, 64
KD = D // P
CB = 4
CH = CB * S
NC = B // CB
HALF = DQ // 2
KT = -(-SK // P)
SKP = KT * P
HD = D // H
EPS = 1e-5
E0, E1 = 8, 16
TOK = 256
PSUM_COLS = 512


def most_tiles(experts):
    return (2 * B * S + experts * (TOK - 1)) // TOK


ROWS = TOK * (-(-B * S // TOK) + most_tiles(E1))


class Core:

    def __init__(self, nc, ctx):
        self.nc, self.ctx = nc, ctx
        self.psum = [ctx.enter_context(nc.psum_tensor(f"bank{i}", [P, PSUM_COLS], F32)) for i in range(8)]

        self.sems = []

    def sem(self, name):
        self.sems.append(self.nc.alloc_semaphore(name=name))
        return self.sems[-1]

    def release(self):
        self.nc.clear_and_free_semaphores(self.sems)
        self.nc.all_engine_barrier()
        self.sems = []


def fixed(ctx, nc, name, shape, dtype=F32):
    return ctx.enter_context(nc.sbuf_tensor(name, shape, dtype))


def as_f32(ap):
    return ap.bitcast(F32)


def layernorm(core, tag, X, XN, ident, XH, XL, loads=None):
    nc, psum = core.nc, core.psum
    with ExitStack() as ctx:
        stats = fixed(ctx, nc, tag + "stats", [S, B, 6])
        small = fixed(ctx, nc, tag + "small", [S, 8, B])
        dve = core.sem(tag + "dve")
        var_ready = core.sem(tag + "var")
        std_ready = core.sem(tag + "std")
        xn_ready = core.sem(tag + "xn")
        turned = core.sem(tag + "turned")
        hi_ready = core.sem(tag + "hi")
        with nc.Block() as block:

            @block.sync
            def _(sp):
                if loads:
                    loads(sp)

            @block.vector
            def _(v):
                for b in range(B):
                    nc.vector.bn_stats(stats[:, b, :], X[:, b, :]).then_inc(dve, 1)
                mean, var, std, rstd, diff, sq, y2 = (small[:, i, :] for i in range(7))
                me, qe, mo, qo = (stats[:, :, i] for i in (1, 2, 4, 5))
                step = B

                def chained(ins):
                    nonlocal step
                    step += 1
                    ins.then_inc(dve, 1)
                    v.wait_ge(dve, step)

                v.wait_ge(dve, step)
                chained(nc.vector.tensor_tensor(mean, me, mo, ALU.add))
                chained(nc.vector.tensor_scalar(mean, mean, 0.5, None, ALU.mult))
                chained(nc.vector.tensor_tensor(diff, me, mo, ALU.subtract))
                chained(nc.vector.tensor_tensor(diff, diff, diff, ALU.mult))
                chained(nc.vector.tensor_tensor(sq, qe, qo, ALU.add))
                chained(nc.vector.tensor_scalar(sq, sq, 1.0 / D, EPS, ALU.mult, ALU.add))
                nc.vector.scalar_tensor_tensor(var, diff, 0.25, sq, ALU.mult, ALU.add).then_inc(var_ready, 1)
                v.wait_ge(std_ready, 1)
                v.wait_ge(var_ready, 1)
                chained(nc.vector.reciprocal(rstd, std))
                chained(nc.vector.tensor_tensor(y2, rstd, rstd, ALU.mult))
                chained(nc.vector.tensor_tensor(y2, y2, var, ALU.mult))
                chained(nc.vector.tensor_scalar(y2, y2, -0.5, 1.5, ALU.mult, ALU.add))
                chained(nc.vector.tensor_tensor(rstd, rstd, y2, ALU.mult))
                for b in range(B):
                    nc.vector.tensor_scalar(XN[:, b, :], X[:, b, :], small[:, 0, b:b + 1], small[:, 3, b:b + 1],
                                            ALU.subtract, ALU.mult).then_inc(xn_ready, 1)
                for n in range(NC * KD):
                    c, k = divmod(n, KD)
                    v.wait_ge(hi_ready, n + 1)
                    hi = XH[:, k, c * CH:(c + 1) * CH]
                    nc.vector.tensor_tensor(XL[:, k, c * CH:(c + 1) * CH], psum[n][:, 0:CH], as_f32(hi), ALU.subtract)

            @block.scalar
            def _(act):
                act.wait_ge(var_ready, 1)
                nc.scalar.activation(small[:, 2, :], small[:, 1, :], ACT.Sqrt).then_inc(std_ready, 1)
                for n in range(NC * KD):
                    c, k = divmod(n, KD)
                    act.wait_ge(turned, n + 1)
                    nc.scalar.activation(XH[:, k, c * CH:(c + 1) * CH], psum[n][:, 0:CH], ACT.Copy).then_inc(hi_ready, 1)

            @block.tensor
            def _(pe):
                for n in range(NC * KD):
                    c, k = divmod(n, KD)
                    pe.wait_ge(xn_ready, (c + 1) * CB)
                    for t in range(CB):
                        last = nc.tensor.transpose(psum[n][:, t * S:(t + 1) * S],
                                                   XN[:, c * CB + t, k * P:(k + 1) * P], ident[0:S, 0:S])
                    last.then_inc(turned, 1)


def split_products(nc, out, parts, first=True, last=True):
    todo = []
    for lh, ll, rh, rl in parts:
        todo += [(lh, rh), (lh, rl), (ll, rh)]
    for n, (lhs, rhs) in enumerate(todo):
        ins = nc.tensor.matmul(out, lhs, rhs, start=first and n == 0, stop=last and n == len(todo) - 1)
    return ins


class FoldInputs:

    def __init__(self, core, ctx, dram):
        nc = core.nc
        self.dram = dram
        self.wq = fixed(ctx, nc, "wq", [K0, H, D])
        self.wkq = fixed(ctx, nc, "wkq", [K0, H, DQ])
        self.wqr = fixed(ctx, nc, "wqr", [R0, H, DQ])
        self.wkr = fixed(ctx, nc, "wkr", [R0, H, DC])
        self.wo = fixed(ctx, nc, "wo", [K0, H, D])
        self.wkv = fixed(ctx, nc, "wkv", [K0, H, DC])
        self.in_q = core.sem("fw_in_q")
        self.in_r = core.sem("fw_in_r")
        self.in_o = core.sem("fw_in_o")

    def load(self, sp):
        dram = self.dram
        sp.dma_start(self.wq[:], dram["Wq"].rearrange("(h k) d -> k h d", k=K0)).then_inc(self.in_q, 16)
        sp.dma_start(self.wkq[:], dram["w_kc_q"].rearrange("h k q -> k h q")).then_inc(self.in_q, 16)
        sp.dma_start(self.wqr[:], dram["W_qrT"]).then_inc(self.in_r, 16)
        sp.dma_start(self.wkr[:], dram["W_krT"]).then_inc(self.in_r, 16)
        sp.dma_start(self.wo[:], dram["WoT"].rearrange("(h k) d -> k h d", k=K0)).then_inc(self.in_o, 16)
        sp.dma_start(self.wkv[:], dram["w_kc_kv"].rearrange("h k q -> k h q")).then_inc(self.in_o, 16)


def fold_weights(core, w, AH, AL, M2, BB):
    nc, psum = core.nc, core.psum
    wq, wkq, wqr, wkr, wo, wkv = w.wq, w.wkq, w.wqr, w.wkr, w.wo, w.wkv
    a_ready = core.sem("fw_a")
    a_hi = core.sem("fw_ahi")
    a_lo = core.sem("fw_alo")
    mb_ready = core.sem("fw_mb")
    mb_out = core.sem("fw_mbout")
    with nc.Block() as block:

        @block.tensor
        def _(pe):
            pe.wait_ge(w.in_q, 32)
            pe.wait_ge(w.in_r, 32)
            pe.wait_ge(w.in_o, 32)
            for h in range(H):
                if h >= 2:
                    pe.wait_ge(a_lo, h - 1)
                    pe.wait_ge(mb_out, h - 1)
                for k in range(KD):
                    last = nc.tensor.matmul(psum[h % 2][:, k * DQ:(k + 1) * DQ], wq[:, h, k * P:(k + 1) * P],
                                            wkq[:, h, :], start=True, stop=True)
                last.then_inc(a_ready, 1)
                for half in range(2):
                    nc.tensor.matmul(psum[2 + h % 2][0:HALF, half * P:(half + 1) * P],
                                     wqr[:, h, half * HALF:(half + 1) * HALF],
                                     wkr[:, h, :].rearrange("p (o d) -> p o d", o=1).to_broadcast([R0, 2, DC]),
                                     start=True, stop=True)
                nc.tensor.matmul(psum[4 + h % 2][0:DC, 0:D], wkv[:, h, :], wo[:, h, :],
                                 start=True, stop=True).then_inc(mb_ready, 1)

        @block.scalar
        def _(act):
            for h in range(H):
                act.wait_ge(a_ready, h + 1)
                nc.scalar.activation(AH[:, :, h, :], psum[h % 2][:, 0:KD * DQ].rearrange("p (k q) -> p k q", k=KD),
                                     ACT.Copy).then_inc(a_hi, 1)

        @block.vector
        def _(v):
            for h in range(H):
                v.wait_ge(a_hi, h + 1)
                nc.vector.tensor_tensor(AL[:, :, h, :], psum[h % 2][:, 0:KD * DQ].rearrange("p (k q) -> p k q", k=KD),
                                        as_f32(AH[:, :, h, :]), ALU.subtract).then_inc(a_lo, 1)
                v.wait_ge(mb_ready, h + 1)
                nc.vector.tensor_copy(M2[:, :, h, :],
                                      psum[2 + h % 2][0:HALF, 0:2 * P].rearrange("p (a c) -> p a c", a=2))
                nc.vector.tensor_copy(BB[(h % 2) * DC:(h % 2 + 1) * DC, h // 2, :],
                                      psum[4 + h % 2][0:DC, 0:D]).then_inc(mb_out, 1)


def latent_queries(core, dram, XH, XL, AH, AL, M2, queries, rows_in):
    nc, psum = core.nc, core.psum
    SLOTS, BUFS = 4, 2
    with ExitStack() as ctx:
        rope = fixed(ctx, nc, "rope_q", [HALF, 4, S])
        prod = fixed(ctx, nc, "rope_prod", [HALF, 2, 4, CH])
        rot = fixed(ctx, nc, "rotated", [HALF, 2, 2, CH])
        out = fixed(ctx, nc, "q_out", [P, SLOTS, CH], F32R)
        zeros = fixed(ctx, nc, "zeros", [P, 14, D])
        zeros_set = core.sem("lq_zeros")
        cleared = core.sem("lq_cleared")
        rope_in = core.sem("lq_rope")
        q_ready = core.sem("lq_q")
        mul_done = core.sem("lq_mul")
        rot_done = core.sem("lq_rot")
        qq_ready = core.sem("lq_qq")
        lo_done = core.sem("lq_lo")
        hi_done = core.sem("lq_hi")
        sent = [core.sem(f"lq_sent{i}") for i in range(SLOTS)]
        with nc.Block() as block:

            @block.sync
            def _(sp):
                sp.dma_start(rope[:], dram["rope_q"]).then_inc(rope_in, 16)
                sp.wait_ge(zeros_set, 1)
                for r in range(0, ROWS // P, 14):
                    sp.dma_start(rows_in[r * P:(r + 14) * P].rearrange("(p j) d -> p j d", p=P), zeros[:]).then_inc(cleared, 16)
                for s in sent:
                    sp.sem_inc(s, 16)
                with sp.Fori(0, NC) as c:
                    for h in range(H):
                        sp.wait_ge(lo_done, c * H + (BUFS + h + 1))
                        sp.dma_start(queries[bass.ts(c, CB)].rearrange("b p h s -> p h b s")[:, h],
                                     as_f32(out[:, h % SLOTS, :]).rearrange("p (b s) -> p b s", b=CB)).then_inc(sent[h % SLOTS], 16)
                for s in sent:
                    sp.wait_ge(s, 16 * (1 + NC * H // SLOTS))
                sp.wait_ge(cleared, 16 * (ROWS // P // 14))

            @block.tensor
            def _(pe):
                def narrow(c, h):
                    pe.wait_ge(rot_done, c * H + (BUFS + h + 1))
                    pe.wait_ge(lo_done, c * H + (h + 1))
                    for half in range(2):
                        last = nc.tensor.matmul(psum[4 + h % 2][:, 0:CH], M2[:, half, h, :], rot[:, h % 2, half, :],
                                                start=half == 0, stop=half == 1)
                    last.then_inc(qq_ready, 1)

                pe.sem_inc(qq_ready, BUFS)
                with pe.Fori(0, NC) as c:
                    for h in range(H):
                        pe.wait_ge(mul_done, c * H + (h + 1))
                        for half in range(2):
                            last = split_products(nc, psum[2 * (h % 2) + half][0:HALF, 0:CH],
                                                  [(AH[:, k, h, half * HALF:(half + 1) * HALF],
                                                    AL[:, k, h, half * HALF:(half + 1) * HALF],
                                                    XH[:, k, bass.ts(c, CH)], XL[:, k, bass.ts(c, CH)]) for k in range(KD)])
                        last.then_inc(q_ready, 1)
                        if h >= 1:
                            narrow(c, h - 1)
                    narrow(c, H - 1)

            @block.vector
            def _(v):
                v.memset(zeros[:], 0.0).then_inc(zeros_set, 1)
                v.wait_ge(rope_in, 16)
                v.sem_inc(mul_done, BUFS)
                v.sem_inc(lo_done, BUFS)

                def low(c, h):
                    v.wait_ge(hi_done, c * H + (h + 1))
                    nc.vector.tensor_tensor(out[DC:P, h % SLOTS, :], psum[4 + h % 2][DC:P, 0:CH],
                                            as_f32(out[DC:P, h % SLOTS, :]), ALU.subtract).then_inc(lo_done, 1)

                with v.Fori(0, NC) as c:
                    for h in range(H):
                        v.wait_ge(q_ready, c * H + (h + 1))
                        v.wait_ge(rot_done, c * H + (h + 1))
                        for n, half in enumerate((0, 1, 1, 0)):
                            last = nc.vector.tensor_tensor(
                                prod[:, h % 2, n, :].rearrange("p (b s) -> p b s", b=CB),
                                psum[2 * (h % 2) + half][0:HALF, 0:CH].rearrange("p (b s) -> p b s", b=CB),
                                rope[:, n:n + 1, :].to_broadcast([HALF, CB, S]), ALU.mult)
                        last.then_inc(mul_done, 1)
                        if h >= 2:
                            low(c, h - 2)
                    low(c, H - 2)
                    low(c, H - 1)

            @block.gpsimd
            def _(pool):
                pool.sem_inc(rot_done, BUFS)
                with pool.Fori(0, NC) as c:
                    for h in range(H):
                        pool.wait_ge(mul_done, c * H + (BUFS + h + 1))
                        pool.wait_ge(qq_ready, c * H + (h + 1))
                        for half in range(2):
                            last = nc.gpsimd.tensor_tensor(rot[:, h % 2, half, :], prod[:, h % 2, 2 * half, :],
                                                           prod[:, h % 2, 2 * half + 1, :], ALU.add)
                        last.then_inc(rot_done, 1)

            @block.scalar
            def _(act):
                with act.Fori(0, NC) as c:
                    for h in range(H):
                        act.wait_ge(qq_ready, c * H + (BUFS + h + 1))
                        act.wait_ge(sent[h % SLOTS], c * (16 * H // SLOTS) + 16 * (h // SLOTS + 1))
                        nc.scalar.activation(out[:, h % SLOTS, :], psum[4 + h % 2][:, 0:CH], ACT.Copy).then_inc(hi_done, 1)


def latent_attention(core, dram, X, ident, queries, BB):
    nc, psum = core.nc, core.psum
    BUFS = 3
    QG = H * S // CH
    HG = CH // S
    QT = -(-H * S // P)
    QW = QT * P
    NS = QG * KT
    KC = 3
    KW = [482, 482, 480]
    NF = QT * KC
    SB, FB, PB = 3, 2, 4
    S0, F0, A0, MISC = 0, 3, 5, 7
    F_AT = 1
    TURN_AT, OUT_AT, HI_AT = 43, 6, 20
    with ExitStack() as ctx:
        QS = [fixed(ctx, nc, f"QS{r}", [P, QW], F32R) for r in range(BUFS)]
        QB = [fixed(ctx, nc, f"QB{r}", [DC + 2, QW], F32R) for r in range(BUFS)]
        KH = [fixed(ctx, nc, f"KH{r}", [P, SKP], F32R) for r in range(BUFS)]
        KB = [fixed(ctx, nc, f"KB{r}", [DC + 2, SKP], F32R) for r in range(BUFS)]
        KV = [fixed(ctx, nc, f"KV{r}", [P, KT, 2 * DC]) for r in range(BUFS)]
        raw = fixed(ctx, nc, "raw", [P, 2, SK])
        rawk = fixed(ctx, nc, "rawk", [P, KT, DC])
        prodk = fixed(ctx, nc, "prodk", [P, 2, KT, DC])
        ropeT = fixed(ctx, nc, "ropeT", [P, 2, SK])
        ropek = fixed(ctx, nc, "ropek", [P, 2, KT, DC])
        E = fixed(ctx, nc, "E", [P, PB, CH])
        PM = fixed(ctx, nc, "PM", [P, NF])
        NM = fixed(ctx, nc, "NM", [P, QT])
        MH = fixed(ctx, nc, "MH", [QT, P], F32R)
        ML = fixed(ctx, nc, "ML", [QT, P], F32R)
        RS = fixed(ctx, nc, "RS", [P, 2, S])
        CT = fixed(ctx, nc, "CT", [P, H // 2, S])

        consts = core.sem("at_consts")
        pads = core.sem("at_pads")
        q_in = [core.sem(f"at_q{r}") for r in range(BUFS)]
        kv_in = core.sem("at_kvin")
        mulT = core.sem("at_mulT")
        rot_ready = core.sem("at_rot")
        kh_ready = core.sem("at_kh")
        k_ready = core.sem("at_k")
        s_ready = core.sem("at_s")
        exp_done = core.sem("at_exp")
        av_done = core.sem("at_av")
        f_ready = core.sem("at_f")
        red_done = core.sem("at_red")
        nm_ready = core.sem("at_nm")
        turned = core.sem("at_turned")
        mh_ready = core.sem("at_mh")
        ml_ready = core.sem("at_ml")
        m_in = core.sem("at_min")
        recip = core.sem("at_recip")
        norm_done = core.sem("at_norm")
        out_ready = core.sem("at_out")
        res_done = core.sem("at_res")

        def key_loads(sp, b):
            sp.dma_start(raw[:], dram["ctx_T"][b]).then_inc(kv_in, 16)
            sp.dma_start(rawk[:], dram["ctx_k"][b]).then_inc(kv_in, 16)

        def query_loads(sp, b, r):
            sp.dma_start(as_f32(QS[r][:, 0:H * S]), queries[b].rearrange("p h s -> p (h s)")).then_inc(q_in[r], 16)
            sp.dma_start(as_f32(QB[r][0:DC, 0:H * S]),
                         queries[b].rearrange("p h s -> p (h s)")[0:DC]).then_inc(q_in[r], 16)

        def max_rows(sp, b, r):
            sp.wait_ge(ml_ready, b + 1)
            for row, part in enumerate((MH, ML)):
                sp.dma_start(as_f32(QB[r][DC + row:DC + row + 1, :]).rearrange("o (t p) -> o t p", p=P),
                             as_f32(part[:, :])).then_inc(m_in, 16)

        def rotate_keys(pool, b, step):
            r = b_mod(b)
            pool.wait_ge(kv_in, b_val(b) * 32 + 32)
            nc.gpsimd.tensor_tensor(raw[:, 0, :], raw[:, 0, :], ropeT[:, 0, :], ALU.mult).then_inc(mulT, 1)
            nc.gpsimd.tensor_tensor(raw[:, 1, :], raw[:, 1, :], ropeT[:, 1, :], ALU.mult).then_inc(mulT, 1)
            nc.gpsimd.tensor_tensor(prodk[:, 0], rawk[:], ropek[:, 0], ALU.mult).then_inc(mulT, 1)
            for half in range(2):
                a, z = half * DC // 2, (1 - half) * DC // 2
                nc.gpsimd.tensor_tensor(prodk[:, 1, :, a:a + DC // 2], rawk[:, :, z:z + DC // 2],
                                        ropek[:, 1, :, a:a + DC // 2], ALU.mult).then_inc(mulT, 1)
            pool.wait_ge(mulT, b_val(b) * 5 + 2)
            nc.gpsimd.tensor_tensor(raw[:, 0, :], raw[:, 0, :], raw[:, 1, :], ALU.add).then_inc(rot_ready, 1)
            if step is not None:
                pool.wait_ge(av_done, b_val(step) * NS + PB)
            pool.wait_ge(mulT, b_val(b) * 5 + 5)
            nc.gpsimd.tensor_tensor(KV[r][:, :, 0:DC], prodk[:, 0], prodk[:, 1], ALU.add)
            pool.wait_ge(kh_ready, b_val(b) + 1)
            nc.gpsimd.tensor_tensor(KB[r][0:DC, 0:SK], raw[0:DC, 0, :], as_f32(KH[r][0:DC, 0:SK]),
                                    ALU.subtract).then_inc(k_ready, 1)

        def keys_high(act, b, step):
            act.wait_ge(rot_ready, b_val(b) + 1)
            if step is not None:
                act.wait_ge(av_done, b_val(step) * NS + PB)
            nc.scalar.activation(KH[b_mod(b)][:, 0:SK], raw[:, 0, :], ACT.Copy).then_inc(kh_ready, 1)

        def max_piece(pe, b, f):
            r = b_mod(b)
            t, j = divmod(f, KC)
            if f >= FB:
                pe.wait_ge(red_done, b_val(b) * NF + (f - FB + 1))
            elif b is not FIRST:
                pe.wait_ge(red_done, b_val(b) * NF)
            nc.tensor.matmul(psum[F0 + f % FB][:, 0:KW[j]], QS[r][:, t * P:(t + 1) * P],
                             KH[r][:, sum(KW[:j]):sum(KW[:j + 1])], start=True, stop=True).then_inc(f_ready, 1)

        def turn_max(pe, b):
            pe.wait_ge(nm_ready, b_val(b) + 1)
            nc.tensor.transpose(psum[MISC][0:QT, 0:P], NM[:, :], ident[:, :]).then_inc(turned, 1)

        def max_high(act, b):
            act.wait_ge(turned, b_val(b) + 1)
            if b is not FIRST:
                act.wait_ge(m_in, b_val(b) * 32)
            nc.scalar.activation(MH[:, :], psum[MISC][0:QT, 0:P], ACT.Copy).then_inc(mh_ready, 1)

        def max_low(v, b):
            v.wait_ge(mh_ready, b_val(b) + 1)
            nc.vector.tensor_tensor(ML[:, :], psum[MISC][0:QT, 0:P], as_f32(MH[:, :]), ALU.subtract).then_inc(ml_ready, 1)

        def reduce_piece(v, b, f):
            v.wait_ge(f_ready, b_val(b) * NF + (f + 1))
            if f == 0 and b is not FIRST:
                v.wait_ge(nm_ready, b_val(b))
            nc.vector.tensor_reduce(PM[:, f:f + 1], psum[F0 + f % FB][:, 0:KW[f % KC]], AX.X, ALU.max).then_inc(red_done, 1)

        def batch_max(v, b):
            v.wait_ge(red_done, b_val(b) * NF + NF)
            if b is not FIRST:
                v.wait_ge(turned, b_val(b))
            nc.vector.tensor_reduce(NM[:, :], PM[:, :].rearrange("p (t k) -> p t k", k=KC), AX.X, ALU.max,
                                    negate=True).then_inc(nm_ready, 1)

        def project(pe, b):
            pe.wait_ge(norm_done, b_val(b) * H + (H + 2 * HG))
            for j in range(H // 2):
                last = nc.tensor.matmul(psum[MISC][0:S, 0:D], CT[:, j, :], BB[:, j, :], start=j == 0, stop=j == H // 2 - 1)
            last.then_inc(out_ready, 1)

        def add_output(v, b):
            v.wait_ge(out_ready, b_val(b) + 1)
            x = X[:, b_val(b), :]
            nc.vector.tensor_tensor(x, psum[MISC][0:S, 0:D], x, ALU.add).then_inc(res_done, 1)

        def normalise(v, b, h):
            g, j = divmod(h, HG)
            acc = psum[A0 + g % 2]
            v.wait_ge(av_done, b_val(b) * NS + (PB + KT * (g + 1)))
            if h == 0 and b is not FIRST:
                v.wait_ge(out_ready, b_val(b))
            if b is not FIRST or h >= 2:
                v.wait_ge(norm_done, b_val(b) * H + (2 * HG + h - 1))
            nc.vector.reciprocal(RS[DC:P, h % 2, :], acc[DC:P, j * S:(j + 1) * S]).then_inc(recip, 1)
            v.wait_ge(recip, b_val(b) * H + (h + 1))
            rows = slice((h % 2) * DC, (h % 2 + 1) * DC)
            nc.vector.tensor_tensor(CT[rows, h // 2, :], acc[0:DC, j * S:(j + 1) * S], RS[DC:P, h % 2, :],
                                    ALU.mult).then_inc(norm_done, 1)

        class Batch:
            def __init__(self, turn, r):
                self.turn, self.r = turn + r // BUFS, r % BUFS

            def __add__(self, n):
                return Batch(self.turn, self.r + n)

        def b_val(b):
            return b.turn * BUFS + b.r

        def b_mod(b):
            return b.r

        FIRST = Batch(0, 0)

        def steps(eng, body):
            body(FIRST, True, True)
            with eng.Fori(0, (B - 1 - BUFS) // BUFS) as i:
                for u in range(BUFS):
                    body(Batch(i, 1 + u), True, True)
            body(Batch(0, B - 3), True, True)
            body(Batch(0, B - 2), True, False)
            body(Batch(0, B - 1), False, False)

        with nc.Block() as block:

            @block.sync
            def _(sp):
                sp.dma_start(ropeT[:], dram["rope_T"]).then_inc(consts, 16)
                sp.dma_start(ropek[:], dram["rope_k"]).then_inc(consts, 16)
                for r in range(BUFS):
                    sp.dma_start(KV[r][:, :, DC:], dram["key_ones"]).then_inc(consts, 16)
                key_loads(sp, 0)
                query_loads(sp, 0, 0)
                query_loads(sp, 1, 1)
                sp.wait_ge(k_ready, 1)
                key_loads(sp, 1)
                max_rows(sp, 0, 0)
                sp.wait_ge(k_ready, 2)
                key_loads(sp, 2)

                def step(b, has_next, has_keys):
                    if has_keys:
                        sp.wait_ge(av_done, b_val(b) * NS + PB)
                        query_loads(sp, b_val(b + 2), b_mod(b + 2))
                        sp.wait_ge(k_ready, b_val(b) + 3)
                        if not (isinstance(b.turn, int) and b_val(b) == B - BUFS):
                            key_loads(sp, b_val(b + 3))
                    if has_next:
                        max_rows(sp, b_val(b + 1), b_mod(b + 1))

                steps(sp, step)

            @block.gpsimd
            def _(pool):
                pool.wait_ge(consts, 16 * (2 + BUFS))
                rotate_keys(pool, FIRST, None)
                rotate_keys(pool, FIRST + 1, None)

                def step(b, has_next, has_keys):
                    if has_keys:
                        rotate_keys(pool, b + 2, b)

                steps(pool, step)

            @block.scalar
            def _(act):
                act.sem_inc(exp_done, SB)
                keys_high(act, FIRST, None)
                max_high(act, FIRST)
                keys_high(act, FIRST + 1, None)

                def step(b, has_next, has_keys):
                    for n in range(NS):
                        act.wait_ge(s_ready, b_val(b) * NS + (n + 1))
                        act.wait_ge(av_done, b_val(b) * NS + (n + 1))
                        nc.scalar.activation(E[:, n % PB, :], psum[S0 + n % SB][:, 0:CH], ACT.Exp).then_inc(exp_done, 1)
                        if n == HI_AT and has_keys:
                            keys_high(act, b + 2, b)
                        if n == TURN_AT and has_next:
                            max_high(act, b + 1)

                steps(act, step)

            @block.tensor
            def _(pe):
                pe.sem_inc(av_done, PB)
                pe.wait_ge(pads, BUFS)
                pe.wait_ge(consts, 16 * (2 + BUFS))
                pe.wait_ge(q_in[0], 32)
                pe.wait_ge(k_ready, 1)
                for f in range(NF):
                    max_piece(pe, FIRST, f)
                turn_max(pe, FIRST)

                def values(b, n):
                    g, t = divmod(n, KT)
                    pe.wait_ge(exp_done, b_val(b) * NS + (SB + n + 1))
                    if t == 0:
                        pe.wait_ge(norm_done, b_val(b) * H + HG * (g + 1))
                    nc.tensor.matmul(psum[A0 + g % 2][:, 0:CH], KV[b_mod(b)][:, t, :], E[:, n % PB, :],
                                     start=t == 0, stop=t == KT - 1).then_inc(av_done, 1)

                def step(b, has_next, has_keys):
                    r = b_mod(b)
                    pe.wait_ge(m_in, b_val(b) * 32 + 32)
                    for n in range(NS):
                        g, t = divmod(n, KT)
                        pe.wait_ge(exp_done, b_val(b) * NS + (n + 1))
                        out = psum[S0 + n % SB][:, 0:CH]
                        keys, cols = slice(t * P, (t + 1) * P), slice(g * CH, (g + 1) * CH)
                        nc.tensor.matmul(out, KH[r][:, keys], QS[r][:, cols], start=True, stop=False)
                        nc.tensor.matmul(out, KB[r][:, keys], QB[r][:, cols], start=False, stop=True).then_inc(s_ready, 1)
                        if has_next and n == F_AT:
                            pe.wait_ge(k_ready, b_val(b) + 2)
                            pe.wait_ge(q_in[b_mod(b + 1)], (b + 1).turn * 32 + 32)
                        if has_next and 0 <= n - F_AT < NF:
                            max_piece(pe, b + 1, n - F_AT)
                        if n >= 2:
                            values(b, n - 2)
                        if n == OUT_AT and b is not FIRST:
                            project(pe, Batch(b.turn, b.r - 1) if b.r else Batch(b.turn - 1, BUFS - 1))
                        if n == TURN_AT and has_next:
                            if b is not FIRST:
                                pe.wait_ge(res_done, b_val(b))
                            turn_max(pe, b + 1)
                    values(b, NS - 2)
                    values(b, NS - 1)

                steps(pe, step)
                project(pe, Batch(0, B - 1))

            @block.vector
            def _(v):
                v.sem_inc(norm_done, 2 * HG)
                for r in range(BUFS):
                    v.memset(as_f32(QS[r][:, H * S:]), 0.0)
                    v.memset(as_f32(KH[r][:, SK:]), 0.0)
                    v.memset(as_f32(KB[r][:, SK:]), 0.0)
                    v.memset(as_f32(KB[r][DC:DC + 2, 0:SK]), 1.0).then_inc(pads, 1)
                for f in range(NF):
                    reduce_piece(v, FIRST, f)
                batch_max(v, FIRST)
                max_low(v, FIRST)

                def step(b, has_next, has_keys):
                    todo = {}
                    for h in range(H - HG):
                        todo[KT * (h // HG + 1) + 3 + 2 * (h % HG)] = h
                    for n in range(NS):
                        if has_next and 0 <= n - F_AT < NF:
                            reduce_piece(v, b + 1, n - F_AT)
                        if n - F_AT == NF and has_next:
                            batch_max(v, b + 1)
                        if n == OUT_AT + 2 and b is not FIRST:
                            add_output(v, Batch(b.turn, b.r - 1) if b.r else Batch(b.turn - 1, BUFS - 1))
                        if n in todo:
                            normalise(v, b, todo[n])
                        if n == TURN_AT + 1 and has_next:
                            max_low(v, b + 1)
                    for h in range(H - HG, H):
                        normalise(v, b, h)

                steps(v, step)
                add_output(v, Batch(0, B - 1))


class RouterInputs:
    NAMES = ("router", "iota", "steps", "below", "order", "tri")

    def __init__(self, core, ctx, dram, tag, E, tiles):
        nc = core.nc
        self.dram, self.tag = dram, tag
        full = -(-B * S // TOK)
        self.router = fixed(ctx, nc, tag + "wr", [P, KD, E])
        self.iota = fixed(ctx, nc, tag + "iota", [S, E])
        self.steps = fixed(ctx, nc, tag + "steps", [S, full])
        self.below = fixed(ctx, nc, tag + "below", [S, E, E])
        self.order = fixed(ctx, nc, tag + "order", [S, tiles])
        self.tri = fixed(ctx, nc, tag + "tri", [S, S])
        self.tiles_of = (self.router, self.iota, self.steps, self.below, self.order, self.tri)
        self.loaded = core.sem(tag + "loaded")

    def load(self, sp):
        for t, name in zip(self.tiles_of, self.NAMES):
            sp.dma_start(t[:], self.dram[self.tag + name]).then_inc(self.loaded, 16)


class Chain:

    def __init__(self, eng, sem):
        self.eng, self.sem, self.done = eng, sem, 0

    def __call__(self, ins):
        self.done += 1
        ins.then_inc(self.sem, 1)
        self.eng.wait_ge(self.sem, self.done)


def route(core, inputs, tag, ident, XH, XL, E, slots, w, tile_expert, tiles, first_tile, grouped):
    nc, psum = core.nc, core.psum
    G = 4
    FULL = -(-B * S // TOK)
    with ExitStack() as ctx:
        iota, steps, below, order, tri = inputs.iota, inputs.steps, inputs.below, inputs.order, inputs.tri
        WH = fixed(ctx, nc, tag + "wrh", [P, KD, P], F32R)
        WL = fixed(ctx, nc, tag + "wrl", [P, KD, P], F32R)
        flat = fixed(ctx, nc, tag + "flat", [E, B * S])
        trib = fixed(ctx, nc, tag + "trib", [S, S], BF16)
        onesb = fixed(ctx, nc, tag + "onesb", [S, S], BF16)
        sc = fixed(ctx, nc, tag + "sc", [S, B, E])
        top = fixed(ctx, nc, tag + "top", [S, B, 8])
        idx = fixed(ctx, nc, tag + "idx", [S, B, 8], U32)
        idf = fixed(ctx, nc, tag + "idf", [S, B, 8])
        one = fixed(ctx, nc, tag + "one", [S, B, E])
        two = fixed(ctx, nc, tag + "two", [S, B, E])
        both = fixed(ctx, nc, tag + "both", [S, B + 1, E], BF16)
        place = fixed(ctx, nc, tag + "place", [S, B, E])
        over = fixed(ctx, nc, tag + "over", [S, E, FULL])
        used = fixed(ctx, nc, tag + "used", [S, E])
        before = fixed(ctx, nc, tag + "before", [S, E, E])
        start = fixed(ctx, nc, tag + "start", [S, E])
        past = fixed(ctx, nc, tag + "past", [S, tiles, E])
        tef = fixed(ctx, nc, tag + "tef", [S, tiles])
        slf = fixed(ctx, nc, tag + "slf", [S, 2, B])
        gs = fixed(ctx, nc, tag + "gs", [S, B, G])
        gt = fixed(ctx, nc, tag + "gt", [S, B, G])
        rank = fixed(ctx, nc, tag + "rank", [S, B, G])
        parts = core.sem(tag + "parts")
        flat_ready = core.sem(tag + "flat")
        flat_in = core.sem(tag + "flat_in")
        scores = core.sem(tag + "scores")
        chosen = core.sem(tag + "chosen")
        ranked = core.sem(tag + "ranked")
        chain = core.sem(tag + "chain")
        asked = core.sem(tag + "asked")
        given = core.sem(tag + "given")
        with nc.Block() as block:

            @block.tensor
            def _(pe):
                pe.wait_ge(parts, 1)
                for c in range(NC):
                    cols = slice(c * CH, (c + 1) * CH)
                    todo = [(w[:, k, :], x[:, k, cols]) for k in range(KD) for x in (XH, XL) for w in (WH, WL)]
                    for n, (lhs, rhs) in enumerate(todo):
                        last = nc.tensor.matmul(psum[2 + c][:, 0:CH], lhs, rhs, start=n == 0, stop=n == len(todo) - 1)
                    last.then_inc(flat_ready, 1)
                for b in range(B):
                    if b % CB == 0:
                        pe.wait_ge(flat_in, b // CB + 1)
                    last = nc.tensor.transpose(psum[0][0:S, b * E:(b + 1) * E], flat[:, b * S:(b + 1) * S], ident[0:E, 0:E])
                last.then_inc(scores, 1)
                pe.wait_ge(chosen, 1)
                nc.tensor.matmul(psum[1][0:S, 0:(B + 1) * E], trib[:], both[:].rearrange("p b e -> p (b e)"),
                                 start=True, stop=False)
                for b in range(B):
                    later = B - b
                    last = nc.tensor.matmul(psum[1][0:S, (b + 1) * E:(B + 1) * E], onesb[:],
                                            both[:, b:b + 1, :].to_broadcast([S, later, E]), start=False, stop=b == B - 1)
                last.then_inc(ranked, 1)

            @block.scalar
            def _(act):
                for c in range(NC):
                    act.wait_ge(flat_ready, c + 1)
                    nc.scalar.activation(flat[:, c * CH:(c + 1) * CH], psum[2 + c][0:E, 0:CH], ACT.Copy).then_inc(flat_in, 1)
                if grouped:
                    act.wait_ge(scores, 1)
                    nc.scalar.activation(sc[:].rearrange("p b e -> p (b e)"), psum[0][0:S, 0:B * E],
                                         ACT.Sigmoid).then_inc(given, 1)
                else:
                    act.wait_ge(asked, 1)
                    nc.scalar.activation(w[:, 1, :], w[:, 0, :], ACT.Exp).then_inc(given, 1)

            @block.vector
            def _(v):
                vec = nc.vector
                do = Chain(v, chain)
                vec.memset(as_f32(WH[:]), 0.0)
                do(vec.memset(as_f32(WL[:]), 0.0))
                v.wait_ge(inputs.loaded, 16 * len(inputs.NAMES))
                do(vec.tensor_copy(WH[:, :, 0:E], inputs.router[:]))
                vec.tensor_tensor(WL[:, :, 0:E], inputs.router[:], as_f32(WH[:, :, 0:E]), ALU.subtract).then_inc(parts, 1)
                vec.tensor_copy(trib[:], tri[:])
                vec.memset(onesb[:], 1.0)
                do(vec.memset(both[:, B:, :], 0.0))
                if grouped:
                    v.wait_ge(given, 1)
                    g = sc[:].rearrange("p b (g i) -> p b g i", g=G)
                    pairs = [(i, j) for i in range(G) for j in range(i + 1, G)]
                    for n, (i, j) in enumerate(pairs):
                        do(vec.tensor_tensor((gt if n else gs)[:], g[:, :, :, i], g[:, :, :, j], ALU.add))
                        if n:
                            do(vec.tensor_tensor(gs[:], gs[:], gt[:], ALU.max))
                    do(vec.memset(rank[:], 0.0))
                    for i in range(G):
                        for j in range(G):
                            if i != j:
                                do(vec.tensor_tensor(gt[:, :, i], gs[:, :, j], gs[:, :, i], ALU.is_ge if j < i else ALU.is_gt))
                                do(vec.tensor_tensor(rank[:, :, i], rank[:, :, i], gt[:, :, i], ALU.add))
                    do(vec.tensor_scalar(rank[:], rank[:], 2.0, None, ALU.is_lt))
                    for i in range(G):
                        do(vec.tensor_tensor(g[:, :, :, i], g[:, :, :, i], rank[:], ALU.mult))
                else:
                    v.wait_ge(scores, 1)
                    do(vec.tensor_copy(sc[:].rearrange("p b e -> p (b e)"), psum[0][0:S, 0:B * E]))
                for b in range(B):
                    vec.max(top[:, b, :], sc[:, b, :]).then_inc(chain, 1)
                do.done += B
                v.wait_ge(chain, do.done)
                for b in range(B):
                    vec.max_index(idx[:, b, :], top[:, b, :], sc[:, b, :]).then_inc(chain, 1)
                do.done += B
                v.wait_ge(chain, do.done)
                do(vec.tensor_copy(idf[:], idx[:]))
                for n, hot in enumerate((one, two)):
                    do(vec.tensor_tensor(hot[:], iota[:].rearrange("p (o e) -> p o e", o=1).to_broadcast([S, B, E]),
                                         idf[:, :, n:n + 1].to_broadcast([S, B, E]), ALU.is_equal))
                vec.tensor_tensor(both[:, 0:B, :], one[:], two[:], ALU.add).then_inc(chosen, 1)
                if grouped:
                    do(vec.tensor_tensor(w[:, 0, :], top[:, :, 0], top[:, :, 1], ALU.add))
                    do(vec.tensor_scalar(w[:, 0, :], w[:, 0, :], 1e-20, None, ALU.add))
                    do(vec.reciprocal(w[:, 1, :], w[:, 0, :]))
                    do(vec.tensor_tensor(w[:, 2, :], top[:, :, 0], w[:, 1, :], ALU.mult))
                    do(vec.tensor_tensor(w[:, 3, :], top[:, :, 1], w[:, 1, :], ALU.mult))
                else:
                    vec.tensor_tensor(w[:, 0, :], top[:, :, 1], top[:, :, 0], ALU.subtract).then_inc(asked, 1)
                    v.wait_ge(given, 1)
                    do(vec.tensor_scalar(w[:, 0, :], w[:, 1, :], 1.0, None, ALU.add))
                    do(vec.reciprocal(w[:, 2, :], w[:, 0, :]))
                    do(vec.tensor_tensor(w[:, 3, :], w[:, 1, :], w[:, 2, :], ALU.mult))
                v.wait_ge(ranked, 1)
                count = psum[1][0:S, B * E:(B + 1) * E].rearrange("p (e o) -> p e o", o=1)
                do(vec.tensor_tensor(over[:], count.to_broadcast([S, E, FULL]),
                                     steps[:].rearrange("p (o j) -> p o j", o=1).to_broadcast([S, E, FULL]), ALU.is_gt))
                do(vec.tensor_reduce(used[:], over[:], AX.X, ALU.add))
                do(vec.tensor_tensor(before[:], used[:].rearrange("p (o e) -> p o e", o=1).to_broadcast([S, E, E]),
                                     below[:], ALU.mult))
                do(vec.tensor_reduce(start[:], before[:], AX.X, ALU.add))
                if first_tile:
                    do(vec.tensor_scalar(start[:], start[:], float(first_tile), None, ALU.add))
                do(vec.scalar_tensor_tensor(place[:], start[:].rearrange("p (o e) -> p o e", o=1).to_broadcast([S, B, E]),
                                            float(TOK), psum[1][0:S, 0:B * E].rearrange("p (b e) -> p b e", b=B),
                                            ALU.mult, ALU.add))
                for n, hot in enumerate((one, two)):
                    do(vec.tensor_tensor(hot[:], hot[:], place[:], ALU.mult))
                    do(vec.tensor_reduce(slf[:, n, :], hot[:], AX.X, ALU.add))
                do(vec.tensor_copy(slots[:], slf[:]))
                do(vec.tensor_tensor(used[:], used[:], start[:], ALU.add))
                do(vec.tensor_tensor(past[:], used[:].rearrange("p (o e) -> p o e", o=1).to_broadcast([S, tiles, E]),
                                     order[:].rearrange("p (t o) -> p t o", o=1).to_broadcast([S, tiles, E]), ALU.is_le))
                do(vec.tensor_reduce(tef[:], past[:], AX.X, ALU.add))
                do(vec.tensor_scalar(tef[:], tef[:], float(E - 1), None, ALU.min))
                if first_tile:
                    do(vec.memset(tef[:, 0:first_tile], float(E)))
                do(vec.tensor_copy(tile_expert[:], tef[:]))


def experts(core, dram, tag, X, XN, ident, slots, w, tile_expert, rows_in, rows_out, E, NU, TR, NT, tiles, first_tile, BUFS):
    nc, psum = core.nc, core.psum
    I = TR * NT
    HT = TOK // P
    LAG = 2
    HB = 3
    XB, YB = HB, HB + 1
    RING = 4
    LOOPS, REST = divmod(tiles - max(first_tile, 1), BUFS)
    assert REST >= 1 and max(first_tile - 1, 0) % BUFS == 0 and BUFS * NT % HB == 0 and YB + BUFS <= 8
    with ExitStack() as ctx:
        stage_u = [fixed(ctx, nc, f"{tag}stage_u{u}", [P, KD, NU, I]) for u in range(BUFS)]
        stage_d = [fixed(ctx, nc, f"{tag}stage_d{u}", [TR, NT, D]) for u in range(BUFS)]
        UH = [fixed(ctx, nc, f"{tag}UH{u}", [P, KD, NU, I], F32R) for u in range(BUFS)]
        UL = [fixed(ctx, nc, f"{tag}UL{u}", [P, KD, NU, I], F32R) for u in range(BUFS)]
        DH = [fixed(ctx, nc, f"{tag}DH{u}", [TR, NT, D], F32R) for u in range(BUFS)]
        DL = [fixed(ctx, nc, f"{tag}DL{u}", [TR, NT, D], F32R) for u in range(BUFS)]
        xg = [fixed(ctx, nc, f"{tag}xg{u}", [P, HT, D]) for u in range(BUFS)]
        xh = [fixed(ctx, nc, f"{tag}xh{u}", [P, KD, TOK], F32R) for u in range(BUFS)]
        xl = [fixed(ctx, nc, f"{tag}xl{u}", [P, KD, TOK], F32R) for u in range(BUFS)]
        ys = [fixed(ctx, nc, f"{tag}ys{u}", [P, HT, D]) for u in range(BUFS)]
        G = fixed(ctx, nc, tag + "G", [TR, HB, TOK])
        HF = fixed(ctx, nc, tag + "HF", [TR, HB, TOK])
        HH = [fixed(ctx, nc, f"{tag}HH{u}", [TR, NT, TOK], F32R) for u in range(BUFS)]
        HL = [fixed(ctx, nc, f"{tag}HL{u}", [TR, NT, TOK], F32R) for u in range(BUFS)]
        back = fixed(ctx, nc, tag + "back", [S, RING, 2, D])
        shared = fixed(ctx, nc, tag + "shared", [S, B, D]) if first_tile else None
        plain = core.sem(tag + "plain")
        scattered = core.sem(tag + "scattered")
        w_in = [core.sem(f"{tag}w_in{u}") for u in range(BUFS)]
        x_in = [core.sem(f"{tag}x_in{u}") for u in range(BUFS)]
        w_hi = core.sem(tag + "w_hi")
        ul_ready = core.sem(tag + "ul")
        dl_ready = core.sem(tag + "dl")
        turned = core.sem(tag + "turned")
        xh_ready = core.sem(tag + "xh")
        xl_ready = core.sem(tag + "xl")
        up_ready = core.sem(tag + "up")
        g_ready = core.sem(tag + "g")
        h_ready = core.sem(tag + "h")
        hh_ready = core.sem(tag + "hh")
        hl_ready = core.sem(tag + "hl")
        down_done = core.sem(tag + "down")
        y_done = core.sem(tag + "y")
        stored = [core.sem(f"{tag}stored{u}") for u in range(BUFS)]
        back_in = [core.sem(f"{tag}back{i}") for i in range(RING)]
        shared_in = core.sem(tag + "shared_in")
        first_in = core.sem(tag + "first_in")
        added = core.sem(tag + "added")

        def steps(eng, body):
            body(0, 0, 0)
            if first_tile:
                with eng.Fori(0, (first_tile - 1) // BUFS) as i:
                    for u in range(BUFS):
                        body(i * BUFS + (1 + u), (1 + u) % BUFS, i + (1 + u) // BUFS)
            base = max(first_tile, 1)
            with eng.Fori(0, LOOPS) as i:
                for u in range(BUFS):
                    k = base + u
                    body(i * BUFS + k, k % BUFS, i + k // BUFS)
            for k in range(base + LOOPS * BUFS, tiles):
                body(k, k % BUFS, k // BUFS)

        def is_last(k):
            return isinstance(k, int) and k == tiles - 1

        def next_of(u, m):
            return (u + 1) % BUFS, m + (u + 1) // BUFS

        with nc.Block() as block:

            @block.sync
            def _(sp):
                BEHIND = BUFS + 1
                HEAD = first_tile or BEHIND

                def load(k, u):
                    load_weights(k, u)
                    load_rows(k, u)

                def load_weights(k, u):
                    last_expert = E if first_tile else E - 1
                    e = bass.ds(sp.value_load(tile_expert[0:1, bass.ds(k, 1)], min_val=0, max_val=last_expert), 1)
                    sp.wait_ge(ul_ready, k + 1)
                    sp.wait_ge(dl_ready, k + 1)
                    sp.dma_start(stage_u[u][:].rearrange("p k n i -> p (k n i)"),
                                 dram[tag + "up"][e].rearrange("o p k n i -> p (o k n i)")).then_inc(w_in[u], 16)
                    sp.dma_start(stage_d[u][:].rearrange("p t d -> p (t d)"),
                                 dram[tag + "down"][e].rearrange("o p t d -> p (o t d)")).then_inc(w_in[u], 16)

                def load_rows(k, u):
                    sp.wait_ge(turned, k + 1)
                    sp.dma_start(xg[u][:], rows_in[bass.ts(k, TOK)].rearrange("(j p) d -> p j d", p=P)).then_inc(x_in[u], 16)

                def store(k, u):
                    sp.wait_ge(y_done, k + (BUFS + 1))
                    sp.dma_start(rows_out[bass.ts(k, TOK)].rearrange("(j p) d -> p j d", p=P), ys[u][:]).then_inc(stored[u], 16)

                for s in stored:
                    sp.sem_inc(s, 16)
                for k in range(BUFS):
                    load_weights(k, k)
                if first_tile:
                    sp.dma_start(rows_in[0:B * S].rearrange("(b s) d -> s b d", b=B), XN[:]).then_inc(plain, 16)
                    sp.wait_ge(plain, 16)
                for k in range(HEAD):
                    if k == first_tile:
                        sp.wait_ge(scattered, 16 * 2 * B)
                    if k < BUFS:
                        load_rows(k, k)
                    else:
                        load(k, k % BUFS)
                    if k >= BEHIND:
                        store(k - BEHIND, (k - BEHIND) % BUFS)
                if HEAD == first_tile:
                    sp.wait_ge(scattered, 16 * 2 * B)
                rounds = (tiles - HEAD) // BUFS
                with sp.Fori(0, rounds) as i:
                    for k in range(HEAD, HEAD + BUFS):
                        load(i * BUFS + k, k % BUFS)
                        store(i * BUFS + (k - BEHIND), (k - BEHIND) % BUFS)
                for k in range(HEAD + rounds * BUFS, tiles + BEHIND):
                    if k < tiles:
                        load(k, k % BUFS)
                    store(k - BEHIND, (k - BEHIND) % BUFS)
                for u, s in enumerate(stored):
                    sp.wait_ge(s, 16 * (1 + len(range(u, tiles, BUFS))))
                if first_tile:
                    sp.dma_start(shared[:], rows_out[0:B * S].rearrange("(b s) d -> s b d", b=B)).then_inc(shared_in, 16)
                    sp.wait_ge(shared_in, 16)

            @block.gpsimd
            def _(pool):
                for n in range(2):
                    for b in range(B):
                        pool.indirect_dma_start(rows_in[:, :], bass.IndirectOffsetOnAxis(slots[:, n, b:b + 1], 0),
                                                XN[:, b, :], None).then_inc(scattered, 16)
                pool.sem_inc(dl_ready, BUFS)

                def split(k, u, m):
                    pool.wait_ge(w_hi, k * (KD + 1) + (KD + 1))
                    nc.gpsimd.tensor_tensor(DL[u][:], stage_d[u][:], as_f32(DH[u][:]), ALU.subtract).then_inc(dl_ready, 1)
                steps(pool, split)
                for u, s in enumerate(stored):
                    pool.wait_ge(s, 16 * (1 + len(range(u, tiles, BUFS))))
                for b in range(B):
                    if b >= RING:
                        pool.wait_ge(added, b - RING + 1)
                    for n in range(2):
                        pool.indirect_dma_start(back[:, b % RING, n, :], None, rows_out[0:tiles * TOK, :],
                                                bass.IndirectOffsetOnAxis(slots[:, n, b:b + 1], 0)).then_inc(back_in[b % RING], 16)

            @block.tensor
            def _(pe):
                pe.sem_inc(down_done, BUFS * NT)
                pe.sem_inc(turned, BUFS)

                def turn(k, u, m):
                    pe.wait_ge(x_in[u], m * 16 + 16)
                    if not isinstance(k, int) or k >= 1:
                        pe.wait_ge(xl_ready, k)
                    for q in range(KD):
                        for j in range(HT):
                            last = nc.tensor.transpose(psum[XB][:, (q * HT + j) * P:(q * HT + j + 1) * P],
                                                       xg[u][:, j, q * P:(q + 1) * P], ident[:, :])
                    last.then_inc(turned, 1)

                def up(k, u, t):
                    if t == 0:
                        pe.wait_ge(xl_ready, k + 1)
                        pe.wait_ge(ul_ready, k + (BUFS + 1))
                    pe.wait_ge(h_ready, k * NT + (t + 1))
                    cols = slice(t * TR, (t + 1) * TR)
                    for n in range(NU):
                        last = split_products(nc, psum[(u * NT + t) % HB][0:TR, n * TOK:(n + 1) * TOK],
                                              [(UH[u][:, q, n, cols], UL[u][:, q, n, cols], xh[u][:, q, :], xl[u][:, q, :])
                                               for q in range(KD)])
                    last.then_inc(up_ready, 1)

                def down(k, u, t):
                    pe.wait_ge(hl_ready, k * NT + (HB + t + 1))
                    if t == 0:
                        pe.wait_ge(dl_ready, k + (BUFS + 1))
                        pe.wait_ge(y_done, k + 1)
                    for j in range(HT):
                        rows = slice(j * P, (j + 1) * P)
                        last = split_products(nc, psum[YB + u][:, j * D:(j + 1) * D],
                                              [(HH[u][:, t, rows], HL[u][:, t, rows], DH[u][:, t, :], DL[u][:, t, :])],
                                              first=t == 0 and j == 0, last=t == NT - 1 and j == HT - 1)
                    last.then_inc(down_done, 1)

                def step(k, u, m):
                    if NT == LAG and not is_last(k):
                        turn(k + 1, *next_of(u, m))
                    for t in range(NT):
                        up(k, u, t)
                        if t >= LAG:
                            down(k, u, t - LAG)
                        elif not isinstance(k, int) or k >= 1:
                            down(k - 1, (u - 1) % BUFS, NT - LAG + t)
                        if t == 1 and NT > LAG and not is_last(k):
                            turn(k + 1, *next_of(u, m))

                turn(0, 0, 0)
                steps(pe, step)
                for t in range(NT - LAG, NT):
                    down(tiles - 1, (tiles - 1) % BUFS, t)

            @block.scalar
            def _(act):
                if NU == 1:
                    act.sem_inc(h_ready, HB)

                def rows_high(k, u):
                    act.wait_ge(turned, k + (BUFS + 1))
                    if not isinstance(k, int) or k >= 2:
                        act.wait_ge(up_ready, (k - 1) * NT)
                    nc.scalar.activation(xh[u][:], psum[XB][:, 0:KD * TOK].rearrange("p (k t) -> p k t", k=KD),
                                         ACT.Copy).then_inc(xh_ready, 1)

                def weights_high(k, u, m, part):
                    if part == 0:
                        act.wait_ge(w_in[u], m * 32 + 32)
                        if not isinstance(k, int) or k >= 2:
                            act.wait_ge(up_ready, (k - 1) * NT)
                    if part == KD:
                        act.wait_ge(down_done, k * NT + NT)
                    if part < KD:
                        nc.scalar.activation(UH[u][:, part], stage_u[u][:, part], ACT.Copy).then_inc(w_hi, 1)
                    else:
                        nc.scalar.activation(DH[u][:], stage_d[u][:], ACT.Copy).then_inc(w_hi, 1)

                def step(k, u, m):
                    def gate(t):
                        act.wait_ge(up_ready, k * NT + (t + 1))
                        src, b = psum[(u * NT + t) % HB][0:TR, 0:TOK], (u * NT + t) % HB
                        if NU == 2:
                            act.wait_ge(h_ready, k * NT + (t + 1))
                            nc.scalar.activation(G[:, b, :], src, ACT.Silu).then_inc(g_ready, 1)
                        else:
                            act.wait_ge(hl_ready, k * NT + (t + 1))
                            nc.scalar.activation(HF[:, b, :], src, ACT.Silu).then_inc(h_ready, 1)

                    def high(t):
                        act.wait_ge(h_ready, k * NT + (HB + t + 1))
                        act.wait_ge(down_done, k * NT + (t + 1))
                        nc.scalar.activation(HH[u][:, t, :], HF[:, (u * NT + t) % HB, :], ACT.Copy).then_inc(hh_ready, 1)

                    if NT == LAG and not is_last(k):
                        rows_high(k + 1, next_of(u, m)[0])
                    for t in range(NT + 1):
                        if t < NT:
                            gate(t)
                        if t >= 1:
                            high(t - 1)
                        if not is_last(k):
                            un, mn = next_of(u, m)
                            for part in range(KD + 1):
                                if ACT_AT[part] == t:
                                    weights_high(k + 1, un, mn, part)
                            if t == 2 and NT > LAG:
                                rows_high(k + 1, un)

                ACT_AT = (0, 1, 3) if NT > 2 else (0, 0, 0)
                for part in range(KD + 1):
                    weights_high(0, 0, 0, part)
                rows_high(0, 0)
                steps(act, step)

            @block.vector
            def _(v):
                if NU == 2:
                    v.sem_inc(h_ready, HB)
                v.sem_inc(hl_ready, HB)
                v.sem_inc(ul_ready, BUFS)
                v.sem_inc(y_done, BUFS)

                def rows_low(k, u):
                    v.wait_ge(xh_ready, k + 1)
                    nc.vector.tensor_tensor(xl[u][:], psum[XB][:, 0:KD * TOK].rearrange("p (k t) -> p k t", k=KD),
                                            as_f32(xh[u][:]), ALU.subtract).then_inc(xl_ready, 1)

                def weights_low(k, u, part):
                    v.wait_ge(w_hi, k * (KD + 1) + (part + 1))
                    ins = nc.vector.tensor_tensor(UL[u][:, part], stage_u[u][:, part], as_f32(UH[u][:, part]), ALU.subtract)
                    if part == KD - 1:
                        ins.then_inc(ul_ready, 1)

                def sums_out(k, u, m):
                    v.wait_ge(down_done, k * NT + (BUFS * NT + NT))
                    v.wait_ge(stored[u], m * 16 + 16)
                    nc.vector.tensor_copy(ys[u][:].rearrange("p j d -> p (j d)"), psum[YB + u][:, 0:HT * D]).then_inc(y_done, 1)

                def step(k, u, m):
                    def hidden(t):
                        b = (u * NT + t) % HB
                        v.wait_ge(g_ready, k * NT + (t + 1))
                        v.wait_ge(hl_ready, k * NT + (t + 1))
                        nc.vector.tensor_tensor(HF[:, b, :], psum[b][0:TR, TOK:2 * TOK], G[:, b, :], ALU.mult).then_inc(h_ready, 1)

                    def low(t):
                        v.wait_ge(hh_ready, k * NT + (t + 1))
                        nc.vector.tensor_tensor(HL[u][:, t, :], HF[:, (u * NT + t) % HB, :], as_f32(HH[u][:, t, :]),
                                                ALU.subtract).then_inc(hl_ready, 1)

                    if NT == LAG and not is_last(k):
                        rows_low(k + 1, next_of(u, m)[0])
                        for part in range(KD):
                            weights_low(k + 1, next_of(u, m)[0], part)
                    for t in range(NT + 1):
                        if t < NT and NU == 2:
                            hidden(t)
                        if t >= 1:
                            low(t - 1)
                        if NT > LAG and not is_last(k):
                            un, mn = next_of(u, m)
                            for part in range(KD):
                                if DVE_AT[part] == t:
                                    weights_low(k + 1, un, part)
                            if t == 3:
                                rows_low(k + 1, un)
                        if t == min(3, NT) and (not isinstance(k, int) or k >= 1):
                            sums_out(k - 1, (u - 1) % BUFS, m if u else m - 1)

                DVE_AT = (1, 2)
                for part in range(KD):
                    weights_low(0, 0, part)
                rows_low(0, 0)
                steps(v, step)
                k = tiles - 1
                sums_out(k, k % BUFS, k // BUFS)
                if first_tile:
                    v.wait_ge(shared_in, 16)
                    nc.vector.tensor_tensor(X[:], X[:], shared[:], ALU.add).then_inc(first_in, 1)
                    v.wait_ge(first_in, 1)
                for b in range(B):
                    v.wait_ge(back_in[b % RING], 32 * (b // RING + 1))
                    for n in range(2):
                        ins = nc.vector.scalar_tensor_tensor(X[:, b, :], back[:, b % RING, n, :], w[:, 2 + n, b:b + 1],
                                                             X[:, b, :], ALU.mult, ALU.add)
                        ins.then_inc(added if n else first_in, 1)
                        if not n:
                            v.wait_ge(first_in, b + 1 + (1 if first_tile else 0))


def moe(core, dram, tag, X, ident, rows_in, rows_out, E, NU, TR, NT, tiles, first_tile, BUFS, grouped):
    nc = core.nc
    with ExitStack() as ctx:
        XN = fixed(ctx, nc, tag + "XN", [S, B, D])
        slots = fixed(ctx, nc, tag + "slots", [S, 2, B], U32)
        w = fixed(ctx, nc, tag + "w", [S, 4, B])
        tile_expert = fixed(ctx, nc, tag + "tile_expert", [S, tiles], U32)
        with ExitStack() as stage:
            XH = fixed(stage, nc, tag + "XH", [P, KD, B * S], F32R)
            XL = fixed(stage, nc, tag + "XL", [P, KD, B * S], F32R)
            inputs = RouterInputs(core, stage, dram, tag, E, tiles)
            layernorm(core, tag + "ln_", X, XN, ident, XH, XL, inputs.load)
            route(core, inputs, tag, ident, XH, XL, E, slots, w, tile_expert, tiles, first_tile, grouped)
        experts(core, dram, tag, X, XN, ident, slots, w, tile_expert, rows_in, rows_out, E, NU, TR, NT, tiles, first_tile, BUFS)


def gated_moe(core, dram, X, ident, rows_in, rows_out):
    moe(core, dram, "m0_", X, ident, rows_in, rows_out, E0, 2, 116, 6, most_tiles(E0), 0, 2, grouped=False)


def grouped_moe(core, dram, X, ident, rows_in, rows_out):
    first = -(-B * S // TOK)
    moe(core, dram, "m1_", X, ident, rows_in, rows_out, E1, 1, 88, 2, first + most_tiles(E1), first, 3, grouped=True)


def causal_attention(core, dram, X, ident):
    nc, psum = core.nc, core.psum
    HT = H // KD
    SCALE = HD ** -0.5
    with ExitStack() as ctx:
        XH = fixed(ctx, nc, "XH_c", [P, KD, B * S], F32R)
        XL = fixed(ctx, nc, "XL_c", [P, KD, B * S], F32R)
        with ExitStack() as stage:
            XN = fixed(stage, nc, "XN_c", [S, B, D])
            layernorm(core, "ln2_", X, XN, ident, XH, XL)
        wq = fixed(ctx, nc, "c_wq", [P, KD, D])
        wqh = fixed(ctx, nc, "c_wqh", [P, KD, D], F32R)
        wql = fixed(ctx, nc, "c_wql", [P, KD, D], F32R)
        wk = fixed(ctx, nc, "c_wk", [DC, D])
        wv = fixed(ctx, nc, "c_wv", [DC, D])
        wo = fixed(ctx, nc, "c_wo", [P, KD, D])
        lat = fixed(ctx, nc, "c_lat", [DC, B * S])
        mask = fixed(ctx, nc, "c_mask", [S, S])
        maskb = fixed(ctx, nc, "c_maskb", [S, S], BF16)
        identb = fixed(ctx, nc, "c_identb", [S, S], BF16)
        blocks = fixed(ctx, nc, "c_blocks", [P, HT])
        QT = fixed(ctx, nc, "c_QT", [P, KD, B * S])
        KTT = fixed(ctx, nc, "c_KT", [P, KD, B * S])
        V = fixed(ctx, nc, "c_V", [S, B, D])

        loaded = core.sem("ca_loaded")
        parts = core.sem("ca_parts")
        chain = core.sem("ca_chain")
        proj = core.sem("ca_proj")
        moved_a = core.sem("ca_moveda")
        moved_v = core.sem("ca_movedv")
        tiles = [("q", k, c) for c in range(NC) for k in range(KD)] + [("k", k, c) for c in range(NC) for k in range(KD)]
        tiles += [("v", b, 0) for b in range(B)]

        with nc.Block() as block:

            @block.sync
            def _(sp):
                for t, name in ((wq, "c_wq"), (wk, "c_wk"), (wv, "c_wv"), (wo, "c_wo"), (lat, "c_lat"),
                                (mask, "c_mask"), (blocks, "c_blocks")):
                    sp.dma_start(t[:], dram[name]).then_inc(loaded, 16)

            @block.tensor
            def _(pe):
                pe.wait_ge(loaded, 16 * 7)
                pe.wait_ge(parts, 1)
                for n, (kind, k, c) in enumerate(tiles):
                    if n >= 8:
                        pe.wait_ge(moved_v if n % 2 else moved_a, (n - 8) // 2 + 1)
                    out = psum[n % 8]
                    cols = slice(c * CH, (c + 1) * CH)
                    if kind == "q":
                        last = split_products(nc, out[:, 0:CH], [(wqh[:, j, k * P:(k + 1) * P], wql[:, j, k * P:(k + 1) * P],
                                                                  XH[:, j, cols], XL[:, j, cols]) for j in range(KD)])
                    elif kind == "k":
                        last = nc.tensor.matmul(out[:, 0:CH], wk[:, k * P:(k + 1) * P], lat[:, cols], start=True, stop=True)
                    else:
                        last = nc.tensor.matmul(out[0:S, 0:D], lat[:, k * S:(k + 1) * S], wv[:], start=True, stop=True)
                    last.then_inc(proj, 1)

            def place(n):
                kind, k, c = tiles[n]
                if kind == "v":
                    return V[:, k, :], psum[n % 8][0:S, 0:D]
                return (QT if kind == "q" else KTT)[:, k, c * CH:(c + 1) * CH], psum[n % 8][:, 0:CH]

            @block.scalar
            def _(act):
                for n in range(0, len(tiles), 2):
                    act.wait_ge(proj, n + 1)
                    nc.scalar.activation(*place(n), ACT.Copy).then_inc(moved_a, 1)

            @block.vector
            def _(v):
                do = Chain(v, chain)
                v.wait_ge(loaded, 16 * 7)
                do(nc.vector.tensor_copy(wqh[:], wq[:]))
                do(nc.vector.tensor_tensor(wql[:], wq[:], as_f32(wqh[:]), ALU.subtract))
                do(nc.vector.tensor_copy(maskb[:], mask[:]))
                nc.vector.tensor_copy(identb[:], ident[0:S, 0:S]).then_inc(parts, 1)
                for n in range(1, len(tiles), 2):
                    v.wait_ge(proj, n + 1)
                    nc.vector.tensor_copy(*place(n)).then_inc(moved_v, 1)

        qb = [fixed(ctx, nc, f"c_qb{u}", [P, S]) for u in range(2)]
        kb = [fixed(ctx, nc, f"c_kb{u}", [P, HT, S]) for u in range(2)]
        nmax = [fixed(ctx, nc, f"c_nmax{u}", [S, 2, HT]) for u in range(2)]
        sums = fixed(ctx, nc, "c_sums", [S, 2, H])
        rsum = fixed(ctx, nc, "c_rsum", [S, H])
        PR = [fixed(ctx, nc, f"c_PR{u}", [S, HT, S]) for u in range(2)]
        PT = [fixed(ctx, nc, f"c_PT{u}", [S, HT, S]) for u in range(2)]
        O = fixed(ctx, nc, "c_O", [S, D])
        OT = fixed(ctx, nc, "c_OT", [P, KD, S])
        HB = HT // 2
        SC, TB, OB, LB = 0, 4, 6, 7

        ops_ready = core.sem("cb_ops")
        s_ready = core.sem("cb_s")
        max_ready = core.sem("cb_max")
        neg_ready = core.sem("cb_neg")
        e_ready = core.sem("cb_e")
        t_ready = core.sem("cb_t")
        tc_act = core.sem("cb_tca")
        tc_dve = core.sem("cb_tcv")
        o_ready = core.sem("cb_o")
        r_ready = core.sem("cb_r")
        on_ready = core.sem("cb_on")
        ot_ready = core.sem("cb_ot")
        otc_ready = core.sem("cb_otc")
        y_ready = core.sem("cb_y")
        x_done = core.sem("cb_x")

        def steps(eng, body):
            for i in (0, 1):
                body(i, i % 2)
            with eng.Fori(0, (B - 4) // 2) as j:
                for w in range(2):
                    body(j * 2 + (2 + w), w)
            for i in range(B - 2, B + 2):
                body(i, i % 2)

        def has(i, first, last):
            return not isinstance(i, int) or first <= i <= last

        def bank_heads(ap):
            return ap.rearrange("p (h s) -> p h s", s=S)

        with nc.Block() as block:

            @block.tensor
            def _(pe):
                def scores(i, u):
                    n = i * 2 + u
                    pe.wait_ge(ops_ready, n + 1)
                    if has(i, 1, B):
                        pe.wait_ge(e_ready, n * HT - HT)
                    for g in range(2):
                        out = psum[SC + 2 * u + g][0:S, 0:HB * S]
                        nc.tensor.matmul(out, qb[u][:], kb[u][:, g * HB:(g + 1) * HB, :].rearrange("p h s -> p (h s)"),
                                         start=True, stop=False)
                        last = nc.tensor.matmul(out, identb[:],
                                                maskb[:].rearrange("p (o s) -> p o s", o=1).to_broadcast([S, HB, S]),
                                                start=False, stop=True)
                    last.then_inc(s_ready, 1)

                def turn(n, u, first):
                    pe.wait_ge(e_ready, n * HT + HT)
                    if not first:
                        pe.wait_ge(tc_act, n)
                        pe.wait_ge(tc_dve, n)
                    for h in range(HT):
                        ins = nc.tensor.transpose(psum[TB + h // HB][0:S, (h % HB) * S:(h % HB + 1) * S], PR[u][:, h, :],
                                                  ident[0:S, 0:S])
                        if h % HB == HB - 1:
                            ins.then_inc(t_ready, 1)

                def values(i, n, u):
                    pe.wait_ge(tc_act, n + 1)
                    pe.wait_ge(tc_dve, n + 1)
                    if u == 0 and has(i, 2, B):
                        pe.wait_ge(on_ready, i - 1)
                    for h in range(HT):
                        d = (u * HT + h) * HD
                        last = nc.tensor.matmul(psum[OB][0:S, d:d + HD], PT[u][:, h, :], V[:, i - 1, d:d + HD],
                                                start=True, stop=True)
                    last.then_inc(o_ready, 1)

                def step(i, w):
                    n = i * 2
                    if has(i, 0, B - 1):
                        scores(i, 0)
                    if has(i, 2, B + 1):
                        pe.wait_ge(on_ready, i - 1)
                        if has(i, 3, B + 1):
                            pe.wait_ge(x_done, i - 2)
                        for k in range(KD):
                            last = nc.tensor.transpose(psum[LB][:, k * S:(k + 1) * S], O[:, k * P:(k + 1) * P], ident[0:S, 0:S])
                        last.then_inc(ot_ready, 1)
                    if has(i, 1, B):
                        turn(n - 1, 1, False)
                        values(i, n - 2, 0)
                    if has(i, 0, B - 1):
                        scores(i, 1)
                        turn(n, 0, isinstance(i, int) and i == 0)
                    if has(i, 2, B + 1):
                        pe.wait_ge(otc_ready, i - 1)
                        for k in range(KD):
                            last = nc.tensor.matmul(psum[LB][0:S, 0:D], OT[:, k, :], wo[:, k, :], start=k == 0, stop=k == KD - 1)
                        last.then_inc(y_ready, 1)
                    if has(i, 1, B):
                        values(i, n - 1, 1)
                steps(pe, step)

            @block.scalar
            def _(act):
                def exps(i, u, w):
                    n = i * 2 + u
                    act.wait_ge(neg_ready, n + 1)
                    if has(i, 1, B):
                        act.wait_ge(t_ready, n * 2 - 2)
                    if has(i, 2, B):
                        act.wait_ge(r_ready, i - 1)
                    for h in range(HT):
                        nc.scalar.activation(PR[u][:, h, :], psum[SC + 2 * u + h // HB][0:S, (h % HB) * S:(h % HB + 1) * S],
                                             ACT.Exp, bias=nmax[u][:, 1, h:h + 1], scale=SCALE,
                                             accum_out=sums[:, w, u * HT + h:u * HT + h + 1]).then_inc(e_ready, 1)

                def move(n, u):
                    act.wait_ge(t_ready, n * 2 + 2)
                    nc.scalar.activation(PT[u][:, 0:HB, :], bank_heads(psum[TB][0:S, 0:HB * S]), ACT.Copy).then_inc(tc_act, 1)

                def step(i, w):
                    n = i * 2
                    if has(i, 0, B - 1):
                        exps(i, 0, w)
                    if has(i, 1, B):
                        move(n - 1, 1)
                    if has(i, 2, B + 1):
                        act.wait_ge(ot_ready, i - 1)
                        if has(i, 3, B + 1):
                            act.wait_ge(y_ready, i - 2)
                        nc.scalar.activation(OT[:], bank_heads(psum[LB][:, 0:KD * S]), ACT.Copy).then_inc(otc_ready, 1)
                    if has(i, 0, B - 1):
                        exps(i, 1, w)
                        move(n, 0)
                steps(act, step)

            @block.vector
            def _(v):
                def operands(i, u):
                    n = i * 2 + u
                    if has(i, 1, B):
                        v.wait_ge(s_ready, n - 1)
                    nc.vector.tensor_tensor(kb[u][:], KTT[:, u:u + 1, bass.ts(i, S)].to_broadcast([P, HT, S]),
                                            blocks[:].rearrange("p (h o) -> p h o", o=1).to_broadcast([P, HT, S]), ALU.mult)
                    nc.vector.tensor_copy(qb[u][:], QT[:, u, bass.ts(i, S)]).then_inc(ops_ready, 1)

                def maxima(i, u):
                    n = i * 2 + u
                    v.wait_ge(s_ready, n + 1)
                    if has(i, 1, B):
                        v.wait_ge(e_ready, n * HT - HT)
                    for g in range(2):
                        nc.vector.tensor_reduce(nmax[u][:, 0, g * HB:(g + 1) * HB],
                                                bank_heads(psum[SC + 2 * u + g][0:S, 0:HB * S]), AX.X,
                                                ALU.max).then_inc(max_ready, 1)
                    v.wait_ge(max_ready, n * 2 + 2)
                    nc.vector.tensor_scalar(nmax[u][:, 1, :], nmax[u][:, 0, :], -SCALE, None, ALU.mult).then_inc(neg_ready, 1)

                def move(n, u):
                    v.wait_ge(t_ready, n * 2 + 2)
                    nc.vector.tensor_copy(PT[u][:, HB:, :], bank_heads(psum[TB + 1][0:S, 0:HB * S])).then_inc(tc_dve, 1)

                operands(0, 0)
                operands(0, 1)

                def step(i, w):
                    n = i * 2
                    if has(i, 0, B - 1):
                        maxima(i, 0)
                    if has(i, 0, B - 2):
                        operands(i + 1, 0)
                    if has(i, 1, B):
                        move(n - 1, 1)
                    if has(i, 0, B - 1):
                        maxima(i, 1)
                    if has(i, 0, B - 2):
                        operands(i + 1, 1)
                    if has(i, 0, B - 1):
                        move(n, 0)
                    if has(i, 2, B + 1):
                        v.wait_ge(y_ready, i - 1)
                        nc.vector.tensor_tensor(X[:, i - 2, :], psum[LB][0:S, 0:D], X[:, i - 2, :], ALU.add).then_inc(x_done, 1)
                    if has(i, 1, B):
                        if has(i, 2, B):
                            v.wait_ge(on_ready, i - 1)
                        v.wait_ge(e_ready, n * HT)
                        nc.vector.reciprocal(rsum[:], sums[:, 1 - w, :]).then_inc(r_ready, 1)
                        v.wait_ge(r_ready, i)
                        v.wait_ge(o_ready, n)
                        if has(i, 2, B):
                            v.wait_ge(ot_ready, i - 1)
                        nc.vector.tensor_tensor(O[:].rearrange("p (h d) -> p h d", h=H),
                                                psum[OB][0:S, 0:D].rearrange("p (h d) -> p h d", h=H),
                                                rsum[:].rearrange("p (h o) -> p h o", o=1).to_broadcast([S, H, HD]),
                                                ALU.mult).then_inc(on_ready, 1)
                steps(v, step)


def model(nc, dram, out):
    with ExitStack() as ctx:
        core = Core(nc, ctx)
        X = fixed(ctx, nc, "X", [S, B, D])
        ident = fixed(ctx, nc, "ident", [P, P])
        loaded = core.sem("loaded")
        queries = nc.dram_tensor("queries", (B, P, H, S), F32).ap()
        rows_in = nc.dram_tensor("rows_in", (ROWS, D), F32).ap()
        rows_out = nc.dram_tensor("rows_out", (ROWS, D), F32).ap()
        with nc.Block() as block:

            @block.sync
            def _(sp):
                sp.dma_start(X[:], dram["x"].rearrange("b s d -> s b d")).then_inc(loaded, 16)
                sp.dma_start(ident[:], dram["ident"]).then_inc(loaded, 16)
                sp.wait_ge(loaded, 32)

        with ExitStack() as layer:
            BB = fixed(layer, nc, "BB", [P, H // 2, D])
            with ExitStack() as stage:
                XH = fixed(stage, nc, "XH_a", [P, KD, B * S], F32R)
                XL = fixed(stage, nc, "XL_a", [P, KD, B * S], F32R)
                AH = fixed(stage, nc, "AH", [P, KD, H, DQ], F32R)
                AL = fixed(stage, nc, "AL", [P, KD, H, DQ], F32R)
                M2 = fixed(stage, nc, "M2", [HALF, 2, H, P])
                with ExitStack() as norm:
                    XN = fixed(norm, nc, "XN_a", [S, B, D])
                    weights = FoldInputs(core, norm, dram)
                    layernorm(core, "ln0_", X, XN, ident, XH, XL, weights.load)
                    fold_weights(core, weights, AH, AL, M2, BB)
                latent_queries(core, dram, XH, XL, AH, AL, M2, queries, rows_in)
            latent_attention(core, dram, X, ident, queries, BB)
        core.release()
        gated_moe(core, dram, X, ident, rows_in, rows_out)
        causal_attention(core, dram, X, ident)
        core.release()
        grouped_moe(core, dram, X, ident, rows_in, rows_out)
        stored = core.sem("stored")
        with nc.Block() as block:

            @block.sync
            def _(sp):
                sp.dma_start(out.rearrange("b s d -> s b d"), X[:]).then_inc(stored, 16)
                sp.wait_ge(stored, 16)


def rope_tables(length, dim):
    import numpy as np
    inv = (np.float32(1.0) / np.power(np.float32(10000.0), np.arange(0, dim, 2, dtype=np.float32) / np.float32(dim)))
    f = np.arange(length, dtype=np.float32)[:, None] * inv.astype(np.float32)[None, :]
    return np.repeat(np.sin(f), 2, axis=-1), np.repeat(np.cos(f), 2, axis=-1)


def layouts(inputs):
    import numpy as np
    a = {k: np.asarray(v) for k, v in inputs.items()}
    T = np.ascontiguousarray
    out = {
        "x": a["x"],
        "Wq": a["L0_xattn_Wq"],
        "w_kc_q": a["L0_xattn_w_kc_q"],
        "w_kc_kv": a["L0_xattn_w_kc_kv"],
        "W_qrT": T(a["L0_xattn_W_qr"].transpose(2, 0, 1)),
        "W_krT": T(a["L0_xattn_W_kr"].transpose(2, 0, 1)),
        "WoT": T(a["L0_xattn_Wo"].T),
        "ident": np.eye(P, dtype=np.float32),
    }
    sin, cos = rope_tables(S, DQ)
    sin, cos = sin.T, cos.T
    out["rope_q"] = T(np.stack([cos[:HALF], -sin[:HALF], cos[HALF:], sin[HALF:]], axis=1))
    ctxT = a["ctx_512"].transpose(0, 2, 1)
    swapped = np.concatenate([ctxT[:, DC // 2:], ctxT[:, :DC // 2]], axis=1)
    out["ctx_T"] = T(np.stack([np.concatenate([ctxT, ctxT], axis=1), np.concatenate([swapped, swapped], axis=1)], axis=2))
    padded = np.zeros((B, SKP, DC), np.float32)
    padded[:, :SK] = a["ctx_512"]
    out["ctx_k"] = T(padded.reshape(B, KT, P, DC).transpose(0, 2, 1, 3))
    sin, cos = rope_tables(SK, DC)
    sign = np.where(np.arange(DC) < DC // 2, -1.0, 1.0).astype(np.float32)
    sin = sin * sign
    out["rope_T"] = T(np.stack([np.concatenate([cos.T, cos.T]), np.concatenate([sin.T, sin.T])], axis=1))
    table = np.zeros((2, SKP, DC), np.float32)
    table[0, :SK], table[1, :SK] = cos, sin
    out["rope_k"] = T(table.reshape(2, KT, P, DC).transpose(2, 0, 1, 3))
    ones = np.zeros((SKP, DC), np.float32)
    ones[:SK] = 1.0
    out["key_ones"] = T(ones.reshape(KT, P, DC).transpose(1, 0, 2))
    more_layouts(a, out)
    return out


def more_layouts(a, out):
    import numpy as np
    T = np.ascontiguousarray

    def by_part(w, ni):
        return w.reshape(w.shape[0], KD, P, ni).transpose(0, 2, 1, 3)

    E, I, NI, TR = 8, 688, 696, 116
    gu = np.zeros((E, P, KD, 2, NI), np.float32)
    gu[:, :, :, 0, :I] = by_part(a["L0_ffn_Wg"].transpose(0, 2, 1), I)
    gu[:, :, :, 1, :I] = by_part(a["L0_ffn_Wu"].transpose(0, 2, 1), I)
    out["m0_up"] = gu
    wd = np.zeros((E, NI, D), np.float32)
    wd[:, :I] = a["L0_ffn_Wd"].transpose(0, 2, 1)
    out["m0_down"] = T(wd.reshape(E, NI // TR, TR, D).transpose(0, 2, 1, 3))
    out["m0_router"] = T(a["L0_ffn_router_w"].T.reshape(KD, P, E).transpose(1, 0, 2))
    route_tables(out, "m0_", E, most_tiles(E))

    wkv = a["L1_xattn_Wkv_expand"]
    out["c_wq"] = T(a["L1_xattn_Wq"].T.reshape(KD, P, D).transpose(1, 0, 2))
    out["c_wk"], out["c_wv"] = T(wkv[:D].T), T(wkv[D:].T)
    out["c_wo"] = T(a["L1_xattn_Wout"].T.reshape(KD, P, D).transpose(1, 0, 2))
    out["c_lat"] = T(a["ctx_512"][:, :S].transpose(2, 0, 1).reshape(DC, B * S))
    out["c_mask"] = np.triu(np.full((S, S), -3.0e38, np.float32), 1)
    out["c_blocks"] = np.repeat(np.eye(H // KD, dtype=np.float32), HD, axis=0)

    E, I, TR = 16, 176, 88
    w1 = np.concatenate([a["L1_ffn_w1"], a["L1_ffn_sw1"]])
    w2 = np.concatenate([a["L1_ffn_w2"], a["L1_ffn_sw2"]])
    out["m1_up"] = T(by_part(w1, I).reshape(E + 1, P, KD, 1, I))
    out["m1_down"] = T(w2.reshape(E + 1, I // TR, TR, D).transpose(0, 2, 1, 3))
    out["m1_router"] = T(a["L1_ffn_gate_w"].T.reshape(KD, P, E).transpose(1, 0, 2))
    route_tables(out, "m1_", E, -(-B * S // TOK) + most_tiles(E))


def route_tables(out, tag, experts, tiles):
    import numpy as np
    every = lambda a: np.ascontiguousarray(np.broadcast_to(np.asarray(a, np.float32), (S,) + np.shape(a)))
    out[tag + "iota"] = every(np.arange(experts))
    out[tag + "steps"] = every(np.arange(-(-B * S // TOK)) * TOK)
    out[tag + "below"] = every(np.tril(np.ones((experts, experts)), -1))
    out[tag + "order"] = every(np.arange(tiles))
    out[tag + "tri"] = np.triu(np.ones((S, S), np.float32), 1)


def kernel(**inputs):
    import numpy as _np
    import concourse.bacc as _bacc
    from concourse import mybir as _mybir
    from concourse.bass_utils import run_bass_kernel_spmd as _run

    nc = _bacc.Bacc("TRN2", target_bir_lowering=False, num_devices=1)
    arrays, dram = {}, {}
    for name, a in layouts(inputs).items():
        a = _np.ascontiguousarray(a)
        arrays[f"in_{name}"] = a
        dram[name] = nc.dram_tensor(f"in_{name}", a.shape, _mybir.dt.from_np(a.dtype), kind="ExternalInput").ap()
    out = nc.dram_tensor("out", (B, S, D), F32, kind="ExternalOutput").ap()
    model(nc, dram, out)
    r = _run(nc, [arrays], core_ids=[0])
    return r.results[0]["out"]
```

```python
from contextlib import ExitStack

import concourse.bass as bass
from concourse import mybir

ALU = mybir.AluOpType
ACT = mybir.ActivationFunctionType
F32 = mybir.dt.float32
F32R = mybir.dt.float32r
BF16 = mybir.dt.bfloat16
U32 = mybir.dt.uint32
AX = mybir.AxisListType

P = 128
B, S, D = 16, 100, 256
SK, DC = 1444, 64
H = 16
K0, DQ, R0 = 128, 192, 64
KD = D // P
CB = 4
CH = CB * S
NC = B // CB
HALF = DQ // 2
KT = -(-SK // P)
SKP = KT * P
HD = D // H
EPS = 1e-5
E0, E1 = 8, 16
TOK = 256
PSUM_COLS = 512


def most_tiles(experts):
    return (2 * B * S + experts * (TOK - 1)) // TOK


ROWS = TOK * (-(-B * S // TOK) + most_tiles(E1))


class Core:

    def __init__(self, nc, ctx):
        self.nc, self.ctx = nc, ctx
        self.psum = [ctx.enter_context(nc.psum_tensor(f"bank{i}", [P, PSUM_COLS], F32)) for i in range(8)]

        self.stats = fixed(ctx, nc, "stats", [S, B, 6])
        self.sems = []

    def batch_stats(self, X, b):
        return self.nc.vector.bn_stats(self.stats[:, b, :], X[:, b, :])

    def sem(self, name):
        self.sems.append(self.nc.alloc_semaphore(name=name))
        return self.sems[-1]

    def release(self):
        self.nc.clear_and_free_semaphores(self.sems)
        self.nc.all_engine_barrier()
        self.sems = []


def fixed(ctx, nc, name, shape, dtype=F32):
    return ctx.enter_context(nc.sbuf_tensor(name, shape, dtype))


def as_f32(ap):
    return ap.bitcast(F32)


def layernorm(core, tag, X, XN, ident, XH, XL, known=0, loads=None, first=None):
    nc, psum = core.nc, core.psum
    with ExitStack() as ctx:
        stats = core.stats
        small = fixed(ctx, nc, tag + "small", [S, 8, B])
        dve = core.sem(tag + "dve")
        var_ready = core.sem(tag + "var")
        std_ready = core.sem(tag + "std")
        xn_ready = core.sem(tag + "xn")
        turned = core.sem(tag + "turned")
        hi_ready = core.sem(tag + "hi")
        with nc.Block() as block:

            @block.sync
            def _(sp):
                if loads:
                    loads(sp)

            @block.vector
            def _(v):
                for b in range(known, B):
                    core.batch_stats(X, b).then_inc(dve, 1)
                mean, var, std, rstd, diff, sq, y2 = (small[:, i, :] for i in range(7))
                me, qe, mo, qo = (stats[:, :, i] for i in (1, 2, 4, 5))
                step = B - known

                def chained(ins):
                    nonlocal step
                    step += 1
                    ins.then_inc(dve, 1)
                    v.wait_ge(dve, step)

                v.wait_ge(dve, step)
                chained(nc.vector.tensor_tensor(mean, me, mo, ALU.add))
                chained(nc.vector.tensor_scalar(mean, mean, 0.5, None, ALU.mult))
                chained(nc.vector.tensor_tensor(diff, me, mo, ALU.subtract))
                chained(nc.vector.tensor_tensor(diff, diff, diff, ALU.mult))
                chained(nc.vector.tensor_tensor(sq, qe, qo, ALU.add))
                chained(nc.vector.tensor_scalar(sq, sq, 1.0 / D, EPS, ALU.mult, ALU.add))
                nc.vector.scalar_tensor_tensor(var, diff, 0.25, sq, ALU.mult, ALU.add).then_inc(var_ready, 1)
                v.wait_ge(std_ready, 1)
                v.wait_ge(var_ready, 1)
                chained(nc.vector.reciprocal(rstd, std))
                chained(nc.vector.tensor_tensor(y2, rstd, rstd, ALU.mult))
                chained(nc.vector.tensor_tensor(y2, y2, var, ALU.mult))
                chained(nc.vector.tensor_scalar(y2, y2, -0.5, 1.5, ALU.mult, ALU.add))
                chained(nc.vector.tensor_tensor(rstd, rstd, y2, ALU.mult))
                for b in range(B):
                    nc.vector.tensor_scalar(XN[:, b, :], X[:, b, :], small[:, 0, b:b + 1], small[:, 3, b:b + 1],
                                            ALU.subtract, ALU.mult).then_inc(xn_ready, 1)
                for n in range(NC * KD):
                    c, k = divmod(n, KD)
                    v.wait_ge(hi_ready, n + 1)
                    hi = XH[:, k, c * CH:(c + 1) * CH]
                    nc.vector.tensor_tensor(XL[:, k, c * CH:(c + 1) * CH], psum[n][:, 0:CH], as_f32(hi), ALU.subtract)

            @block.scalar
            def _(act):
                act.wait_ge(var_ready, 1)
                nc.scalar.activation(small[:, 2, :], small[:, 1, :], ACT.Sqrt).then_inc(std_ready, 1)
                if first:
                    first[1](act)
                for n in range(NC * KD):
                    c, k = divmod(n, KD)
                    act.wait_ge(turned, n + 1)
                    nc.scalar.activation(XH[:, k, c * CH:(c + 1) * CH], psum[n][:, 0:CH], ACT.Copy).then_inc(hi_ready, 1)

            @block.tensor
            def _(pe):
                if first:
                    first[0](pe)
                for n in range(NC * KD):
                    c, k = divmod(n, KD)
                    pe.wait_ge(xn_ready, (c + 1) * CB)
                    for t in range(CB):
                        last = nc.tensor.transpose(psum[n][:, t * S:(t + 1) * S],
                                                   XN[:, c * CB + t, k * P:(k + 1) * P], ident[0:S, 0:S])
                    last.then_inc(turned, 1)


def split_products(nc, out, parts, first=True, last=True):
    todo = []
    for lh, ll, rh, rl in parts:
        todo += [(lh, rh), (lh, rl), (ll, rh)]
    for n, (lhs, rhs) in enumerate(todo):
        ins = nc.tensor.matmul(out, lhs, rhs, start=first and n == 0, stop=last and n == len(todo) - 1)
    return ins


class FoldInputs:

    def __init__(self, core, ctx, dram):
        nc = core.nc
        self.dram = dram
        self.wq = fixed(ctx, nc, "wq", [K0, H, D])
        self.wkq = fixed(ctx, nc, "wkq", [K0, H, DQ])
        self.wqr = fixed(ctx, nc, "wqr", [R0, H, DQ])
        self.wkr = fixed(ctx, nc, "wkr", [R0, H, DC])
        self.wo = fixed(ctx, nc, "wo", [K0, H, D])
        self.wkv = fixed(ctx, nc, "wkv", [K0, H, DC])
        self.in_q = core.sem("fw_in_q")
        self.in_r = core.sem("fw_in_r")
        self.in_o = core.sem("fw_in_o")

    def load(self, sp):
        dram = self.dram
        sp.dma_start(self.wq[:], dram["Wq"].rearrange("(h k) d -> k h d", k=K0)).then_inc(self.in_q, 16)
        sp.dma_start(self.wkq[:], dram["w_kc_q"].rearrange("h k q -> k h q")).then_inc(self.in_q, 16)
        sp.dma_start(self.wqr[:], dram["W_qrT"]).then_inc(self.in_r, 16)
        sp.dma_start(self.wkr[:], dram["W_krT"]).then_inc(self.in_r, 16)
        sp.dma_start(self.wo[:], dram["WoT"].rearrange("(h k) d -> k h d", k=K0)).then_inc(self.in_o, 16)
        sp.dma_start(self.wkv[:], dram["w_kc_kv"].rearrange("h k q -> k h q")).then_inc(self.in_o, 16)


def fold_weights(core, w, AH, AL, M2, BB):
    nc, psum = core.nc, core.psum
    wq, wkq, wqr, wkr, wo, wkv = w.wq, w.wkq, w.wqr, w.wkr, w.wo, w.wkv
    a_ready = core.sem("fw_a")
    a_hi = core.sem("fw_ahi")
    a_lo = core.sem("fw_alo")
    mb_ready = core.sem("fw_mb")
    m_out = core.sem("fw_mout")
    b_out = core.sem("fw_bout")
    with nc.Block() as block:

        @block.tensor
        def _(pe):
            pe.wait_ge(w.in_q, 32)
            for h in range(H):
                if h >= 2:
                    pe.wait_ge(a_lo, h - 1)
                for k in range(KD):
                    last = nc.tensor.matmul(psum[h % 2][:, k * DQ:(k + 1) * DQ], wq[:, h, k * P:(k + 1) * P],
                                            wkq[:, h, :], start=True, stop=True)
                last.then_inc(a_ready, 1)
            pe.wait_ge(w.in_r, 32)
            pe.wait_ge(w.in_o, 32)
            for h in range(H):
                if h >= 2:
                    pe.wait_ge(m_out, h - 1)
                    pe.wait_ge(b_out, h - 1)
                for half in range(2):
                    nc.tensor.matmul(psum[2 + h % 2][0:HALF, half * P:(half + 1) * P],
                                     wqr[:, h, half * HALF:(half + 1) * HALF],
                                     wkr[:, h, :].rearrange("p (o d) -> p o d", o=1).to_broadcast([R0, 2, DC]),
                                     start=True, stop=True)
                nc.tensor.matmul(psum[4 + h % 2][0:DC, 0:D], wkv[:, h, :], wo[:, h, :],
                                 start=True, stop=True).then_inc(mb_ready, 1)

        @block.scalar
        def _(act):
            for h in range(H):
                act.wait_ge(a_ready, h + 1)
                nc.scalar.activation(AH[:, :, h, :], psum[h % 2][:, 0:KD * DQ].rearrange("p (k q) -> p k q", k=KD),
                                     ACT.Copy).then_inc(a_hi, 1)
            for h in range(H):
                act.wait_ge(mb_ready, h + 1)
                nc.scalar.activation(BB[(h % 2) * DC:(h % 2 + 1) * DC, h // 2, :], psum[4 + h % 2][0:DC, 0:D],
                                     ACT.Copy).then_inc(b_out, 1)

        @block.vector
        def _(v):
            for h in range(H):
                v.wait_ge(a_hi, h + 1)
                nc.vector.tensor_tensor(AL[:, :, h, :], psum[h % 2][:, 0:KD * DQ].rearrange("p (k q) -> p k q", k=KD),
                                        as_f32(AH[:, :, h, :]), ALU.subtract).then_inc(a_lo, 1)
            for h in range(H):
                v.wait_ge(mb_ready, h + 1)
                nc.vector.tensor_copy(M2[:, :, h, :],
                                      psum[2 + h % 2][0:HALF, 0:2 * P].rearrange("p (a c) -> p a c", a=2)).then_inc(m_out, 1)


def latent_queries(core, dram, XH, XL, AH, AL, M2, queries, rows_in):
    nc, psum = core.nc, core.psum
    SLOTS, BUFS, TURNS = 4, 2, 4
    with ExitStack() as ctx:
        rope = fixed(ctx, nc, "rope_q", [HALF, 4, S])
        prod = fixed(ctx, nc, "rope_prod", [HALF, 2, 4, CH])
        rot = fixed(ctx, nc, "rotated", [HALF, TURNS, 2, CH])
        out = fixed(ctx, nc, "q_out", [P, SLOTS, CH], F32R)
        zeros = fixed(ctx, nc, "zeros", [P, 14, D])
        zeros_set = core.sem("lq_zeros")
        cleared = core.sem("lq_cleared")
        rope_in = core.sem("lq_rope")
        q_ready = core.sem("lq_q")
        mul_half = core.sem("lq_mulhalf")
        mul_done = core.sem("lq_mul")
        rot_done = core.sem("lq_rot")
        qq_ready = core.sem("lq_qq")
        lo_done = core.sem("lq_lo")
        hi_done = core.sem("lq_hi")
        sent = [core.sem(f"lq_sent{i}") for i in range(SLOTS)]
        with nc.Block() as block:

            @block.sync
            def _(sp):
                sp.dma_start(rope[:], dram["rope_q"]).then_inc(rope_in, 16)
                sp.wait_ge(zeros_set, 1)
                for r in range(0, ROWS // P, 14):
                    sp.dma_start(rows_in[r * P:(r + 14) * P].rearrange("(p j) d -> p j d", p=P), zeros[:]).then_inc(cleared, 16)
                for s in sent:
                    sp.sem_inc(s, 16)
                with sp.Fori(0, NC) as c:
                    for h in range(H):
                        sp.wait_ge(lo_done, c * H + (BUFS + h + 1))
                        sp.dma_start(queries[bass.ts(c, CB)].rearrange("b p h s -> p h b s")[:, h],
                                     as_f32(out[:, h % SLOTS, :]).rearrange("p (b s) -> p b s", b=CB)).then_inc(sent[h % SLOTS], 16)
                for s in sent:
                    sp.wait_ge(s, 16 * (1 + NC * H // SLOTS))
                sp.wait_ge(cleared, 16 * (ROWS // P // 14))

            @block.tensor
            def _(pe):
                def narrow(c, h):
                    pe.wait_ge(rot_done, c * H + (BUFS + h + 1))
                    pe.wait_ge(lo_done, c * H + (h + 1))
                    for half in range(2):
                        last = nc.tensor.matmul(psum[4 + h % 2][:, 0:CH], M2[:, half, h, :], rot[:, h % TURNS, half, :],
                                                start=half == 0, stop=half == 1)
                    last.then_inc(qq_ready, 1)

                pe.sem_inc(qq_ready, TURNS)
                with pe.Fori(0, NC) as c:
                    for h in range(H):
                        pe.wait_ge(mul_done, c * H + (h + 1))
                        for half in range(2):
                            last = split_products(nc, psum[2 * (h % 2) + half][0:HALF, 0:CH],
                                                  [(AH[:, k, h, half * HALF:(half + 1) * HALF],
                                                    AL[:, k, h, half * HALF:(half + 1) * HALF],
                                                    XH[:, k, bass.ts(c, CH)], XL[:, k, bass.ts(c, CH)]) for k in range(KD)])
                        last.then_inc(q_ready, 1)
                        if h >= 2:
                            narrow(c, h - 2)
                    narrow(c, H - 2)
                    narrow(c, H - 1)

            @block.vector
            def _(v):
                v.memset(zeros[:], 0.0).then_inc(zeros_set, 1)
                v.wait_ge(rope_in, 16)
                v.sem_inc(mul_done, BUFS)
                v.sem_inc(lo_done, BUFS)

                def low(c, h):
                    v.wait_ge(hi_done, c * H + (h + 1))
                    nc.vector.tensor_tensor(out[DC:P, h % SLOTS, :], psum[4 + h % 2][DC:P, 0:CH],
                                            as_f32(out[DC:P, h % SLOTS, :]), ALU.subtract).then_inc(lo_done, 1)

                with v.Fori(0, NC) as c:
                    for h in range(H):
                        v.wait_ge(q_ready, c * H + (h + 1))
                        v.wait_ge(rot_done, c * H + (h + 1))
                        for n, half in enumerate((0, 1, 1, 0)):
                            last = nc.vector.tensor_tensor(
                                prod[:, h % 2, n, :].rearrange("p (b s) -> p b s", b=CB),
                                psum[2 * (h % 2) + half][0:HALF, 0:CH].rearrange("p (b s) -> p b s", b=CB),
                                rope[:, n:n + 1, :].to_broadcast([HALF, CB, S]), ALU.mult)
                            if n == 1:
                                last.then_inc(mul_half, 1)
                        last.then_inc(mul_done, 1)
                        if h >= 2:
                            low(c, h - 2)
                    low(c, H - 2)
                    low(c, H - 1)

            @block.gpsimd
            def _(pool):
                pool.sem_inc(rot_done, BUFS)
                with pool.Fori(0, NC) as c:
                    for h in range(H):
                        pool.wait_ge(mul_half, c * H + (h + 1))
                        pool.wait_ge(qq_ready, c * H + (h + 1))
                        for half in range(2):
                            if half:
                                pool.wait_ge(mul_done, c * H + (BUFS + h + 1))
                            last = nc.gpsimd.tensor_tensor(rot[:, h % TURNS, half, :], prod[:, h % 2, 2 * half, :],
                                                           prod[:, h % 2, 2 * half + 1, :], ALU.add)
                        last.then_inc(rot_done, 1)

            @block.scalar
            def _(act):
                with act.Fori(0, NC) as c:
                    for h in range(H):
                        act.wait_ge(qq_ready, c * H + (TURNS + h + 1))
                        act.wait_ge(sent[h % SLOTS], c * (16 * H // SLOTS) + 16 * (h // SLOTS + 1))
                        nc.scalar.activation(out[:, h % SLOTS, :], psum[4 + h % 2][:, 0:CH], ACT.Copy).then_inc(hi_done, 1)


def latent_attention(core, dram, X, ident, queries, recips, BB):
    nc, psum = core.nc, core.psum
    BUFS = 3
    QG = H * S // CH
    HG = CH // S
    QT = -(-H * S // P)
    QW = QT * P
    NS = QG * KT
    KC = 3
    KW = [482, 482, 480]
    NF = QT * KC
    SB, FB = 3, 2
    EB, PB = 4, 6
    BEHIND = 4
    KS = DC + 2
    KR = SK // 2
    S0, F0, A0, MISC = 0, 3, 5, 7
    F_AT = 1
    TURN_AT, HI_AT = 42, 26
    RECIP_AT, CT_AT, OUT_AT = 9, 17, 20
    ROT_AT = (3, 5, 7, 10, 11, 12, 13, 19, 21, 24, 32, 34, 37)
    LOW_ON_VECTOR = (39, 41, 43, 45, 47)
    ROT = len(ROT_AT) - 1
    with ExitStack() as ctx:
        QS = [fixed(ctx, nc, f"QS{r}", [P, QW], F32R) for r in range(BUFS)]
        QB = [fixed(ctx, nc, f"QB{r}", [DC + 2, QW], F32R) for r in range(BUFS)]
        KH = [fixed(ctx, nc, f"KH{r}", [P, SKP], F32R) for r in range(BUFS)]
        KB = [fixed(ctx, nc, f"KB{r}", [DC + 2, SKP], F32R) for r in range(BUFS)]
        KVH = [fixed(ctx, nc, f"KVH{r}", [P, KT * KS + P - KS], F32R) for r in range(BUFS)]
        KVL = [fixed(ctx, nc, f"KVL{r}", [P, KT * KS + P - KS], F32R) for r in range(BUFS)]
        raw = fixed(ctx, nc, "raw", [P, 2, SK])
        rawk = fixed(ctx, nc, "rawk", [P, KT, DC])
        prodk = fixed(ctx, nc, "prodk", [P, KT, DC])
        ropeT = fixed(ctx, nc, "ropeT", [P, 2, SK])
        ropek = fixed(ctx, nc, "ropek", [P, 2, KT, DC])
        there = fixed(ctx, nc, "there", [P, KT, KS - DC])
        E = fixed(ctx, nc, "E", [P, EB, CH])
        EH = fixed(ctx, nc, "EH", [P, PB, CH], F32R)
        EL = fixed(ctx, nc, "EL", [P, PB, CH], F32R)
        PM = fixed(ctx, nc, "PM", [P, NF])
        NM = fixed(ctx, nc, "NM", [P, QT])
        MH = fixed(ctx, nc, "MH", [QT, P], F32R)
        ML = fixed(ctx, nc, "ML", [QT, P], F32R)
        CU = fixed(ctx, nc, "CU", [DC + 1, H, S])
        SR = fixed(ctx, nc, "SR", [H, S])
        RR = fixed(ctx, nc, "RR", [H, S])
        RS = fixed(ctx, nc, "RS", [DC, H, S])
        CT = fixed(ctx, nc, "CT", [P, H // 2, S])

        consts = core.sem("at_consts")
        ones_set = core.sem("at_ones")
        pads = core.sem("at_pads")
        q_in = [core.sem(f"at_q{r}") for r in range(BUFS)]
        kv_in = core.sem("at_kvin")
        rot_step = core.sem("at_rotstep")
        kh_ready = core.sem("at_kh")
        kvh_ready = core.sem("at_kvh")
        k_ready = core.sem("at_k")
        s_ready = core.sem("at_s")
        exp_done = core.sem("at_exp")
        hi_done = core.sem("at_hi")
        lo_pool, lo_vector = core.sem("at_lopool"), core.sem("at_lovector")
        av_done = core.sem("at_av")
        f_ready = core.sem("at_f")
        red_done = core.sem("at_red")
        nm_ready = core.sem("at_nm")
        turned = core.sem("at_turned")
        mh_ready = core.sem("at_mh")
        ml_ready = core.sem("at_ml")
        m_in = core.sem("at_min")
        cu_done = core.sem("at_cu")
        sr_in = core.sem("at_sr")
        recip = core.sem("at_recip")
        rr_out = core.sem("at_rrout")
        rs_in = core.sem("at_rs")
        ct_ready = core.sem("at_ct")
        out_ready = core.sem("at_out")
        res_done = core.sem("at_res")

        def key_loads(sp, b):
            sp.dma_start(raw[:], dram["ctx_T"][b]).then_inc(kv_in, 16)
            sp.dma_start(rawk[:], dram["ctx_k"][b]).then_inc(kv_in, 16)

        def query_loads(sp, b, r):
            sp.dma_start(as_f32(QS[r][:, 0:H * S]), queries[b].rearrange("p h s -> p (h s)")).then_inc(q_in[r], 16)
            sp.dma_start(as_f32(QB[r][0:DC, 0:H * S]),
                         queries[b].rearrange("p h s -> p (h s)")[0:DC]).then_inc(q_in[r], 16)

        def max_rows(sp, b, r):
            sp.wait_ge(ml_ready, b + 1)
            for row, part in enumerate((MH, ML)):
                sp.dma_start(as_f32(QB[r][DC + row:DC + row + 1, :]).rearrange("o (t p) -> o t p", p=P),
                             as_f32(part[:, :])).then_inc(m_in, 16)

        def wait_low(eng, b, n):
            earlier = sum(1 for t in LOW_ON_VECTOR if t <= n)
            if n in LOW_ON_VECTOR:
                eng.wait_ge(lo_vector, b_val(b) * len(LOW_ON_VECTOR) + earlier)
            else:
                eng.wait_ge(lo_pool, b_val(b) * (NS - len(LOW_ON_VECTOR)) + (EB + n + 1 - earlier))

        def low_part(eng, ops, b, n, sem):
            eng.wait_ge(hi_done, b_val(b) * NS + (n + 1))
            ops.tensor_tensor(EL[:, n % PB, :], E[:, n % EB, :], as_f32(EH[:, n % PB, :]), ALU.subtract).then_inc(sem, 1)

        def divisors(sp, b):
            sp.wait_ge(cu_done, b_val(b) * QG + (2 + QG))
            sp.dma_start(SR[:], CU[DC:DC + 1, :, :]).then_inc(sr_in, 16)
            sp.wait_ge(recip, b_val(b) + 1)
            sp.dma_start(recips[b_val(b)], RR[:]).then_inc(rr_out, 16)
            sp.wait_ge(rr_out, b_val(b) * 16 + 32)
            sp.wait_ge(ct_ready, b_val(b) + 1)
            sp.dma_start(RS[:], recips[b_val(b)].rearrange("(o h) s -> o h s", o=1).to_broadcast([DC, H, S])).then_inc(rs_in, 16)

        def rotate_part(eng, ops, b, i, step):
            r = b_mod(b)

            def parts_done(n):
                eng.wait_ge(rot_step, b_val(b) * ROT + n)

            half = slice((i % 2) * KR, (i % 2 + 1) * KR)
            rows_h = KVH[r][:, 0:KT * KS].rearrange("p (t c) -> p t c", c=KS)[:, :, 0:DC]
            rows_l = KVL[r][:, 0:KT * KS].rearrange("p (t c) -> p t c", c=KS)[:, :, 0:DC]
            if i == 0:
                eng.wait_ge(kv_in, b_val(b) * 32 + 32)
            if i < 4:
                row = i // 2
                ins = ops.tensor_tensor(raw[:, row, half], raw[:, row, half], ropeT[:, row, half], ALU.mult)
            elif i < 6:
                a, z = (i - 4) * DC // 2, (5 - i) * DC // 2
                ins = ops.tensor_tensor(prodk[:, :, a:a + DC // 2], rawk[:, :, z:z + DC // 2],
                                        ropek[:, 1, :, a:a + DC // 2], ALU.mult)
            elif i == 6:
                parts_done(6)
                ins = ops.tensor_tensor(rawk[:], rawk[:], ropek[:, 0], ALU.mult)
            elif i < 9:
                half = slice((i - 7) * KR, (i - 6) * KR)
                parts_done(4)
                ins = ops.tensor_tensor(raw[:, 0, half], raw[:, 0, half], raw[:, 1, half], ALU.add)
            elif i == 9:
                parts_done(7)
                ins = ops.tensor_tensor(rawk[:], rawk[:], prodk[:], ALU.add)
            elif i < 12:
                half = slice((i - 10) * KR, (i - 9) * KR)
                eng.wait_ge(kh_ready, b_val(b) * 2 + (i - 9))
                ins = ops.tensor_tensor(KB[r][0:DC, half], raw[0:DC, 0, half], as_f32(KH[r][0:DC, half]), ALU.subtract)
            else:
                eng.wait_ge(kvh_ready, b_val(b) + 1)
                ops.tensor_tensor(rows_l, rawk[:], as_f32(rows_h), ALU.subtract).then_inc(k_ready, 1)
                return
            ins.then_inc(rot_step, 1)

        def keys_high(act, b, part, step):
            half = slice(part * KR, (part + 1) * KR)
            act.wait_ge(rot_step, b_val(b) * ROT + 9)
            if step is not None:
                act.wait_ge(av_done, b_val(step) * NS + PB)
            nc.scalar.activation(KH[b_mod(b)][:, half], raw[:, 0, half], ACT.Copy).then_inc(kh_ready, 1)

        def rows_high(act, b):
            act.wait_ge(rot_step, b_val(b) * ROT + 10)
            out = KVH[b_mod(b)][:, 0:KT * KS].rearrange("p (t c) -> p t c", c=KS)[:, :, 0:DC]
            nc.scalar.activation(out, rawk[:], ACT.Copy).then_inc(kvh_ready, 1)

        def f_banks(b):
            return FB + 2 if b is FIRST else FB

        def max_piece(pe, b, f):
            r = b_mod(b)
            t, j = divmod(f, KC)
            banks = f_banks(b)
            if f >= banks:
                pe.wait_ge(red_done, b_val(b) * NF + (f - banks + 1))
            elif b is not FIRST:
                pe.wait_ge(red_done, b_val(b) * NF)
            nc.tensor.matmul(psum[F0 + f % banks][:, 0:KW[j]], QS[r][:, t * P:(t + 1) * P],
                             KH[r][:, sum(KW[:j]):sum(KW[:j + 1])], start=True, stop=True).then_inc(f_ready, 1)

        def turn_max(pe, b):
            pe.wait_ge(nm_ready, b_val(b) + 1)
            nc.tensor.transpose(psum[MISC][0:QT, 0:P], NM[:, :], ident[:, :]).then_inc(turned, 1)

        def max_high(act, b):
            act.wait_ge(turned, b_val(b) + 1)
            if b is not FIRST:
                act.wait_ge(m_in, b_val(b) * 32)
            nc.scalar.activation(MH[:, :], psum[MISC][0:QT, 0:P], ACT.Copy).then_inc(mh_ready, 1)

        def max_low(v, b):
            v.wait_ge(mh_ready, b_val(b) + 1)
            nc.vector.tensor_tensor(ML[:, :], psum[MISC][0:QT, 0:P], as_f32(MH[:, :]), ALU.subtract).then_inc(ml_ready, 1)

        def reduce_piece(v, b, f):
            v.wait_ge(f_ready, b_val(b) * NF + (f + 1))
            if f == 0 and b is not FIRST:
                v.wait_ge(nm_ready, b_val(b))
            nc.vector.tensor_reduce(PM[:, f:f + 1], psum[F0 + f % f_banks(b)][:, 0:KW[f % KC]], AX.X, ALU.max).then_inc(red_done, 1)

        def batch_max(v, b):
            v.wait_ge(red_done, b_val(b) * NF + NF)
            if b is not FIRST:
                v.wait_ge(turned, b_val(b))
            nc.vector.tensor_reduce(NM[:, :], PM[:, :].rearrange("p (t k) -> p t k", k=KC), AX.X, ALU.max,
                                    negate=True).then_inc(nm_ready, 1)

        def project(pe, b):
            pe.wait_ge(ct_ready, b_val(b) + 2)
            for j in range(H // 2):
                last = nc.tensor.matmul(psum[MISC][0:S, 0:D], CT[:, j, :], BB[:, j, :], start=j == 0, stop=j == H // 2 - 1)
            last.then_inc(out_ready, 1)

        def add_output(v, b):
            v.wait_ge(out_ready, b_val(b) + 2)
            x = X[:, b_val(b), :]
            nc.vector.tensor_tensor(x, psum[MISC][0:S, 0:D], x, ALU.add).then_inc(res_done, 1)

        def reciprocals(v, b):
            v.wait_ge(sr_in, b_val(b) * 16 + 16)
            v.wait_ge(rr_out, b_val(b) * 16 + 16)
            nc.vector.reciprocal(RR[:], SR[:]).then_inc(recip, 1)

        def divide(v, b):
            v.wait_ge(rs_in, b_val(b) * 16 + 16)
            v.wait_ge(out_ready, b_val(b) + 1)
            for odd in range(2):
                heads = CU[0:DC].rearrange("p (j o) s -> p o j s", o=2)[:, odd]
                shares = RS[:].rearrange("p (j o) s -> p o j s", o=2)[:, odd]
                ins = nc.vector.tensor_tensor(CT[odd * DC:(odd + 1) * DC], heads, shares, ALU.mult)
            ins.then_inc(ct_ready, 1)

        def sums_out(act, b, g):
            act.wait_ge(av_done, b_val(b) * NS + (PB + KT * (g + 1)))
            if g == 0:
                act.wait_ge(ct_ready, b_val(b) + 1)
            nc.scalar.activation(CU[:, g * HG:(g + 1) * HG, :],
                                 psum[A0 + g % 2][0:DC + 1, 0:CH].rearrange("p (h s) -> p h s", s=S), ACT.Copy).then_inc(cu_done, 1)

        class Batch:
            def __init__(self, turn, r):
                self.turn, self.r = turn + r // BUFS, r % BUFS

            def __add__(self, n):
                return Batch(self.turn, self.r + n)

        def b_val(b):
            return b.turn * BUFS + b.r

        def b_mod(b):
            return b.r

        FIRST = Batch(0, 0)

        def before(b):
            return Batch(b.turn, b.r - 1) if b.r else Batch(b.turn - 1, BUFS - 1)

        def steps(eng, body):
            body(FIRST, True, True)
            with eng.Fori(0, (B - 1 - BUFS) // BUFS) as i:
                for u in range(BUFS):
                    body(Batch(i, 1 + u), True, True)
            body(Batch(0, B - 3), True, True)
            body(Batch(0, B - 2), True, False)
            body(Batch(0, B - 1), False, False)

        with nc.Block() as block:

            @block.sync
            def _(sp):
                sp.sem_inc(rr_out, 16)
                key_loads(sp, 0)
                sp.dma_start(ropeT[:], dram["rope_T"]).then_inc(consts, 16)
                sp.dma_start(ropek[:], dram["rope_k"]).then_inc(consts, 16)
                sp.dma_start(there[:], dram["key_ones"]).then_inc(consts, 16)
                query_loads(sp, 0, 0)
                query_loads(sp, 1, 1)
                sp.wait_ge(k_ready, 1)
                key_loads(sp, 1)
                max_rows(sp, 0, 0)
                sp.wait_ge(k_ready, 2)
                key_loads(sp, 2)

                def step(b, has_next, has_keys):
                    if b is not FIRST:
                        divisors(sp, before(b))
                    if has_keys:
                        sp.wait_ge(av_done, b_val(b) * NS + PB)
                        query_loads(sp, b_val(b + 2), b_mod(b + 2))
                        sp.wait_ge(k_ready, b_val(b) + 3)
                        if not (isinstance(b.turn, int) and b_val(b) == B - BUFS):
                            key_loads(sp, b_val(b + 3))
                    if has_next:
                        max_rows(sp, b_val(b + 1), b_mod(b + 1))

                steps(sp, step)
                divisors(sp, Batch(0, B - 1))

            @block.gpsimd
            def _(pool):
                pool.sem_inc(lo_pool, EB)
                pool.wait_ge(consts, 48)
                pool.wait_ge(k_ready, 1)
                for i in range(ROT + 1):
                    rotate_part(pool, nc.gpsimd, FIRST + 1, i, None)

                def step(b, has_next, has_keys):
                    for n in range(NS):
                        if n not in LOW_ON_VECTOR:
                            low_part(pool, nc.gpsimd, b, n, lo_pool)

                steps(pool, step)

            @block.scalar
            def _(act):
                act.sem_inc(exp_done, SB)
                act.sem_inc(cu_done, 2)
                for part in range(2):
                    keys_high(act, FIRST, part, None)
                act.wait_ge(ones_set, BUFS)
                rows_high(act, FIRST)
                max_high(act, FIRST)
                for part in range(2):
                    keys_high(act, FIRST + 1, part, None)
                rows_high(act, FIRST + 1)

                def high(b, n):
                    act.wait_ge(exp_done, b_val(b) * NS + (SB + n + 1))
                    act.wait_ge(av_done, b_val(b) * NS + (n + 1))
                    nc.scalar.activation(EH[:, n % PB, :], E[:, n % EB, :], ACT.Copy).then_inc(hi_done, 1)

                def step(b, has_next, has_keys):
                    for n in range(NS):
                        act.wait_ge(s_ready, b_val(b) * NS + (n + 1))
                        if n >= EB:
                            wait_low(act, b, n - EB)
                        elif b is not FIRST:
                            wait_low(act, before(b), NS + n - EB)
                        nc.scalar.activation(E[:, n % EB, :], psum[S0 + n % SB][:, 0:CH], ACT.Exp).then_inc(exp_done, 1)
                        if n:
                            high(b, n - 1)
                        if n in (HI_AT, HI_AT + 2) and has_keys:
                            keys_high(act, b + 2, (n - HI_AT) // 2, b)
                        if n == HI_AT + 4 and has_keys:
                            rows_high(act, b + 2)
                        if n == TURN_AT and has_next:
                            max_high(act, b + 1)
                        for g in range(QG):
                            if n == KT * (g + 1) + BEHIND + 2:
                                sums_out(act, b, g)
                        if n == KT * QG + BEHIND + 2 - NS and b is not FIRST:
                            sums_out(act, before(b), QG - 1)
                    high(b, NS - 1)

                steps(act, step)
                sums_out(act, Batch(0, B - 1), QG - 1)

            @block.tensor
            def _(pe):
                pe.sem_inc(av_done, PB)
                pe.sem_inc(out_ready, 1)
                pe.wait_ge(pads, BUFS)
                pe.wait_ge(consts, 48)
                pe.wait_ge(q_in[0], 32)
                pe.wait_ge(k_ready, 1)
                for f in range(NF):
                    max_piece(pe, FIRST, f)
                turn_max(pe, FIRST)

                def values(b, n):
                    g, t = divmod(n, KT)
                    wait_low(pe, b, n)
                    if t == 0:
                        pe.wait_ge(cu_done, b_val(b) * QG + (g + 1))
                    cols = slice(t * KS, t * KS + P)
                    split_products(nc, psum[A0 + g % 2][:, 0:CH],
                                   [(KVH[b_mod(b)][:, cols], KVL[b_mod(b)][:, cols], EH[:, n % PB, :], EL[:, n % PB, :])],
                                   first=t == 0, last=t == KT - 1).then_inc(av_done, 1)

                def step(b, has_next, has_keys):
                    r = b_mod(b)
                    pe.wait_ge(m_in, b_val(b) * 32 + 32)
                    for n in range(NS):
                        g, t = divmod(n, KT)
                        pe.wait_ge(exp_done, b_val(b) * NS + (n + 1))
                        out = psum[S0 + n % SB][:, 0:CH]
                        keys, cols = slice(t * P, (t + 1) * P), slice(g * CH, (g + 1) * CH)
                        nc.tensor.matmul(out, KH[r][:, keys], QS[r][:, cols], start=True, stop=False)
                        nc.tensor.matmul(out, KB[r][:, keys], QB[r][:, cols], start=False, stop=True).then_inc(s_ready, 1)
                        if has_next and n == F_AT:
                            pe.wait_ge(k_ready, b_val(b) + 2)
                            pe.wait_ge(q_in[b_mod(b + 1)], (b + 1).turn * 32 + 32)
                        if has_next and 0 <= n - F_AT < NF:
                            max_piece(pe, b + 1, n - F_AT)
                        if n >= BEHIND:
                            values(b, n - BEHIND)
                        elif b is not FIRST:
                            values(before(b), NS - BEHIND + n)
                        if n == OUT_AT and b is not FIRST:
                            project(pe, before(b))
                        if n == TURN_AT and has_next:
                            if b is not FIRST:
                                pe.wait_ge(res_done, b_val(b))
                            turn_max(pe, b + 1)

                steps(pe, step)
                for n in range(NS - BEHIND, NS):
                    values(Batch(0, B - 1), n)
                project(pe, Batch(0, B - 1))

            @block.vector
            def _(v):
                v.sem_inc(ct_ready, 1)
                for r in range(BUFS):
                    v.memset(as_f32(QS[r][:, H * S:]), 0.0)
                    v.memset(as_f32(KH[r][:, SK:]), 0.0)
                    v.memset(as_f32(KB[r][:, SK:]), 0.0)
                    v.memset(as_f32(KVL[r][:]), 0.0)
                    v.memset(as_f32(KVH[r][:]), 0.0)
                    v.memset(as_f32(KB[r][DC:DC + 2, 0:SK]), 1.0).then_inc(pads, 1)
                v.wait_ge(pads, BUFS)
                v.wait_ge(consts, 48)
                for r in range(BUFS):
                    out = KVH[r][:, 0:KT * KS].rearrange("p (t c) -> p t c", c=KS)[:, :, DC:KS]
                    nc.vector.tensor_copy(out, there[:]).then_inc(ones_set, 1)
                for i in range(ROT + 1):
                    rotate_part(v, nc.vector, FIRST, i, None)
                for f in range(NF):
                    reduce_piece(v, FIRST, f)
                batch_max(v, FIRST)
                max_low(v, FIRST)

                def step(b, has_next, has_keys):
                    for n in range(NS):
                        if has_next and 0 <= n - F_AT < NF:
                            reduce_piece(v, b + 1, n - F_AT)
                        if n - F_AT == NF and has_next:
                            batch_max(v, b + 1)
                        if n == RECIP_AT and b is not FIRST:
                            reciprocals(v, before(b))
                        if n == CT_AT and b is not FIRST:
                            divide(v, before(b))
                        if n == OUT_AT + 2 and b is not FIRST:
                            add_output(v, before(b))
                        if n in ROT_AT and has_keys:
                            rotate_part(v, nc.vector, b + 2, ROT_AT.index(n), b)
                        if n == TURN_AT + 1 and has_next:
                            max_low(v, b + 1)
                        if n - 1 in LOW_ON_VECTOR:
                            low_part(v, nc.vector, b, n - 1, lo_vector)
                    low_part(v, nc.vector, b, NS - 1, lo_vector)

                steps(v, step)
                v.wait_ge(res_done, B - 1)
                for b in range(B - 1):
                    core.batch_stats(X, b)
                reciprocals(v, Batch(0, B - 1))
                divide(v, Batch(0, B - 1))
                add_output(v, Batch(0, B - 1))


class RouterInputs:
    NAMES = ("router", "iota", "steps", "below", "order", "tri")

    def __init__(self, core, ctx, dram, tag, E, tiles):
        nc = core.nc
        self.dram, self.tag = dram, tag
        full = -(-B * S // TOK)
        self.router = fixed(ctx, nc, tag + "wr", [P, KD, E])
        self.iota = fixed(ctx, nc, tag + "iota", [S, E])
        self.steps = fixed(ctx, nc, tag + "steps", [S, full])
        self.below = fixed(ctx, nc, tag + "below", [S, E, E])
        self.order = fixed(ctx, nc, tag + "order", [S, tiles])
        self.tri = fixed(ctx, nc, tag + "tri", [S, S])
        self.tiles_of = (self.router, self.iota, self.steps, self.below, self.order, self.tri)
        self.loaded = core.sem(tag + "loaded")

    def load(self, sp):
        for t, name in zip(self.tiles_of, self.NAMES):
            sp.dma_start(t[:], self.dram[self.tag + name]).then_inc(self.loaded, 16)


class Chain:

    def __init__(self, eng, sem):
        self.eng, self.sem, self.done = eng, sem, 0

    def apart(self, ins):
        self.done += 1
        ins.then_inc(self.sem, 1)

    def catch_up(self):
        self.eng.wait_ge(self.sem, self.done)

    def __call__(self, ins):
        self.apart(ins)
        self.catch_up()


def route(core, inputs, tag, ident, XH, XL, E, slots, w, tile_expert, tiles, first_tile, grouped, stores):
    nc, psum = core.nc, core.psum
    G = 4
    FULL = -(-B * S // TOK)
    with ExitStack() as ctx:
        iota, steps, below, order, tri = inputs.iota, inputs.steps, inputs.below, inputs.order, inputs.tri
        WH = fixed(ctx, nc, tag + "wrh", [P, KD, P], F32R)
        WL = fixed(ctx, nc, tag + "wrl", [P, KD, P], F32R)
        flat = fixed(ctx, nc, tag + "flat", [E, B * S])
        trib = fixed(ctx, nc, tag + "trib", [S, S], BF16)
        onesb = fixed(ctx, nc, tag + "onesb", [S, S], BF16)
        sc = fixed(ctx, nc, tag + "sc", [S, B, E])
        top = fixed(ctx, nc, tag + "top", [S, B, 8])
        idx = fixed(ctx, nc, tag + "idx", [S, B, 8], U32)
        idf = fixed(ctx, nc, tag + "idf", [S, B, 8])
        one = fixed(ctx, nc, tag + "one", [S, B, E])
        two = fixed(ctx, nc, tag + "two", [S, B, E])
        both = fixed(ctx, nc, tag + "both", [S, B + 1, E], BF16)
        place = fixed(ctx, nc, tag + "place", [S, B, E])
        over = fixed(ctx, nc, tag + "over", [S, E, FULL])
        used = fixed(ctx, nc, tag + "used", [S, E])
        before = fixed(ctx, nc, tag + "before", [S, E, E])
        start = fixed(ctx, nc, tag + "start", [S, E])
        past = fixed(ctx, nc, tag + "past", [S, tiles, E])
        tef = fixed(ctx, nc, tag + "tef", [S, tiles])
        slf = fixed(ctx, nc, tag + "slf", [S, 2, B])
        gs = fixed(ctx, nc, tag + "gs", [S, B, G])
        sums = fixed(ctx, nc, tag + "sums", [S, B, G, G * (G - 1) // 2])
        ahead = fixed(ctx, nc, tag + "ahead", [S, B, G, G])
        rank = fixed(ctx, nc, tag + "rank", [S, B, G])
        parts = core.sem(tag + "parts")
        flat_ready = core.sem(tag + "flat")
        flat_in = core.sem(tag + "flat_in")
        scores = core.sem(tag + "scores")
        chosen = core.sem(tag + "chosen")
        ranked = core.sem(tag + "ranked")
        chain = core.sem(tag + "chain")
        asked = core.sem(tag + "asked")
        given = core.sem(tag + "given")
        with nc.Block() as block:

            @block.sync
            def _(sp):
                stores(sp)

            @block.tensor
            def _(pe):
                pe.wait_ge(parts, 1)
                for c in range(NC):
                    cols = slice(c * CH, (c + 1) * CH)
                    todo = [(w[:, k, :], x[:, k, cols]) for k in range(KD) for x in (XH, XL) for w in (WH, WL)]
                    for n, (lhs, rhs) in enumerate(todo):
                        last = nc.tensor.matmul(psum[2 + c][:, 0:CH], lhs, rhs, start=n == 0, stop=n == len(todo) - 1)
                    last.then_inc(flat_ready, 1)
                for b in range(B):
                    if b % CB == 0:
                        pe.wait_ge(flat_in, b // CB + 1)
                    last = nc.tensor.transpose(psum[0][0:S, b * E:(b + 1) * E], flat[:, b * S:(b + 1) * S], ident[0:E, 0:E])
                last.then_inc(scores, 1)
                pe.wait_ge(chosen, 1)
                nc.tensor.matmul(psum[1][0:S, 0:(B + 1) * E], trib[:], both[:].rearrange("p b e -> p (b e)"),
                                 start=True, stop=False)
                for b in range(B):
                    later = B - b
                    last = nc.tensor.matmul(psum[1][0:S, (b + 1) * E:(B + 1) * E], onesb[:],
                                            both[:, b:b + 1, :].to_broadcast([S, later, E]), start=False, stop=b == B - 1)
                last.then_inc(ranked, 1)

            @block.scalar
            def _(act):
                for c in range(NC):
                    act.wait_ge(flat_ready, c + 1)
                    nc.scalar.activation(flat[:, c * CH:(c + 1) * CH], psum[2 + c][0:E, 0:CH], ACT.Copy).then_inc(flat_in, 1)
                if grouped:
                    act.wait_ge(scores, 1)
                    nc.scalar.activation(sc[:].rearrange("p b e -> p (b e)"), psum[0][0:S, 0:B * E],
                                         ACT.Sigmoid).then_inc(given, 1)
                else:
                    act.wait_ge(asked, 1)
                    nc.scalar.activation(w[:, 1, :], w[:, 0, :], ACT.Exp).then_inc(given, 1)

            @block.vector
            def _(v):
                vec = nc.vector
                do = Chain(v, chain)
                vec.memset(as_f32(WH[:]), 0.0)
                do(vec.memset(as_f32(WL[:]), 0.0))
                v.wait_ge(inputs.loaded, 16 * len(inputs.NAMES))
                do(vec.tensor_copy(WH[:, :, 0:E], inputs.router[:]))
                vec.tensor_tensor(WL[:, :, 0:E], inputs.router[:], as_f32(WH[:, :, 0:E]), ALU.subtract).then_inc(parts, 1)
                vec.tensor_copy(trib[:], tri[:])
                vec.memset(onesb[:], 1.0)
                vec.memset(ahead[:], 0.0)
                do(vec.memset(both[:, B:, :], 0.0))
                if grouped:
                    v.wait_ge(given, 1)
                    g = sc[:].rearrange("p b (g i) -> p b g i", g=G)
                    pairs = [(i, j) for i in range(G) for j in range(i + 1, G)]
                    for n, (i, j) in enumerate(pairs):
                        do.apart(vec.tensor_tensor(sums[:, :, :, n], g[:, :, :, i], g[:, :, :, j], ALU.add))
                    do.catch_up()
                    do(vec.tensor_reduce(gs[:], sums[:], AX.X, ALU.max))
                    for i in range(G):
                        this = gs[:, :, i:i + 1]
                        if i:
                            do.apart(vec.tensor_tensor(ahead[:, :, i, 0:i], gs[:, :, 0:i], this.to_broadcast([S, B, i]), ALU.is_ge))
                        if i + 1 < G:
                            do.apart(vec.tensor_tensor(ahead[:, :, i, i + 1:], gs[:, :, i + 1:],
                                                       this.to_broadcast([S, B, G - 1 - i]), ALU.is_gt))
                    do.catch_up()
                    do(vec.tensor_reduce(rank[:], ahead[:], AX.X, ALU.add))
                    do(vec.tensor_scalar(rank[:], rank[:], 2.0, None, ALU.is_lt))
                    for i in range(G):
                        do.apart(vec.tensor_tensor(g[:, :, :, i], g[:, :, :, i], rank[:], ALU.mult))
                    do.catch_up()
                else:
                    v.wait_ge(scores, 1)
                    do(vec.tensor_copy(sc[:].rearrange("p b e -> p (b e)"), psum[0][0:S, 0:B * E]))
                for b in range(B):
                    do.apart(vec.max(top[:, b, :], sc[:, b, :]))
                do.catch_up()
                for b in range(B):
                    do.apart(vec.max_index(idx[:, b, :], top[:, b, :], sc[:, b, :]))
                do.catch_up()
                do(vec.tensor_copy(idf[:], idx[:]))
                for n, hot in enumerate((one, two)):
                    do.apart(vec.tensor_tensor(hot[:], iota[:].rearrange("p (o e) -> p o e", o=1).to_broadcast([S, B, E]),
                                         idf[:, :, n:n + 1].to_broadcast([S, B, E]), ALU.is_equal))
                do.catch_up()
                vec.tensor_tensor(both[:, 0:B, :], one[:], two[:], ALU.add).then_inc(chosen, 1)
                if grouped:
                    do(vec.tensor_tensor(w[:, 0, :], top[:, :, 0], top[:, :, 1], ALU.add))
                    do(vec.tensor_scalar(w[:, 0, :], w[:, 0, :], 1e-20, None, ALU.add))
                    do(vec.reciprocal(w[:, 1, :], w[:, 0, :]))
                    do(vec.tensor_tensor(w[:, 2, :], top[:, :, 0], w[:, 1, :], ALU.mult))
                    do(vec.tensor_tensor(w[:, 3, :], top[:, :, 1], w[:, 1, :], ALU.mult))
                else:
                    vec.tensor_tensor(w[:, 0, :], top[:, :, 1], top[:, :, 0], ALU.subtract).then_inc(asked, 1)
                    v.wait_ge(given, 1)
                    do(vec.tensor_scalar(w[:, 0, :], w[:, 1, :], 1.0, None, ALU.add))
                    do(vec.reciprocal(w[:, 2, :], w[:, 0, :]))
                    do(vec.tensor_tensor(w[:, 3, :], w[:, 1, :], w[:, 2, :], ALU.mult))
                v.wait_ge(ranked, 1)
                count = psum[1][0:S, B * E:(B + 1) * E].rearrange("p (e o) -> p e o", o=1)
                do(vec.tensor_tensor(over[:], count.to_broadcast([S, E, FULL]),
                                     steps[:].rearrange("p (o j) -> p o j", o=1).to_broadcast([S, E, FULL]), ALU.is_gt))
                do(vec.tensor_reduce(used[:], over[:], AX.X, ALU.add))
                do(vec.tensor_tensor(before[:], used[:].rearrange("p (o e) -> p o e", o=1).to_broadcast([S, E, E]),
                                     below[:], ALU.mult))
                do(vec.tensor_reduce(start[:], before[:], AX.X, ALU.add))
                if first_tile:
                    do(vec.tensor_scalar(start[:], start[:], float(first_tile), None, ALU.add))
                do(vec.scalar_tensor_tensor(place[:], start[:].rearrange("p (o e) -> p o e", o=1).to_broadcast([S, B, E]),
                                            float(TOK), psum[1][0:S, 0:B * E].rearrange("p (b e) -> p b e", b=B),
                                            ALU.mult, ALU.add))
                for hot in (one, two):
                    do.apart(vec.tensor_tensor(hot[:], hot[:], place[:], ALU.mult))
                do.catch_up()
                for n, hot in enumerate((one, two)):
                    do.apart(vec.tensor_reduce(slf[:, n, :], hot[:], AX.X, ALU.add))
                do.catch_up()
                do(vec.tensor_copy(slots[:], slf[:]))
                do(vec.tensor_tensor(used[:], used[:], start[:], ALU.add))
                do(vec.tensor_tensor(past[:], used[:].rearrange("p (o e) -> p o e", o=1).to_broadcast([S, tiles, E]),
                                     order[:].rearrange("p (t o) -> p t o", o=1).to_broadcast([S, tiles, E]), ALU.is_le))
                do(vec.tensor_reduce(tef[:], past[:], AX.X, ALU.add))
                do(vec.tensor_scalar(tef[:], tef[:], float(E - 1), None, ALU.min))
                if first_tile:
                    do(vec.memset(tef[:, 0:first_tile], float(E)))
                do(vec.tensor_copy(tile_expert[:], tef[:]))


def experts(core, dram, tag, X, XN, ident, slots, w, tile_expert, rows_in, rows_out, E, NU, TR, NT, tiles, first_tile, BUFS,
            finish):
    nc, psum = core.nc, core.psum
    I = TR * NT
    HT = TOK // P
    LAG = 2
    HB = 3
    XB, YB = HB, HB + 1
    RING = 4
    LOOPS, REST = divmod(tiles - max(first_tile, 1), BUFS)
    assert REST >= 1 and max(first_tile - 1, 0) % BUFS == 0 and BUFS * NT % HB == 0 and YB + BUFS <= 8
    with ExitStack() as ctx:
        stage_u = [fixed(ctx, nc, f"{tag}stage_u{u}", [P, KD, NU, I]) for u in range(BUFS)]
        stage_d = [fixed(ctx, nc, f"{tag}stage_d{u}", [TR, NT, D]) for u in range(BUFS)]
        UH = [fixed(ctx, nc, f"{tag}UH{u}", [P, KD, NU, I], F32R) for u in range(BUFS)]
        UL = [fixed(ctx, nc, f"{tag}UL{u}", [P, KD, NU, I], F32R) for u in range(BUFS)]
        DH = [fixed(ctx, nc, f"{tag}DH{u}", [TR, NT, D], F32R) for u in range(BUFS)]
        DL = [fixed(ctx, nc, f"{tag}DL{u}", [TR, NT, D], F32R) for u in range(BUFS)]
        xg = [fixed(ctx, nc, f"{tag}xg{u}", [P, HT, D]) for u in range(BUFS)]
        xh = [fixed(ctx, nc, f"{tag}xh{u}", [P, KD, TOK], F32R) for u in range(BUFS)]
        xl = [fixed(ctx, nc, f"{tag}xl{u}", [P, KD, TOK], F32R) for u in range(BUFS)]
        ys = [fixed(ctx, nc, f"{tag}ys{u}", [P, HT, D]) for u in range(BUFS)]
        G = fixed(ctx, nc, tag + "G", [TR, HB, TOK])
        HF = fixed(ctx, nc, tag + "HF", [TR, HB, TOK])
        HH = [fixed(ctx, nc, f"{tag}HH{u}", [TR, NT, TOK], F32R) for u in range(BUFS)]
        HL = [fixed(ctx, nc, f"{tag}HL{u}", [TR, NT, TOK], F32R) for u in range(BUFS)]
        back = fixed(ctx, nc, tag + "back", [S, RING, 2, D])
        shared = fixed(ctx, nc, tag + "shared", [S, B, D]) if first_tile else None
        scattered = core.sem(tag + "scattered")
        w_in = [core.sem(f"{tag}w_in{u}") for u in range(BUFS)]
        x_in = [core.sem(f"{tag}x_in{u}") for u in range(BUFS)]
        w_hi = core.sem(tag + "w_hi")
        ul_ready = core.sem(tag + "ul")
        dl_ready = core.sem(tag + "dl")
        turned = core.sem(tag + "turned")
        xh_ready = core.sem(tag + "xh")
        xl_ready = core.sem(tag + "xl")
        up_ready = core.sem(tag + "up")
        g_ready = core.sem(tag + "g")
        h_ready = core.sem(tag + "h")
        hh_ready = core.sem(tag + "hh")
        hl_ready = core.sem(tag + "hl")
        down_done = core.sem(tag + "down")
        y_done = core.sem(tag + "y")
        stored = [core.sem(f"{tag}stored{u}") for u in range(BUFS)]
        back_in = [core.sem(f"{tag}back{i}") for i in range(RING)]
        shared_in = core.sem(tag + "shared_in")
        first_in = core.sem(tag + "first_in")
        added = core.sem(tag + "added")

        def steps(eng, body):
            body(0, 0, 0)
            if first_tile:
                with eng.Fori(0, (first_tile - 1) // BUFS) as i:
                    for u in range(BUFS):
                        body(i * BUFS + (1 + u), (1 + u) % BUFS, i + (1 + u) // BUFS)
            base = max(first_tile, 1)
            with eng.Fori(0, LOOPS) as i:
                for u in range(BUFS):
                    k = base + u
                    body(i * BUFS + k, k % BUFS, i + k // BUFS)
            for k in range(base + LOOPS * BUFS, tiles):
                body(k, k % BUFS, k // BUFS)

        def is_last(k):
            return isinstance(k, int) and k == tiles - 1

        def next_of(u, m):
            return (u + 1) % BUFS, m + (u + 1) // BUFS

        with nc.Block() as block:

            @block.sync
            def _(sp):
                BEHIND = BUFS + 1
                HEAD = first_tile + BEHIND

                def load(k, u):
                    load_weights(k, u)
                    load_rows(k, u)

                def load_weights(k, u):
                    last_expert = E if first_tile else E - 1
                    e = bass.ds(sp.value_load(tile_expert[0:1, bass.ds(k, 1)], min_val=0, max_val=last_expert), 1)
                    sp.wait_ge(ul_ready, k + 1)
                    sp.wait_ge(dl_ready, k + 1)
                    sp.dma_start(stage_u[u][:].rearrange("p k n i -> p (k n i)"),
                                 dram[tag + "up"][e].rearrange("o p k n i -> p (o k n i)")).then_inc(w_in[u], 16)
                    sp.dma_start(stage_d[u][:].rearrange("p t d -> p (t d)"),
                                 dram[tag + "down"][e].rearrange("o p t d -> p (o t d)")).then_inc(w_in[u], 16)

                def load_rows(k, u):
                    sp.wait_ge(turned, k + 1)
                    sp.dma_start(xg[u][:], rows_in[bass.ts(k, TOK)].rearrange("(j p) d -> p j d", p=P)).then_inc(x_in[u], 16)

                def store(k, u):
                    sp.wait_ge(y_done, k + (BUFS + 1))
                    sp.dma_start(rows_out[bass.ts(k, TOK)].rearrange("(j p) d -> p j d", p=P), ys[u][:]).then_inc(stored[u], 16)

                for s in stored:
                    sp.sem_inc(s, 16)
                for k in range(BUFS):
                    load_weights(k, k)
                for k in range(HEAD):
                    if k >= BUFS:
                        load_weights(k, k % BUFS)
                    if k == first_tile:
                        sp.wait_ge(scattered, 16 * 2 * B)
                    load_rows(k, k % BUFS)
                    if k >= BEHIND:
                        store(k - BEHIND, (k - BEHIND) % BUFS)
                rounds = (tiles - HEAD) // BUFS
                with sp.Fori(0, rounds) as i:
                    for k in range(HEAD, HEAD + BUFS):
                        load(i * BUFS + k, k % BUFS)
                        store(i * BUFS + (k - BEHIND), (k - BEHIND) % BUFS)
                for k in range(HEAD + rounds * BUFS, tiles + BEHIND):
                    if k < tiles:
                        load(k, k % BUFS)
                    store(k - BEHIND, (k - BEHIND) % BUFS)
                for u, s in enumerate(stored):
                    sp.wait_ge(s, 16 * (1 + len(range(u, tiles, BUFS))))
                if first_tile:
                    sp.dma_start(shared[:], rows_out[0:B * S].rearrange("(b s) d -> s b d", b=B)).then_inc(shared_in, 16)
                    sp.wait_ge(shared_in, 16)
                if finish:
                    finish(sp, added)

            @block.gpsimd
            def _(pool):
                pool.sem_inc(dl_ready, BUFS)

                def scatter(i):
                    n, b = divmod(i, B)
                    pool.indirect_dma_start(rows_in[:, :], bass.IndirectOffsetOnAxis(slots[:, n, b:b + 1], 0),
                                            XN[:, b, :], None).then_inc(scattered, 16)

                def split(k, u):
                    pool.wait_ge(w_hi, k * (KD + 1) + (KD + 1))
                    nc.gpsimd.tensor_tensor(DL[u][:], stage_d[u][:], as_f32(DH[u][:]), ALU.subtract).then_inc(dl_ready, 1)

                SHARE = -(-2 * B // max(first_tile - 3, 1))
                for k in range(first_tile):
                    split(k, k % BUFS)
                    for i in range(SHARE * k, min(SHARE * (k + 1), 2 * B)):
                        scatter(i)
                if not first_tile:
                    for i in range(2 * B):
                        scatter(i)
                    split(0, 0)
                base = max(first_tile, 1)
                with pool.Fori(0, LOOPS) as i:
                    for k in range(base, base + BUFS):
                        split(i * BUFS + k, k % BUFS)
                for k in range(base + LOOPS * BUFS, tiles):
                    split(k, k % BUFS)
                for u, s in enumerate(stored):
                    pool.wait_ge(s, 16 * (1 + len(range(u, tiles, BUFS))))
                for b in range(B):
                    if b >= RING:
                        pool.wait_ge(added, b - RING + 1)
                    for n in range(2):
                        pool.indirect_dma_start(back[:, b % RING, n, :], None, rows_out[0:tiles * TOK, :],
                                                bass.IndirectOffsetOnAxis(slots[:, n, b:b + 1], 0)).then_inc(back_in[b % RING], 16)

            @block.tensor
            def _(pe):
                pe.sem_inc(down_done, BUFS * NT)
                pe.sem_inc(turned, BUFS)

                def turn(k, u, m):
                    pe.wait_ge(x_in[u], m * 16 + 16)
                    if not isinstance(k, int) or k >= 1:
                        pe.wait_ge(xl_ready, k)
                    for q in range(KD):
                        for j in range(HT):
                            last = nc.tensor.transpose(psum[XB][:, (q * HT + j) * P:(q * HT + j + 1) * P],
                                                       xg[u][:, j, q * P:(q + 1) * P], ident[:, :])
                    last.then_inc(turned, 1)

                def up(k, u, t):
                    if t == 0:
                        pe.wait_ge(xl_ready, k + 1)
                        pe.wait_ge(ul_ready, k + (BUFS + 1))
                    pe.wait_ge(h_ready, k * NT + (t + 1))
                    cols = slice(t * TR, (t + 1) * TR)
                    for n in range(NU):
                        last = split_products(nc, psum[(u * NT + t) % HB][0:TR, n * TOK:(n + 1) * TOK],
                                              [(UH[u][:, q, n, cols], UL[u][:, q, n, cols], xh[u][:, q, :], xl[u][:, q, :])
                                               for q in range(KD)])
                    last.then_inc(up_ready, 1)

                def down(k, u, t):
                    pe.wait_ge(hl_ready, k * NT + (HB + t + 1))
                    if t == 0:
                        pe.wait_ge(dl_ready, k + (BUFS + 1))
                        pe.wait_ge(y_done, k + 1)
                    for j in range(HT):
                        rows = slice(j * P, (j + 1) * P)
                        last = split_products(nc, psum[YB + u][:, j * D:(j + 1) * D],
                                              [(HH[u][:, t, rows], HL[u][:, t, rows], DH[u][:, t, :], DL[u][:, t, :])],
                                              first=t == 0 and j == 0, last=t == NT - 1 and j == HT - 1)
                    last.then_inc(down_done, 1)

                def step(k, u, m):
                    if NT == LAG and not is_last(k):
                        turn(k + 1, *next_of(u, m))
                    for t in range(NT):
                        up(k, u, t)
                        if t >= LAG:
                            down(k, u, t - LAG)
                        elif not isinstance(k, int) or k >= 1:
                            down(k - 1, (u - 1) % BUFS, NT - LAG + t)
                        if t == 1 and NT > LAG and not is_last(k):
                            turn(k + 1, *next_of(u, m))

                turn(0, 0, 0)
                steps(pe, step)
                for t in range(NT - LAG, NT):
                    down(tiles - 1, (tiles - 1) % BUFS, t)

            @block.scalar
            def _(act):
                if NU == 1:
                    act.sem_inc(h_ready, HB)

                def rows_high(k, u):
                    act.wait_ge(turned, k + (BUFS + 1))
                    if not isinstance(k, int) or k >= 2:
                        act.wait_ge(up_ready, (k - 1) * NT)
                    nc.scalar.activation(xh[u][:], psum[XB][:, 0:KD * TOK].rearrange("p (k t) -> p k t", k=KD),
                                         ACT.Copy).then_inc(xh_ready, 1)

                def weights_high(k, u, m, part):
                    if part == 0:
                        act.wait_ge(w_in[u], m * 32 + 32)
                        if not isinstance(k, int) or k >= 2:
                            act.wait_ge(up_ready, (k - 1) * NT)
                    if part == KD:
                        act.wait_ge(down_done, k * NT + NT)
                    if part < KD:
                        nc.scalar.activation(UH[u][:, part], stage_u[u][:, part], ACT.Copy).then_inc(w_hi, 1)
                    else:
                        nc.scalar.activation(DH[u][:], stage_d[u][:], ACT.Copy).then_inc(w_hi, 1)

                def step(k, u, m):
                    def gate(t):
                        act.wait_ge(up_ready, k * NT + (t + 1))
                        src, b = psum[(u * NT + t) % HB][0:TR, 0:TOK], (u * NT + t) % HB
                        if NU == 2:
                            act.wait_ge(h_ready, k * NT + (t + 1))
                            nc.scalar.activation(G[:, b, :], src, ACT.Silu).then_inc(g_ready, 1)
                        else:
                            act.wait_ge(hl_ready, k * NT + (t + 1))
                            nc.scalar.activation(HF[:, b, :], src, ACT.Silu).then_inc(h_ready, 1)

                    def high(t):
                        act.wait_ge(h_ready, k * NT + (HB + t + 1))
                        act.wait_ge(down_done, k * NT + (t + 1))
                        nc.scalar.activation(HH[u][:, t, :], HF[:, (u * NT + t) % HB, :], ACT.Copy).then_inc(hh_ready, 1)

                    if NT == LAG and not is_last(k):
                        rows_high(k + 1, next_of(u, m)[0])
                    for t in range(NT + 1):
                        if t < NT:
                            gate(t)
                        if t >= 1:
                            high(t - 1)
                        if not is_last(k):
                            un, mn = next_of(u, m)
                            for part in range(KD + 1):
                                if ACT_AT[part] == t:
                                    weights_high(k + 1, un, mn, part)
                            if t == 2 and NT > LAG:
                                rows_high(k + 1, un)

                ACT_AT = (0, 1, 3) if NT > 2 else (0, 0, 0)
                for part in range(KD + 1):
                    weights_high(0, 0, 0, part)
                rows_high(0, 0)
                steps(act, step)

            @block.vector
            def _(v):
                if NU == 2:
                    v.sem_inc(h_ready, HB)
                v.sem_inc(hl_ready, HB)
                v.sem_inc(ul_ready, BUFS)
                v.sem_inc(y_done, BUFS)

                def rows_low(k, u):
                    v.wait_ge(xh_ready, k + 1)
                    nc.vector.tensor_tensor(xl[u][:], psum[XB][:, 0:KD * TOK].rearrange("p (k t) -> p k t", k=KD),
                                            as_f32(xh[u][:]), ALU.subtract).then_inc(xl_ready, 1)

                def weights_low(k, u, part):
                    v.wait_ge(w_hi, k * (KD + 1) + (part + 1))
                    ins = nc.vector.tensor_tensor(UL[u][:, part], stage_u[u][:, part], as_f32(UH[u][:, part]), ALU.subtract)
                    if part == KD - 1:
                        ins.then_inc(ul_ready, 1)

                def sums_out(k, u, m):
                    v.wait_ge(down_done, k * NT + (BUFS * NT + NT))
                    v.wait_ge(stored[u], m * 16 + 16)
                    nc.vector.tensor_copy(ys[u][:].rearrange("p j d -> p (j d)"), psum[YB + u][:, 0:HT * D]).then_inc(y_done, 1)

                def step(k, u, m):
                    def hidden(t):
                        b = (u * NT + t) % HB
                        v.wait_ge(g_ready, k * NT + (t + 1))
                        v.wait_ge(hl_ready, k * NT + (t + 1))
                        nc.vector.tensor_tensor(HF[:, b, :], psum[b][0:TR, TOK:2 * TOK], G[:, b, :], ALU.mult).then_inc(h_ready, 1)

                    def low(t):
                        v.wait_ge(hh_ready, k * NT + (t + 1))
                        nc.vector.tensor_tensor(HL[u][:, t, :], HF[:, (u * NT + t) % HB, :], as_f32(HH[u][:, t, :]),
                                                ALU.subtract).then_inc(hl_ready, 1)

                    if NT == LAG and not is_last(k):
                        rows_low(k + 1, next_of(u, m)[0])
                        for part in range(KD):
                            weights_low(k + 1, next_of(u, m)[0], part)
                    for t in range(NT + 1):
                        if t < NT and NU == 2:
                            hidden(t)
                        if t >= 1:
                            low(t - 1)
                        if NT > LAG and not is_last(k):
                            un, mn = next_of(u, m)
                            for part in range(KD):
                                if DVE_AT[part] == t:
                                    weights_low(k + 1, un, part)
                            if t == 3:
                                rows_low(k + 1, un)
                        if t == min(3, NT) and (not isinstance(k, int) or k >= 1):
                            sums_out(k - 1, (u - 1) % BUFS, m if u else m - 1)

                DVE_AT = (1, 2)
                for part in range(KD):
                    weights_low(0, 0, part)
                rows_low(0, 0)
                steps(v, step)
                k = tiles - 1
                sums_out(k, k % BUFS, k // BUFS)
                if first_tile:
                    v.wait_ge(shared_in, 16)
                    nc.vector.tensor_tensor(X[:], X[:], shared[:], ALU.add).then_inc(first_in, 1)
                    v.wait_ge(first_in, 1)
                for b in range(B):
                    v.wait_ge(back_in[b % RING], 32 * (b // RING + 1))
                    for n in range(2):
                        ins = nc.vector.scalar_tensor_tensor(X[:, b, :], back[:, b % RING, n, :], w[:, 2 + n, b:b + 1],
                                                             X[:, b, :], ALU.mult, ALU.add)
                        ins.then_inc(added if n else first_in, 1)
                        if not n:
                            v.wait_ge(first_in, b + 1 + (1 if first_tile else 0))
                    if b and not finish:
                        v.wait_ge(added, b)
                        core.batch_stats(X, b - 1)


def moe(core, dram, tag, X, ident, rows_in, rows_out, E, NU, TR, NT, tiles, first_tile, BUFS, grouped, finish=None):
    nc = core.nc
    with ExitStack() as ctx:
        XN = fixed(ctx, nc, tag + "XN", [S, B, D])
        slots = fixed(ctx, nc, tag + "slots", [S, 2, B], U32)
        w = fixed(ctx, nc, tag + "w", [S, 4, B])
        tile_expert = fixed(ctx, nc, tag + "tile_expert", [S, tiles], U32)
        with ExitStack() as stage:
            XH = fixed(stage, nc, tag + "XH", [P, KD, B * S], F32R)
            XL = fixed(stage, nc, tag + "XL", [P, KD, B * S], F32R)
            inputs = RouterInputs(core, stage, dram, tag, E, tiles)
            plain = core.sem(tag + "plain")

            def plain_rows(sp):
                if first_tile:
                    sp.dma_start(rows_in[0:B * S].rearrange("(b s) d -> s b d", b=B), XN[:]).then_inc(plain, 16)
                    sp.wait_ge(plain, 16)

            layernorm(core, tag + "ln_", X, XN, ident, XH, XL, B - 1, inputs.load)
            route(core, inputs, tag, ident, XH, XL, E, slots, w, tile_expert, tiles, first_tile, grouped, plain_rows)
        experts(core, dram, tag, X, XN, ident, slots, w, tile_expert, rows_in, rows_out, E, NU, TR, NT, tiles, first_tile, BUFS,
                finish)


def gated_moe(core, dram, X, ident, rows_in, rows_out):
    moe(core, dram, "m0_", X, ident, rows_in, rows_out, E0, 2, 116, 6, most_tiles(E0), 0, 2, grouped=False)


def grouped_moe(core, dram, X, ident, rows_in, rows_out, finish=None):
    first = -(-B * S // TOK)
    moe(core, dram, "m1_", X, ident, rows_in, rows_out, E1, 1, 88, 2, first + most_tiles(E1), first, 3, grouped=True,
        finish=finish)


def causal_attention(core, dram, X, ident):
    nc, psum = core.nc, core.psum
    HT = H // KD
    SCALE = HD ** -0.5
    with ExitStack() as ctx:
        XH = fixed(ctx, nc, "XH_c", [P, KD, B * S], F32R)
        XL = fixed(ctx, nc, "XL_c", [P, KD, B * S], F32R)
        wq = fixed(ctx, nc, "c_wq", [P, KD, D])
        wqh = fixed(ctx, nc, "c_wqh", [P, KD, D], F32R)
        wql = fixed(ctx, nc, "c_wql", [P, KD, D], F32R)
        wk = fixed(ctx, nc, "c_wk", [DC, D])
        wv = fixed(ctx, nc, "c_wv", [DC, D])
        wo = fixed(ctx, nc, "c_wo", [P, KD, D])
        lat = fixed(ctx, nc, "c_lat", [DC, B * S])
        mask = fixed(ctx, nc, "c_mask", [S, S])
        maskb = fixed(ctx, nc, "c_maskb", [S, S], BF16)
        identb = fixed(ctx, nc, "c_identb", [S, S], BF16)
        blocks = fixed(ctx, nc, "c_blocks", [P, HT])
        QT = fixed(ctx, nc, "c_QT", [P, KD, B * S])
        KTT = fixed(ctx, nc, "c_KT", [P, KD, B * S])
        V = fixed(ctx, nc, "c_V", [S, B, D])

        loaded = core.sem("ca_loaded")

        latents_in = core.sem("ca_latents")
        k_proj = core.sem("ca_kproj")
        k_moved = core.sem("ca_kmoved")

        def loads(sp):
            for t, name in ((lat, "c_lat"), (wk, "c_wk"), (wv, "c_wv")):
                sp.dma_start(t[:], dram[name]).then_inc(latents_in, 16)
            for t, name in ((wq, "c_wq"), (wo, "c_wo"), (mask, "c_mask"), (blocks, "c_blocks")):
                sp.dma_start(t[:], dram[name]).then_inc(loaded, 16)

        def project_keys(pe):
            pe.wait_ge(latents_in, 48)
            for n in range(NC * KD):
                c, k = divmod(n, KD)
                nc.tensor.matmul(psum[n][:, 0:CH], wk[:, k * P:(k + 1) * P], lat[:, c * CH:(c + 1) * CH],
                                 start=True, stop=True).then_inc(k_proj, 1)
            pe.wait_ge(k_moved, NC * KD)

        def move_keys(act):
            for n in range(NC * KD):
                c, k = divmod(n, KD)
                act.wait_ge(k_proj, n + 1)
                nc.scalar.activation(KTT[:, k, c * CH:(c + 1) * CH], psum[n][:, 0:CH], ACT.Copy).then_inc(k_moved, 1)

        with ExitStack() as stage:
            XN = fixed(stage, nc, "XN_c", [S, B, D])
            layernorm(core, "ln2_", X, XN, ident, XH, XL, B - 1, loads,
                      (project_keys, move_keys))

        parts = core.sem("ca_parts")
        chain = core.sem("ca_chain")
        proj = core.sem("ca_proj")
        moved_a = core.sem("ca_moveda")
        moved_v = core.sem("ca_movedv")
        tiles = [("v", b, 0) for b in range(B)] + [("q", k, c) for c in range(NC) for k in range(KD)]

        def place(n):
            kind, k, c = tiles[n]
            if kind == "v":
                return V[:, k, :], psum[n % 8][0:S, 0:D]
            return QT[:, k, c * CH:(c + 1) * CH], psum[n % 8][:, 0:CH]

        with nc.Block() as block:

            @block.tensor
            def _(pe):
                for n, (kind, k, c) in enumerate(tiles):
                    if n >= 8:
                        pe.wait_ge(moved_v if n % 2 else moved_a, (n - 8) // 2 + 1)
                    if n == B:
                        pe.wait_ge(parts, 1)
                    out = psum[n % 8]
                    cols = slice(c * CH, (c + 1) * CH)
                    if kind == "q":
                        last = split_products(nc, out[:, 0:CH], [(wqh[:, j, k * P:(k + 1) * P], wql[:, j, k * P:(k + 1) * P],
                                                                  XH[:, j, cols], XL[:, j, cols]) for j in range(KD)])
                    else:
                        last = nc.tensor.matmul(out[0:S, 0:D], lat[:, k * S:(k + 1) * S], wv[:], start=True, stop=True)
                    last.then_inc(proj, 1)

            @block.scalar
            def _(act):
                for n in range(0, len(tiles), 2):
                    act.wait_ge(proj, n + 1)
                    nc.scalar.activation(*place(n), ACT.Copy).then_inc(moved_a, 1)

            @block.vector
            def _(v):
                do = Chain(v, chain)
                v.wait_ge(loaded, 16 * 4)
                do(nc.vector.tensor_copy(wqh[:], wq[:]))
                nc.vector.tensor_tensor(wql[:], wq[:], as_f32(wqh[:]), ALU.subtract).then_inc(parts, 1)
                nc.vector.tensor_copy(maskb[:], mask[:])
                nc.vector.tensor_copy(identb[:], ident[0:S, 0:S])
                for n in range(1, len(tiles), 2):
                    v.wait_ge(proj, n + 1)
                    nc.vector.tensor_copy(*place(n)).then_inc(moved_v, 1)

        qb = [fixed(ctx, nc, f"c_qb{u}", [P, S]) for u in range(2)]
        kb = [fixed(ctx, nc, f"c_kb{u}", [P, HT, S]) for u in range(2)]
        nmax = [fixed(ctx, nc, f"c_nmax{u}", [S, 2, HT]) for u in range(2)]
        sums = fixed(ctx, nc, "c_sums", [S, 2, H])
        rsum = fixed(ctx, nc, "c_rsum", [S, H])
        PR = [fixed(ctx, nc, f"c_PR{u}", [S, HT, S]) for u in range(2)]
        PT = [fixed(ctx, nc, f"c_PT{u}", [S, HT, S]) for u in range(2)]
        O = fixed(ctx, nc, "c_O", [S, D])
        OT = fixed(ctx, nc, "c_OT", [P, KD, S])
        HB = HT // 2
        SC, TB, OB, LB = 0, 4, 6, 7

        ops_ready = core.sem("cb_ops")
        s_ready = core.sem("cb_s")
        max_ready = core.sem("cb_max")
        neg_ready = core.sem("cb_neg")
        e_ready = core.sem("cb_e")
        t_ready = core.sem("cb_t")
        tc_act = core.sem("cb_tca")
        tc_dve = core.sem("cb_tcv")
        o_ready = core.sem("cb_o")
        r_ready = core.sem("cb_r")
        on_ready = core.sem("cb_on")
        ot_ready = core.sem("cb_ot")
        otc_ready = core.sem("cb_otc")
        y_ready = core.sem("cb_y")
        x_done = core.sem("cb_x")

        def steps(eng, body):
            for i in (0, 1):
                body(i, i % 2)
            with eng.Fori(0, (B - 4) // 2) as j:
                for w in range(2):
                    body(j * 2 + (2 + w), w)
            for i in range(B - 2, B + 2):
                body(i, i % 2)

        def has(i, first, last):
            return not isinstance(i, int) or first <= i <= last

        def bank_heads(ap):
            return ap.rearrange("p (h s) -> p h s", s=S)

        with nc.Block() as block:

            @block.tensor
            def _(pe):
                def scores(i, u):
                    n = i * 2 + u
                    pe.wait_ge(ops_ready, n + 1)
                    if has(i, 1, B):
                        pe.wait_ge(e_ready, n * HT - HT)
                    for g in range(2):
                        out = psum[SC + 2 * u + g][0:S, 0:HB * S]
                        nc.tensor.matmul(out, qb[u][:], kb[u][:, g * HB:(g + 1) * HB, :].rearrange("p h s -> p (h s)"),
                                         start=True, stop=False)
                        last = nc.tensor.matmul(out, identb[:],
                                                maskb[:].rearrange("p (o s) -> p o s", o=1).to_broadcast([S, HB, S]),
                                                start=False, stop=True)
                    last.then_inc(s_ready, 1)

                def turn(n, u, first):
                    pe.wait_ge(e_ready, n * HT + HT)
                    if not first:
                        pe.wait_ge(tc_act, n)
                        pe.wait_ge(tc_dve, n)
                    for h in range(HT):
                        ins = nc.tensor.transpose(psum[TB + h // HB][0:S, (h % HB) * S:(h % HB + 1) * S], PR[u][:, h, :],
                                                  ident[0:S, 0:S])
                        if h % HB == HB - 1:
                            ins.then_inc(t_ready, 1)

                def values(i, n, u):
                    pe.wait_ge(tc_act, n + 1)
                    pe.wait_ge(tc_dve, n + 1)
                    if u == 0 and has(i, 2, B):
                        pe.wait_ge(on_ready, i - 1)
                    for h in range(HT):
                        d = (u * HT + h) * HD
                        last = nc.tensor.matmul(psum[OB][0:S, d:d + HD], PT[u][:, h, :], V[:, i - 1, d:d + HD],
                                                start=True, stop=True)
                    last.then_inc(o_ready, 1)

                def step(i, w):
                    n = i * 2
                    if has(i, 0, B - 1):
                        scores(i, 0)
                    if has(i, 2, B + 1):
                        pe.wait_ge(on_ready, i - 1)
                        if has(i, 3, B + 1):
                            pe.wait_ge(x_done, i - 1)
                        for k in range(KD):
                            last = nc.tensor.transpose(psum[LB][:, k * S:(k + 1) * S], O[:, k * P:(k + 1) * P], ident[0:S, 0:S])
                        last.then_inc(ot_ready, 1)
                    if has(i, 1, B):
                        turn(n - 1, 1, False)
                        values(i, n - 2, 0)
                    if has(i, 0, B - 1):
                        scores(i, 1)
                        turn(n, 0, isinstance(i, int) and i == 0)
                    if has(i, 2, B + 1):
                        pe.wait_ge(otc_ready, i - 1)
                        for k in range(KD):
                            last = nc.tensor.matmul(psum[LB][0:S, 0:D], OT[:, k, :], wo[:, k, :], start=k == 0, stop=k == KD - 1)
                        last.then_inc(y_ready, 1)
                    if has(i, 1, B):
                        values(i, n - 1, 1)
                pe.sem_inc(y_ready, 1)
                steps(pe, step)

            @block.scalar
            def _(act):
                def exps(i, u, w):
                    n = i * 2 + u
                    act.wait_ge(neg_ready, n + 1)
                    if has(i, 1, B):
                        act.wait_ge(t_ready, n * 2 - 2)
                    if has(i, 2, B):
                        act.wait_ge(r_ready, i - 1)
                    for h in range(HT):
                        nc.scalar.activation(PR[u][:, h, :], psum[SC + 2 * u + h // HB][0:S, (h % HB) * S:(h % HB + 1) * S],
                                             ACT.Exp, bias=nmax[u][:, 1, h:h + 1], scale=SCALE,
                                             accum_out=sums[:, w, u * HT + h:u * HT + h + 1]).then_inc(e_ready, 1)

                def move(n, u):
                    act.wait_ge(t_ready, n * 2 + 2)
                    nc.scalar.activation(PT[u][:, 0:HB, :], bank_heads(psum[TB][0:S, 0:HB * S]), ACT.Copy).then_inc(tc_act, 1)

                def step(i, w):
                    n = i * 2
                    if has(i, 0, B - 1):
                        exps(i, 0, w)
                    if has(i, 1, B):
                        move(n - 1, 1)
                    if has(i, 2, B + 1):
                        act.wait_ge(ot_ready, i - 1)
                        if has(i, 3, B + 1):
                            act.wait_ge(y_ready, i - 1)
                        nc.scalar.activation(OT[:], bank_heads(psum[LB][:, 0:KD * S]), ACT.Copy).then_inc(otc_ready, 1)
                    if has(i, 0, B - 1):
                        exps(i, 1, w)
                        move(n, 0)
                steps(act, step)

            @block.vector
            def _(v):
                def operands(i, u):
                    n = i * 2 + u
                    if has(i, 1, B):
                        v.wait_ge(s_ready, n - 1)
                    nc.vector.tensor_tensor(kb[u][:], KTT[:, u:u + 1, bass.ts(i, S)].to_broadcast([P, HT, S]),
                                            blocks[:].rearrange("p (h o) -> p h o", o=1).to_broadcast([P, HT, S]), ALU.mult)
                    nc.vector.tensor_copy(qb[u][:], QT[:, u, bass.ts(i, S)]).then_inc(ops_ready, 1)

                def maxima(i, u):
                    n = i * 2 + u
                    v.wait_ge(s_ready, n + 1)
                    if has(i, 1, B):
                        v.wait_ge(e_ready, n * HT - HT)
                    for g in range(2):
                        nc.vector.tensor_reduce(nmax[u][:, 0, g * HB:(g + 1) * HB],
                                                bank_heads(psum[SC + 2 * u + g][0:S, 0:HB * S]), AX.X,
                                                ALU.max).then_inc(max_ready, 1)
                    v.wait_ge(max_ready, n * 2 + 2)
                    nc.vector.tensor_scalar(nmax[u][:, 1, :], nmax[u][:, 0, :], -SCALE, None, ALU.mult).then_inc(neg_ready, 1)

                def move(n, u):
                    v.wait_ge(t_ready, n * 2 + 2)
                    nc.vector.tensor_copy(PT[u][:, HB:, :], bank_heads(psum[TB + 1][0:S, 0:HB * S])).then_inc(tc_dve, 1)

                v.sem_inc(x_done, 1)
                operands(0, 0)
                operands(0, 1)

                def step(i, w):
                    n = i * 2
                    if has(i, 0, B - 1):
                        maxima(i, 0)
                    if has(i, 0, B - 2):
                        operands(i + 1, 0)
                    if has(i, 1, B):
                        move(n - 1, 1)
                    if has(i, 0, B - 1):
                        maxima(i, 1)
                    if has(i, 0, B - 2):
                        operands(i + 1, 1)
                    if has(i, 0, B - 1):
                        move(n, 0)
                    if isinstance(i, int) and i == B + 1:
                        v.wait_ge(x_done, B)
                        for b in range(B - 1):
                            core.batch_stats(X, b)
                    if has(i, 2, B + 1):
                        v.wait_ge(y_ready, i)
                        nc.vector.tensor_tensor(X[:, i - 2, :], psum[LB][0:S, 0:D], X[:, i - 2, :], ALU.add).then_inc(x_done, 1)
                    if has(i, 1, B):
                        if has(i, 2, B):
                            v.wait_ge(on_ready, i - 1)
                        v.wait_ge(e_ready, n * HT)
                        nc.vector.reciprocal(rsum[:], sums[:, 1 - w, :]).then_inc(r_ready, 1)
                        v.wait_ge(r_ready, i)
                        v.wait_ge(o_ready, n)
                        if has(i, 2, B):
                            v.wait_ge(ot_ready, i - 1)
                        nc.vector.tensor_tensor(O[:].rearrange("p (h d) -> p h d", h=H),
                                                psum[OB][0:S, 0:D].rearrange("p (h d) -> p h d", h=H),
                                                rsum[:].rearrange("p (h o) -> p h o", o=1).to_broadcast([S, H, HD]),
                                                ALU.mult).then_inc(on_ready, 1)
                steps(v, step)


def model(nc, dram, out):
    with ExitStack() as ctx:
        core = Core(nc, ctx)
        X = fixed(ctx, nc, "X", [S, B, D])
        ident = fixed(ctx, nc, "ident", [P, P])
        loaded = core.sem("loaded")
        queries = nc.dram_tensor("queries", (B, P, H, S), F32).ap()
        recips = nc.dram_tensor("recips", (B, H, S), F32).ap()
        rows_in = nc.dram_tensor("rows_in", (ROWS, D), F32).ap()
        rows_out = nc.dram_tensor("rows_out", (ROWS, D), F32).ap()
        with nc.Block() as block:

            @block.sync
            def _(sp):
                sp.dma_start(X[:], dram["x"].rearrange("b s d -> s b d")).then_inc(loaded, 16)
                sp.dma_start(ident[:], dram["ident"]).then_inc(loaded, 16)
                sp.wait_ge(loaded, 32)

        with ExitStack() as layer:
            BB = fixed(layer, nc, "BB", [P, H // 2, D])
            with ExitStack() as stage:
                XH = fixed(stage, nc, "XH_a", [P, KD, B * S], F32R)
                XL = fixed(stage, nc, "XL_a", [P, KD, B * S], F32R)
                AH = fixed(stage, nc, "AH", [P, KD, H, DQ], F32R)
                AL = fixed(stage, nc, "AL", [P, KD, H, DQ], F32R)
                M2 = fixed(stage, nc, "M2", [HALF, 2, H, P])
                with ExitStack() as norm:
                    XN = fixed(norm, nc, "XN_a", [S, B, D])
                    weights = FoldInputs(core, norm, dram)
                    layernorm(core, "ln0_", X, XN, ident, XH, XL, 0, weights.load)
                    fold_weights(core, weights, AH, AL, M2, BB)
                latent_queries(core, dram, XH, XL, AH, AL, M2, queries, rows_in)
            latent_attention(core, dram, X, ident, queries, recips, BB)
        core.release()
        gated_moe(core, dram, X, ident, rows_in, rows_out)
        causal_attention(core, dram, X, ident)
        core.release()

        def store(sp, done):
            stored = core.sem("stored")
            for b in range(B):
                sp.wait_ge(done, b + 1)
                sp.dma_start(out[b], X[:, b, :]).then_inc(stored, 16)
            sp.wait_ge(stored, 16 * B)

        grouped_moe(core, dram, X, ident, rows_in, rows_out, store)


def rope_tables(length, dim):
    import numpy as np
    inv = (np.float32(1.0) / np.power(np.float32(10000.0), np.arange(0, dim, 2, dtype=np.float32) / np.float32(dim)))
    f = np.arange(length, dtype=np.float32)[:, None] * inv.astype(np.float32)[None, :]
    return np.repeat(np.sin(f), 2, axis=-1), np.repeat(np.cos(f), 2, axis=-1)


def layouts(inputs):
    import numpy as np
    a = {k: np.asarray(v) for k, v in inputs.items()}
    T = np.ascontiguousarray
    out = {
        "x": a["x"],
        "Wq": a["L0_xattn_Wq"],
        "w_kc_q": a["L0_xattn_w_kc_q"],
        "w_kc_kv": a["L0_xattn_w_kc_kv"],
        "W_qrT": T(a["L0_xattn_W_qr"].transpose(2, 0, 1)),
        "W_krT": T(a["L0_xattn_W_kr"].transpose(2, 0, 1)),
        "WoT": T(a["L0_xattn_Wo"].T),
        "ident": np.eye(P, dtype=np.float32),
    }
    sin, cos = rope_tables(S, DQ)
    sin, cos = sin.T, cos.T
    out["rope_q"] = T(np.stack([cos[:HALF], -sin[:HALF], cos[HALF:], sin[HALF:]], axis=1))
    ctxT = a["ctx_512"].transpose(0, 2, 1)
    swapped = np.concatenate([ctxT[:, DC // 2:], ctxT[:, :DC // 2]], axis=1)
    out["ctx_T"] = T(np.stack([np.concatenate([ctxT, ctxT], axis=1), np.concatenate([swapped, swapped], axis=1)], axis=2))
    padded = np.zeros((B, SKP, DC), np.float32)
    padded[:, :SK] = a["ctx_512"]
    out["ctx_k"] = T(padded.reshape(B, KT, P, DC).transpose(0, 2, 1, 3))
    sin, cos = rope_tables(SK, DC)
    sign = np.where(np.arange(DC) < DC // 2, -1.0, 1.0).astype(np.float32)
    sin = sin * sign
    out["rope_T"] = T(np.stack([np.concatenate([cos.T, cos.T]), np.concatenate([sin.T, sin.T])], axis=1))
    table = np.zeros((2, SKP, DC), np.float32)
    table[0, :SK], table[1, :SK] = cos, sin
    out["rope_k"] = T(table.reshape(2, KT, P, DC).transpose(2, 0, 1, 3))
    ones = np.zeros((P, KT, 2), np.float32)
    ones[:, :, 0] = (np.arange(SKP) < SK).reshape(KT, P).T
    out["key_ones"] = ones
    more_layouts(a, out)
    return out


def more_layouts(a, out):
    import numpy as np
    T = np.ascontiguousarray

    def by_part(w, ni):
        return w.reshape(w.shape[0], KD, P, ni).transpose(0, 2, 1, 3)

    E, I, NI, TR = 8, 688, 696, 116
    gu = np.zeros((E, P, KD, 2, NI), np.float32)
    gu[:, :, :, 0, :I] = by_part(a["L0_ffn_Wg"].transpose(0, 2, 1), I)
    gu[:, :, :, 1, :I] = by_part(a["L0_ffn_Wu"].transpose(0, 2, 1), I)
    out["m0_up"] = gu
    wd = np.zeros((E, NI, D), np.float32)
    wd[:, :I] = a["L0_ffn_Wd"].transpose(0, 2, 1)
    out["m0_down"] = T(wd.reshape(E, NI // TR, TR, D).transpose(0, 2, 1, 3))
    out["m0_router"] = T(a["L0_ffn_router_w"].T.reshape(KD, P, E).transpose(1, 0, 2))
    route_tables(out, "m0_", E, most_tiles(E))

    wkv = a["L1_xattn_Wkv_expand"]
    out["c_wq"] = T(a["L1_xattn_Wq"].T.reshape(KD, P, D).transpose(1, 0, 2))
    out["c_wk"], out["c_wv"] = T(wkv[:D].T), T(wkv[D:].T)
    out["c_wo"] = T(a["L1_xattn_Wout"].T.reshape(KD, P, D).transpose(1, 0, 2))
    out["c_lat"] = T(a["ctx_512"][:, :S].transpose(2, 0, 1).reshape(DC, B * S))
    out["c_mask"] = np.triu(np.full((S, S), -3.0e38, np.float32), 1)
    out["c_blocks"] = np.repeat(np.eye(H // KD, dtype=np.float32), HD, axis=0)

    E, I, TR = 16, 176, 88
    w1 = np.concatenate([a["L1_ffn_w1"], a["L1_ffn_sw1"]])
    w2 = np.concatenate([a["L1_ffn_w2"], a["L1_ffn_sw2"]])
    out["m1_up"] = T(by_part(w1, I).reshape(E + 1, P, KD, 1, I))
    out["m1_down"] = T(w2.reshape(E + 1, I // TR, TR, D).transpose(0, 2, 1, 3))
    out["m1_router"] = T(a["L1_ffn_gate_w"].T.reshape(KD, P, E).transpose(1, 0, 2))
    route_tables(out, "m1_", E, -(-B * S // TOK) + most_tiles(E))


def route_tables(out, tag, experts, tiles):
    import numpy as np
    every = lambda a: np.ascontiguousarray(np.broadcast_to(np.asarray(a, np.float32), (S,) + np.shape(a)))
    out[tag + "iota"] = every(np.arange(experts))
    out[tag + "steps"] = every(np.arange(-(-B * S // TOK)) * TOK)
    out[tag + "below"] = every(np.tril(np.ones((experts, experts)), -1))
    out[tag + "order"] = every(np.arange(tiles))
    out[tag + "tri"] = np.triu(np.ones((S, S), np.float32), 1)


def kernel(**inputs):
    import numpy as _np
    import concourse.bacc as _bacc
    from concourse import mybir as _mybir
    from concourse.bass_utils import run_bass_kernel_spmd as _run

    nc = _bacc.Bacc("TRN2", target_bir_lowering=False, num_devices=1)
    arrays, dram = {}, {}
    for name, a in layouts(inputs).items():
        a = _np.ascontiguousarray(a)
        arrays[f"in_{name}"] = a
        dram[name] = nc.dram_tensor(f"in_{name}", a.shape, _mybir.dt.from_np(a.dtype), kind="ExternalInput").ap()
    out = nc.dram_tensor("out", (B, S, D), F32, kind="ExternalOutput").ap()
    model(nc, dram, out)
    r = _run(nc, [arrays], core_ids=[0])
    return r.results[0]["out"]
```
